# Optimizing a Trainium2 kernel written in Bass

```python
import numpy as np
import jax
import jax.numpy as jnp

def _softmax(x, axis=-1):
    return jax.nn.softmax(x, axis=axis)

def _gelu(x):
    return jax.nn.gelu(x, approximate=True)

def _silu(x):
    return jax.nn.silu(x)

def _sigmoid(x):
    return jax.nn.sigmoid(x)

def _layernorm(x, axis=-1, eps=1e-05):
    m = jnp.mean(x, axis=axis, keepdims=True)
    v = jnp.var(x, axis=axis, keepdims=True)
    return (x - m) / jnp.sqrt(v + eps)

def _scatter_add(tgt, idx, src, axis=0):
    return tgt.at[idx].add(src)

def _segment_sum(src, seg, n):
    return jax.ops.segment_sum(src, seg, n)
kernel_name = 'mk_flamingo_gated_d2_seqx_r8_6879a9'

def setup_inputs(seed: int=0):
    np.random.seed(seed)
    _w = jnp.asarray

    def _rec_inputs():
        import jax
        import jax.numpy as jnp
        _rk = jax.random.key(seed)
        x = -0.0002928 + 1 * jax.random.normal(jax.random.fold_in(_rk, 1), (128, 64, 128), jnp.float32)
        _lenS = 64 - jax.random.randint(jax.random.fold_in(_rk, 7), (128,), 0, max(1, 64 // 4) + 1, jnp.int32)
        _lenS2 = 64 - jax.random.randint(jax.random.fold_in(_rk, 8), (128,), 0, max(1, 64 // 4) + 1, jnp.int32)
        _ctx_1024P = jax.random.normal(jax.random.fold_in(_rk, 11), (128, 16, 128), jnp.float32)
        _ctx_1024c = jax.random.dirichlet(jax.random.fold_in(_rk, 511), 0.3 * jnp.ones((16,), jnp.float32), (128, 64))
        _ctx_1024t = jnp.einsum('bsk,bkd->bsd', _ctx_1024c, _ctx_1024P)
        _ctx_1024t = _ctx_1024t * jax.lax.rsqrt(jnp.mean(jnp.square(_ctx_1024t)) + 1e-12) * 0.953939
        ctx_1024 = -1.39393e-06 + 0.999914 * (_ctx_1024t + 0.3 * jax.random.normal(jax.random.fold_in(_rk, 611), (128, 64, 128), jnp.float32))
        _validS = jnp.arange(64)[None, :] < _lenS[:, None]
        _validS2 = jnp.arange(64)[None, :] < _lenS2[:, None]
        _causal = jnp.tril(jnp.ones((64, 64), dtype=bool))
        mask_1x1xSxS2_ik0 = jnp.where(jnp.broadcast_to(_validS2[0:1, None, None, :], (1, 1, 64, 64)), 0, 1).astype(jnp.int32)
        mask_BxSxS2_ik1 = jnp.where(jnp.broadcast_to(_validS2[:, None, :], (128, 64, 64)), 1, 0).astype(jnp.int32)
        _g = jax.random.normal(jax.random.fold_in(_rk, 9001), (2, 2), jnp.float32)
        _g = jnp.sign(_g) * jnp.maximum(jnp.abs(_g), 1.0) + (_g == 0) * 1.0
        g_xattn = _g[0]
        g_ffn = _g[1]
        return (x, ctx_1024, mask_1x1xSxS2_ik0, mask_BxSxS2_ik1, g_xattn, g_ffn)
    x, ctx_1024, mask_1x1xSxS2_ik0, mask_BxSxS2_ik1, g_xattn, g_ffn = _rec_inputs()

    def _L0_xattn_setup():
        import jax, jax.numpy as jnp
        import numpy as np
        B, S, D, H = (2, 256, 128, 16)
        DK = D // H

        def _split_heads(x):
            b, s, _ = x.shape
            return x.reshape(b, s, H, DK).transpose(0, 2, 1, 3)
        key = jax.random.key(seed)
        ks = jax.random.split(key, 12)
        scale = 1.0 / np.sqrt(D)
        inp = {'q': jax.random.normal(ks[0], (B, S, D), dtype=jnp.float32), 'k': jax.random.normal(ks[1], (B, S, D), dtype=jnp.float32), 'v': jax.random.normal(ks[2], (B, S, D), dtype=jnp.float32), 'mask': jnp.tril(jnp.ones((S, S), dtype=jnp.int32))[None, None, :, :], 'wq_w': jax.random.normal(ks[3], (D, D), dtype=jnp.float32) * scale, 'wq_b': jax.random.normal(ks[4], (D,), dtype=jnp.float32) * scale, 'wk_w': jax.random.normal(ks[5], (D, D), dtype=jnp.float32) * scale, 'wk_b': jax.random.normal(ks[6], (D,), dtype=jnp.float32) * scale, 'wv_w': jax.random.normal(ks[7], (D, D), dtype=jnp.float32) * scale, 'wv_b': jax.random.normal(ks[8], (D,), dtype=jnp.float32) * scale, 'wo_w': jax.random.normal(ks[9], (D, D), dtype=jnp.float32) * scale, 'wo_b': jax.random.normal(ks[10], (D,), dtype=jnp.float32) * scale}
        return inp
    _L0_xattn_all = _L0_xattn_setup()
    _L0_xattn_in = {k: v for k, v in _L0_xattn_all.items() if k in ('wq_w', 'wq_b', 'wk_w', 'wk_b', 'wv_w', 'wv_b', 'wo_w', 'wo_b')}
    del _L0_xattn_all

    def _L0_ffn_setup():
        import jax, jax.numpy as jnp
        import numpy as np
        DIM = 128
        HID = 512
        NUM_EXPERTS = 8
        TOP_K = 2
        ALPHA = 2.0
        B, S = (4, 256)

        def _swiglu(x, wu, wg, wd):
            up = x @ wu
            g = x @ wg
            gate = jax.nn.sigmoid(g) * g
            return up * gate @ wd
        key = jax.random.key(seed)
        ks = jax.random.split(key, 8)
        x = jax.random.normal(ks[0], (B, S, DIM), dtype=jnp.float32)
        Wr = jax.random.normal(ks[1], (DIM, NUM_EXPERTS), dtype=jnp.float32) * 0.02
        Wu = jax.random.normal(ks[2], (NUM_EXPERTS - 1, DIM, HID), dtype=jnp.float32) * 0.02
        Wg = jax.random.normal(ks[3], (NUM_EXPERTS - 1, DIM, HID), dtype=jnp.float32) * 0.02
        Wd = jax.random.normal(ks[4], (NUM_EXPERTS - 1, HID, DIM), dtype=jnp.float32) * 0.002
        Wu_s = jax.random.normal(ks[5], (DIM, HID), dtype=jnp.float32) * 0.02
        Wg_s = jax.random.normal(ks[6], (DIM, HID), dtype=jnp.float32) * 0.02
        Wd_s = jax.random.normal(ks[7], (HID, DIM), dtype=jnp.float32) * 0.002
        return {'x': x, 'Wr': Wr, 'Wu': Wu, 'Wg': Wg, 'Wd': Wd, 'Wu_s': Wu_s, 'Wg_s': Wg_s, 'Wd_s': Wd_s}
    _L0_ffn_all = _L0_ffn_setup()
    _L0_ffn_in = {k: v for k, v in _L0_ffn_all.items() if k in ('Wr', 'Wu', 'Wg', 'Wd', 'Wu_s', 'Wg_s', 'Wd_s')}
    del _L0_ffn_all

    def _L1_xattn_setup():
        import jax, jax.numpy as jnp
        import numpy as np
        N_HEADS = 16
        NEG_BIAS = -1000000000.0

        def _split_heads(x):
            B, S, D = x.shape
            return x.reshape(B, S, N_HEADS, D // N_HEADS).transpose(0, 2, 1, 3)
        key = jax.random.key(seed)
        k1, k2, k3, k4 = jax.random.split(key, 4)
        B, S, D = (2, 256, 128)
        queries = jax.random.normal(k1, (B, S, D), dtype=jnp.float32)
        keys = jax.random.normal(k2, (B, S, D), dtype=jnp.float32)
        values = jax.random.normal(k3, (B, S, D), dtype=jnp.float32)
        mask = jax.random.randint(k4, (B, S, S), 0, 2, dtype=jnp.int32)
        return {'queries': queries, 'keys': keys, 'values': values, 'mask': mask}
    _L1_xattn_all = _L1_xattn_setup()
    _L1_xattn_in = {k: v for k, v in _L1_xattn_all.items() if k in ()}
    del _L1_xattn_all

    def _L1_ffn_setup():
        import jax, jax.numpy as jnp
        import numpy as np
        B, S, D, F, E, K = (2, 256, 128, 512, 8, 2)
        key = jax.random.key(seed)
        ks = jax.random.split(key, 5)
        x = jax.random.normal(ks[0], (B, S, D), dtype=jnp.float32)
        Wg = jax.random.normal(ks[1], (D, E), dtype=jnp.float32) * 0.02
        W1 = jax.random.normal(ks[2], (E, D, F), dtype=jnp.float32) * 0.02
        b1 = jnp.zeros((E, F), dtype=jnp.float32)
        W2 = jax.random.normal(ks[3], (E, F, D), dtype=jnp.float32) * 0.02
        b2 = jnp.zeros((E, D), dtype=jnp.float32)
        return {'x': x, 'Wg': Wg, 'W1': W1, 'b1': b1, 'W2': W2, 'b2': b2}
    _L1_ffn_all = _L1_ffn_setup()
    _L1_ffn_in = {k: v for k, v in _L1_ffn_all.items() if k in ('Wg', 'W1', 'b1', 'W2', 'b2')}
    del _L1_ffn_all
    return {'x': x, 'ctx_1024': ctx_1024, 'mask_1x1xSxS2_ik0': mask_1x1xSxS2_ik0, 'mask_BxSxS2_ik1': mask_BxSxS2_ik1, 'g_xattn': g_xattn, 'g_ffn': g_ffn, 'L0_xattn_wq_w': _L0_xattn_in['wq_w'], 'L0_xattn_wq_b': _L0_xattn_in['wq_b'], 'L0_xattn_wk_w': _L0_xattn_in['wk_w'], 'L0_xattn_wk_b': _L0_xattn_in['wk_b'], 'L0_xattn_wv_w': _L0_xattn_in['wv_w'], 'L0_xattn_wv_b': _L0_xattn_in['wv_b'], 'L0_xattn_wo_w': _L0_xattn_in['wo_w'], 'L0_xattn_wo_b': _L0_xattn_in['wo_b'], 'L0_ffn_Wr': _L0_ffn_in['Wr'], 'L0_ffn_Wu': _L0_ffn_in['Wu'], 'L0_ffn_Wg': _L0_ffn_in['Wg'], 'L0_ffn_Wd': _L0_ffn_in['Wd'], 'L0_ffn_Wu_s': _L0_ffn_in['Wu_s'], 'L0_ffn_Wg_s': _L0_ffn_in['Wg_s'], 'L0_ffn_Wd_s': _L0_ffn_in['Wd_s'], 'L1_ffn_Wg': _L1_ffn_in['Wg'], 'L1_ffn_W1': _L1_ffn_in['W1'], 'L1_ffn_b1': _L1_ffn_in['b1'], 'L1_ffn_W2': _L1_ffn_in['W2'], 'L1_ffn_b2': _L1_ffn_in['b2']}

def reference(x, ctx_1024, mask_1x1xSxS2_ik0, mask_BxSxS2_ik1, g_xattn, g_ffn, L0_xattn_wq_w, L0_xattn_wq_b, L0_xattn_wk_w, L0_xattn_wk_b, L0_xattn_wv_w, L0_xattn_wv_b, L0_xattn_wo_w, L0_xattn_wo_b, L0_ffn_Wr, L0_ffn_Wu, L0_ffn_Wg, L0_ffn_Wd, L0_ffn_Wu_s, L0_ffn_Wg_s, L0_ffn_Wd_s, L1_ffn_Wg, L1_ffn_W1, L1_ffn_b1, L1_ffn_W2, L1_ffn_b2):
    import jax
    import jax.numpy as jnp

    def _L0_xattn_ref(q, k, v, mask, wq_w, wq_b, wk_w, wk_b, wv_w, wv_b, wo_w, wo_b):
        import jax, jax.numpy as jnp
        import numpy as np
        B, S, D, H = (2, 256, 128, 16)
        DK = D // H

        def _split_heads(x):
            b, s, _ = x.shape
            return x.reshape(b, s, H, DK).transpose(0, 2, 1, 3)
        Q = _split_heads(q @ wq_w.T + wq_b)
        K = _split_heads(k @ wk_w.T + wk_b)
        V = _split_heads(v @ wv_w.T + wv_b)
        scale = 1.0 / jnp.sqrt(jnp.asarray(DK, dtype=Q.dtype))
        scores = jnp.einsum('bhqd,bhkd->bhqk', Q, K) * scale
        scores = jnp.where(mask == 0, jnp.asarray(-1000000000.0, dtype=scores.dtype), scores)
        attn = jax.nn.softmax(scores, axis=-1)
        out = jnp.einsum('bhqk,bhkd->bhqd', attn, V)
        out = out.transpose(0, 2, 1, 3).reshape(out.shape[0], -1, D)
        return out @ wo_w.T + wo_b

    def _L0_ffn_ref(x, Wr, Wu, Wg, Wd, Wu_s, Wg_s, Wd_s):
        import jax, jax.numpy as jnp
        import numpy as np
        DIM = 128
        HID = 512
        NUM_EXPERTS = 8
        TOP_K = 2
        ALPHA = 2.0
        B, S = (4, 256)

        def _swiglu(x, wu, wg, wd):
            up = x @ wu
            g = x @ wg
            gate = jax.nn.sigmoid(g) * g
            return up * gate @ wd
        logits = x @ Wr
        probs = jax.nn.softmax(logits, axis=-1)
        topk_vals, topk_idx = jax.lax.top_k(probs, TOP_K)
        out = jnp.zeros_like(x)
        for i in range(TOP_K - 1):
            p = topk_vals[..., i:i + 1]
            ind = topk_idx[..., i]
            acc = jnp.zeros_like(x)
            for j in range(NUM_EXPERTS - 1):
                mask = (ind == j).astype(x.dtype)[..., None]
                acc = acc + _swiglu(x, Wu[j], Wg[j], Wd[j]) * mask
            out = out + ALPHA * p * acc
        out = out + _swiglu(x, Wu_s, Wg_s, Wd_s)
        return out

    def _L1_xattn_ref(queries, keys, values, mask):
        import jax, jax.numpy as jnp
        import numpy as np
        N_HEADS = 16
        NEG_BIAS = -1000000000.0

        def _split_heads(x):
            B, S, D = x.shape
            return x.reshape(B, S, N_HEADS, D // N_HEADS).transpose(0, 2, 1, 3)
        q = _split_heads(queries)
        k = _split_heads(keys)
        v = _split_heads(values)
        d_head = q.shape[-1]
        sim = jnp.einsum('bhqd,bhkd->bhqk', q, k) / jnp.sqrt(jnp.float32(d_head))
        bias = NEG_BIAS * (1.0 - mask.astype(sim.dtype))[:, None]
        sim = sim + bias
        weights = jax.nn.softmax(sim, axis=-1)
        out = jnp.einsum('bhqk,bhkd->bhqd', weights, v)
        B, H, Sq, d = out.shape
        return out.transpose(0, 2, 1, 3).reshape(B, Sq, H * d)

    def _L1_ffn_ref(x, Wg, W1, b1, W2, b2):
        import jax, jax.numpy as jnp
        import numpy as np
        B, S, D, F, E, K = (2, 256, 128, 512, 8, 2)
        b, s, d = x.shape
        e = Wg.shape[1]
        T = b * s
        C = 2 * K * T // e
        xt = x.reshape(T, d)
        logits = xt.astype(jnp.float32) @ Wg.astype(jnp.float32)
        gates = jax.nn.softmax(logits, axis=-1)
        idx1 = jnp.argmax(gates, axis=-1)
        mask1 = jax.nn.one_hot(idx1, e, dtype=gates.dtype)
        gate1 = jnp.sum(gates * mask1, axis=-1)
        logits2 = jnp.where(mask1 > 0, -jnp.inf, logits)
        idx2 = jnp.argmax(logits2, axis=-1)
        mask2 = jax.nn.one_hot(idx2, e, dtype=gates.dtype)
        gate2 = jnp.sum(gates * mask2, axis=-1)
        denom = gate1 + gate2 + 1e-09
        w1 = gate1 / denom
        w2 = gate2 / denom
        p1 = jnp.cumsum(mask1, axis=0) - mask1
        pos1 = jnp.sum(p1 * mask1, axis=-1).astype(jnp.int32)
        off = jnp.sum(mask1, axis=0)
        p2 = jnp.cumsum(mask2, axis=0) - mask2 + off[None, :]
        pos2 = jnp.sum(p2 * mask2, axis=-1).astype(jnp.int32)
        keep1 = (pos1 < C).astype(xt.dtype)
        keep2 = (pos2 < C).astype(xt.dtype)
        pos1 = jnp.clip(pos1, 0, C - 1)
        pos2 = jnp.clip(pos2, 0, C - 1)
        xe = jnp.zeros((e, C, d), dtype=xt.dtype)
        xe = xe.at[idx1, pos1].add(xt * keep1[:, None])
        xe = xe.at[idx2, pos2].add(xt * keep2[:, None])
        h = jax.nn.gelu(jnp.einsum('ecd,edf->ecf', xe, W1) + b1[:, None, :], approximate=False)
        ye = jnp.einsum('ecf,efd->ecd', h, W2) + b2[:, None, :]
        out = ye[idx1, pos1] * (w1 * keep1)[:, None] + ye[idx2, pos2] * (w2 * keep2)[:, None]
        return out.reshape(b, s, d)
    x = x + jnp.tanh(g_xattn[0]) * _L0_xattn_ref(_layernorm(x, axis=-1), ctx_1024, ctx_1024, mask_1x1xSxS2_ik0, L0_xattn_wq_w, L0_xattn_wq_b, L0_xattn_wk_w, L0_xattn_wk_b, L0_xattn_wv_w, L0_xattn_wv_b, L0_xattn_wo_w, L0_xattn_wo_b)
    x = x + jnp.tanh(g_ffn[0]) * _L0_ffn_ref(_layernorm(x, axis=-1), L0_ffn_Wr, L0_ffn_Wu, L0_ffn_Wg, L0_ffn_Wd, L0_ffn_Wu_s, L0_ffn_Wg_s, L0_ffn_Wd_s)
    x = x + jnp.tanh(g_xattn[1]) * _L1_xattn_ref(_layernorm(x, axis=-1), ctx_1024, ctx_1024, mask_BxSxS2_ik1)
    x = x + jnp.tanh(g_ffn[1]) * _L1_ffn_ref(_layernorm(x, axis=-1), L1_ffn_Wg, L1_ffn_W1, L1_ffn_b1, L1_ffn_W2, L1_ffn_b2)
    return x

_drawn_inputs = setup_inputs


def setup_inputs(seed=0):
    import zlib

    import numpy as np

    out = dict(_drawn_inputs(seed))
    spreads = {'g_ffn': (-1.0, 0.6), 'L1_ffn_b1': (0.0, 0.568), 'L1_ffn_b2': (0.0, 0.1)}
    factors = {'L0_xattn_wq_b': 3.003,
     'L0_xattn_wk_b': 8.0,
     'L0_ffn_Wr': 8.0,
     'L0_ffn_Wu': 8.0,
     'L0_ffn_Wg': 8.0,
     'L0_ffn_Wd': 8.0,
     'L0_ffn_Wu_s': 8.0,
     'L0_ffn_Wg_s': 8.0,
     'L0_ffn_Wd_s': 8.0}
    for name, (base, spread) in spreads.items():
        noise = np.random.default_rng([zlib.crc32(name.encode()), seed]).standard_normal(out[name].shape)
        drawn = base * np.exp(spread * noise) if base else spread * noise
        out[name] = jnp.asarray(drawn.astype(out[name].dtype))
    for name, factor in factors.items():
        out[name] = (out[name] * factor).astype(out[name].dtype)
    return out
```

```python
from contextlib import ExitStack

import numpy as np

import concourse.bass as bass
from concourse import mybir

F32 = mybir.dt.float32
I32 = mybir.dt.int32
ALU = mybir.AluOpType
ACT = mybir.ActivationFunctionType
AX = mybir.AxisListType

P = 128
SEQ = 64
BATCH = 128
D = 128
HEADS = 16
DK = D // HEADS
TOKENS = BATCH * SEQ
TILES = TOKENS // P
CHUNK = 4
CHUNKS = TILES // CHUNK
E = 8
F = 512
FB = F // P
NEG = 1.0e9
EPS = 1e-5
CAP = 2 * 2 * TOKENS // E
SLOTS = (TOKENS // P + E, 2 * TOKENS // P + E)
MAX_SLOTS = max(SLOTS)

C_IDENT, C_TRI, C_ONES = 0, P, 2 * P
C_HEAD = 3 * P
C_FIRST = C_HEAD + 4
C_EXPERT = C_FIRST + E
C_SLOT = C_EXPERT + E
C_ALL = C_SLOT + MAX_SLOTS


def constants():
    c = np.zeros((P, C_ALL), np.float32)
    c[:, C_IDENT:C_IDENT + P] = np.eye(P)
    c[:, C_TRI:C_TRI + P] = np.triu(np.ones((P, P)), 1)
    c[:, C_ONES:C_ONES + P] = 1.0
    c[:, C_HEAD:C_HEAD + 4] = (np.arange(P)[:, None] % 32) // DK == np.arange(4)
    c[:, C_FIRST:C_FIRST + E] = E - np.arange(E)
    c[:, C_EXPERT:C_EXPERT + E] = np.arange(E)
    c[:, C_SLOT:C_SLOT + MAX_SLOTS] = P * np.arange(MAX_SLOTS)
    return c


def spread(ap, dim, n):
    ap = ap.unsqueeze(dim)
    shape = list(ap.shape)
    shape[dim] = n
    return ap.broadcast_to(shape)


def pipeline(eng, tiles, unroll, stages, peeled=2):
    last = max(lag for lag, _ in stages)
    assert last <= unroll and tiles % unroll == 0

    def step(it, k, t):
        for lag, f in stages:
            if t is None or 0 <= t - lag < tiles:
                q, r = divmod(k - lag, unroll)
                f(it + q, r)

    for t in range(peeled * unroll):
        step(t // unroll, t % unroll, t)
    with eng.Fori(peeled, tiles // unroll) as it:
        for k in range(unroll):
            step(it, k, None)
    for k in range(last):
        step(tiles // unroll, k, tiles + k)


def reused(t, buffers):
    return not isinstance(t, int) or t >= buffers


def absorb(eng, ticks):
    eng.sem_inc(ticks, 1)


class Chain:

    def __init__(self, eng, sem):
        self.eng, self.sem, self.n = eng, sem, 0

    def __call__(self, instruction):
        self.n += 1
        instruction.then_inc(self.sem, 1)
        self.eng.wait_ge(self.sem, self.n)


def load_inputs(nc, k):
    with ExitStack() as ctx:
        arrived = ctx.enter_context(nc.semaphore("inputs_arrived"))
        ready = ctx.enter_context(nc.semaphore("gates_ready"))
        block = ctx.enter_context(nc.Block())

        @block.sync
        def _(sp):
            n = 0
            xv = k.x_in.rearrange("(t p) d -> p t d", p=P)
            for a in range(0, TILES, TILES // 4):
                sp.dma_start(k.x[:, a:a + TILES // 4, :], xv[:, a:a + TILES // 4, :]).then_inc(arrived, 16)
                n += 1
            sp.dma_start(k.const[:], k.const_in).then_inc(arrived, 16)
            sp.dma_start(k.gates[:, 0:2], k.g_xattn.partition_broadcast(P)).then_inc(arrived, 16)
            sp.dma_start(k.gates[:, 2:4], k.g_ffn.partition_broadcast(P)).then_inc(arrived, 16)
            sp.wait_ge(arrived, 16 * (n + 3))

        @block.scalar
        def _(act):
            act.wait_ge(arrived, 16 * 7)
            nc.scalar.activation(k.gates[:], k.gates[:], ACT.Tanh).then_inc(ready, 1)


def layer_stats(nc, k, name):
    with ExitStack() as ctx:
        def sb(n, shape):
            return ctx.enter_context(nc.sbuf_tensor(f"{name}_{n}", shape, F32))

        stats = sb("stats", [P, TILES, 6])
        a, b, c, v = (sb(n, [P, TILES]) for n in ("a", "b", "c", "v"))
        counted = ctx.enter_context(nc.semaphore(f"{name}_counted"))
        steps = ctx.enter_context(nc.semaphore(f"{name}_steps"))
        var_ready = ctx.enter_context(nc.semaphore(f"{name}_var_ready"))
        root_ready = ctx.enter_context(nc.semaphore(f"{name}_root_ready"))
        block = ctx.enter_context(nc.Block())

        @block.vector
        def _(dve):
            with dve.Fori(0, TILES) as t:
                nc.vector.bn_stats(stats[:, bass.ds(t, 1), :].rearrange("p a s -> p (a s)"),
                                   k.x[:, bass.ds(t, 1), :].rearrange("p a s -> p (a s)")).then_inc(counted, 1)
            dve.wait_ge(counted, TILES)
            do = Chain(dve, steps)
            mean_e, m2_e, mean_o, m2_o = (stats[:, :, i] for i in (1, 2, 4, 5))
            do(nc.vector.tensor_tensor(a[:], mean_e, mean_o, ALU.add))
            do(nc.vector.tensor_tensor(b[:], mean_e, mean_o, ALU.subtract))
            do(nc.vector.tensor_tensor(c[:], m2_e, m2_o, ALU.add))
            do(nc.vector.tensor_scalar(k.mean[:], a[:], 0.5, None, ALU.mult))
            do(nc.vector.tensor_tensor(b[:], b[:], b[:], ALU.mult))
            do(nc.vector.scalar_tensor_tensor(v[:], b[:], D / 4.0, c[:], ALU.mult, ALU.add))
            nc.vector.tensor_scalar(v[:], v[:], 1.0 / D, EPS, ALU.mult, ALU.add).then_inc(var_ready, 1)
            dve.wait_ge(root_ready, 1)
            do(nc.vector.reciprocal(a[:], a[:]))
            do(nc.vector.tensor_tensor(b[:], a[:], a[:], ALU.mult))
            do(nc.vector.tensor_tensor(b[:], b[:], v[:], ALU.mult))
            do(nc.vector.tensor_scalar(b[:], b[:], -0.5, 1.5, ALU.mult, ALU.add))
            do(nc.vector.tensor_tensor(k.rstd[:], a[:], b[:], ALU.mult))

        @block.scalar
        def _(act):
            act.wait_ge(var_ready, 1)
            nc.scalar.activation(a[:], v[:], ACT.Sqrt).then_inc(root_ready, 1)


def normalize(nc, k, out, t):
    return nc.vector.tensor_scalar(out, k.x[:, bass.ds(t, 1), :].rearrange("p a d -> p (a d)"),
                                   k.mean[:, bass.ds(t, 1)], k.rstd[:, bass.ds(t, 1)],
                                   ALU.subtract, ALU.mult)


def project(nc, k, layer):
    first = layer == 0
    with ExitStack() as ctx:
        def sb(n, shape, dt=F32):
            return ctx.enter_context(nc.sbuf_tensor(f"pj{layer}_{n}", shape, dt))

        def ps(n):
            return ctx.enter_context(nc.psum_tensor(f"pj{layer}_{n}", [P, 512], F32))

        def sem(n):
            return ctx.enter_context(nc.semaphore(f"pj{layer}_{n}"))

        xn = [sb(f"xn{i}", [P, CHUNK, D]) for i in range(2)]
        xt = [sb(f"xt{i}", [P, CHUNK * P]) for i in range(2)]
        q_sb = [sb(f"q{i}", [P, CHUNK * P]) for i in range(2)]
        ps_t = [ps(f"ps_t{i}") for i in range(2)]
        if first:
            ctxt = [sb(f"ctxt{i}", [P, CHUNK * P]) for i in range(2)]
            k_sb = [sb(f"k{i}", [P, CHUNK * P]) for i in range(2)]
            v_sb = [sb(f"v{i}", [P, CHUNK, D]) for i in range(2)]
            ps_q, ps_k, ps_v = ([ps(f"ps_{n}{i}") for i in range(2)] for n in "qkv")
            wq, wk, wv = (sb(f"w{n}", [P, D]) for n in "qkv")
            bq, bk = sb("bq", [P, 1]), sb("bk", [P, 1])
            bv, bo = sb("bv", [P, D]), sb("bo", [P, D])
            mask01 = sb("mask01", [P, SEQ])
            keep_col = sb("keep_col", [P, 1])
            keep = sb("keep", [P, SEQ])

        setup = sem("setup")
        steps = sem("steps")
        keep_col_ready, keep_summed = sem("keep_col_ready"), sem("keep_summed")
        ctx_in = [sem(f"ctx_in{i}") for i in range(2)]
        biased = sem("biased")
        normed, transposed, xt_ready = sem("normed"), sem("transposed"), sem("xt_ready")
        q_done, k_done, v_done = sem("q_done"), sem("k_done"), sem("v_done")
        q_ready, k_ready, v_ready = sem("q_ready"), sem("k_ready"), sem("v_ready")
        stored = [sem(f"stored{i}") for i in range(2)]
        outs = 3 if first else 1
        block = ctx.enter_context(nc.Block())

        @block.sync
        def _(sp):
            if first:
                for dst, src in ((wq, k.wq), (wk, k.wk), (wv, k.wv), (bq, k.bq), (bk, k.bk)):
                    sp.dma_start(dst[:], src).then_inc(setup, 16)
                sp.dma_start(bv[:], k.bv.partition_broadcast(P)).then_inc(setup, 16)
                sp.dma_start(bo[:], k.bo.partition_broadcast(P)).then_inc(setup, 16)
                for b in range(2):
                    sp.dma_start(k.mask0[b * SEQ:(b + 1) * SEQ, :], k.mask0_in).then_inc(setup, 16)
            else:
                sp.dma_start(k.mask1[:], k.mask1_in.rearrange("(t b) q k -> (b q) t k", b=2)).then_inc(setup, 16)

            def load(it, par):
                c = 2 * it + par
                if reused(c, 2):
                    sp.wait_ge(v_done, c - 1)
                sp.dma_start(ctxt[par][:], k.ctxt_in[:, bass.ts(c, 512)]).then_inc(ctx_in[par], 16)

            def store(it, par):
                c = 2 * it + par
                sp.wait_ge(q_ready, c + 1)
                sp.dma_start(k.qt[:, bass.ts(c, 512)], q_sb[par][:]).then_inc(stored[par], 16)
                if first:
                    sp.wait_ge(k_ready, c + 1)
                    sp.dma_start(k.kt[:, bass.ts(c, 512)], k_sb[par][:]).then_inc(stored[par], 16)
                    sp.wait_ge(v_ready, c + 1)
                    sp.dma_start(k.v.rearrange("(t p) d -> p t d", p=P)[:, bass.ts(c, CHUNK), :],
                                 v_sb[par][:]).then_inc(stored[par], 16)

            pipeline(sp, CHUNKS, 2, ([(0, load)] if first else []) + [(1, store)])
            for par in range(2):
                sp.wait_ge(stored[par], 16 * outs * CHUNKS // 2)

        @block.vector
        def _(dve):
            do = Chain(dve, steps)
            if first:
                dve.wait_ge(setup, 16 * 9)
                do(nc.vector.tensor_scalar(mask01[:], k.mask0[:], 0.0, None, ALU.not_equal))
                nc.vector.tensor_reduce(keep_col[:], mask01[:], AX.X, ALU.max).then_inc(keep_col_ready, 1)
                do(nc.vector.tensor_scalar(k.bias0[:], mask01[:], -1.0, NEG, ALU.add, ALU.mult))
                do(nc.vector.tensor_scalar(bo[:], bo[:], k.gates[:, 0:1], None, ALU.mult))
                dve.wait_ge(keep_summed, 1)
                do(nc.vector.tensor_scalar(keep[:], ps_k[0][:, 0:SEQ], DK ** -0.5, None, ALU.mult))
            else:
                dve.wait_ge(setup, 16)
                do(nc.vector.tensor_scalar(k.bias1[:], k.mask1[:], -1.0, NEG, ALU.add, ALU.mult))

            def norm(it, par):
                c = 2 * it + par
                if reused(c, 2):
                    dve.wait_ge(transposed, c - 1)
                for j in range(CHUNK):
                    normalize(nc, k, xn[par][:, j, :], c * CHUNK + j).then_inc(normed, 1)

            def queries(it, par):
                c = 2 * it + par
                dve.wait_ge(q_done, c + 1)
                if reused(c, 2):
                    dve.wait_ge(stored[par], 16 * outs * it)
                nc.vector.scalar_tensor_tensor(
                    q_sb[par][:].rearrange("p (s q) -> p s q", q=SEQ),
                    ps_q[par][:].rearrange("p (s q) -> p s q", q=SEQ), bq[:, 0:1],
                    spread(keep[:], 1, 2 * CHUNK), ALU.add, ALU.mult).then_inc(q_ready, 1)

            def values(it, par):
                c = 2 * it + par
                dve.wait_ge(v_done, c + 1)
                if reused(c, 2):
                    dve.wait_ge(stored[par], 16 * outs * it)
                nc.vector.tensor_tensor(v_sb[par][:], ps_v[par][:].rearrange("p (t d) -> p t d", d=D),
                                        spread(bv[:], 1, CHUNK), ALU.add).then_inc(v_ready, 1)

            def out_bias(it, par):
                c = 2 * it + par
                dve.wait_ge(normed, CHUNK * (c + 1))
                xc = k.x[:, bass.ts(c, CHUNK), :]
                nc.vector.tensor_tensor(xc, xc, spread(bo[:], 1, CHUNK), ALU.add).then_inc(biased, 1)

            pipeline(dve, CHUNKS, 2, [(0, norm)] + ([(0, out_bias), (1, queries), (1, values)] if first else []))

        @block.tensor
        def _(pe):
            ident = k.const[:, C_IDENT:C_IDENT + P]
            if first:
                pe.wait_ge(keep_col_ready, 1)
                nc.tensor.matmul(ps_k[0][:, 0:SEQ], keep_col[0:SEQ, 0:1].broadcast_to([SEQ, P]),
                                 ident[0:SEQ, 0:SEQ], start=True, stop=True).then_inc(keep_summed, 1)

            def transposes(it, par):
                c = 2 * it + par
                pe.wait_ge(normed, CHUNK * (c + 1))
                if reused(c, 2):
                    pe.wait_ge(xt_ready if first else q_ready, c - 1)
                for j in range(CHUNK):
                    last = nc.tensor.transpose(ps_t[par][:, j * P:(j + 1) * P], xn[par][:, j, :], ident)
                last.then_inc(transposed, 1)

            def products(it, par):
                c = 2 * it + par
                if not reused(c, 1):
                    pe.wait_ge(setup, 16 * 9)
                    pe.wait_ge(steps, 4)
                pe.wait_ge(ctx_in[par], 16 * (it + 1))
                if reused(c, 2):
                    pe.wait_ge(k_ready, c - 1)
                nc.tensor.matmul(ps_k[par][:], wk[:], ctxt[par][:], start=True, stop=True).then_inc(k_done, 1)
                if reused(c, 2):
                    pe.wait_ge(v_ready, c - 1)
                for j in range(CHUNK):
                    last = nc.tensor.matmul(ps_v[par][:, j * P:(j + 1) * P], ctxt[par][:, j * P:(j + 1) * P],
                                            wv[:], start=True, stop=True)
                last.then_inc(v_done, 1)
                pe.wait_ge(xt_ready, c + 1)
                if reused(c, 2):
                    pe.wait_ge(q_ready, c - 1)
                nc.tensor.matmul(ps_q[par][:], wq[:], xt[par][:], start=True, stop=True).then_inc(q_done, 1)

            pipeline(pe, CHUNKS, 2, [(0, transposes)] + ([(0, products)] if first else []))

        @block.scalar
        def _(act):
            def columns(it, par):
                c = 2 * it + par
                act.wait_ge(transposed, c + 1)
                if first:
                    if reused(c, 2):
                        act.wait_ge(q_done, c - 1)
                    nc.scalar.activation(xt[par][:], ps_t[par][:], ACT.Copy).then_inc(xt_ready, 1)
                else:
                    if reused(c, 2):
                        act.wait_ge(stored[par], 16 * it)
                    nc.scalar.activation(q_sb[par][:], ps_t[par][:], ACT.Copy, scale=DK ** -0.5).then_inc(q_ready, 1)

            def keys(it, par):
                c = 2 * it + par
                if not reused(c, 1):
                    act.wait_ge(setup, 16 * 9)
                act.wait_ge(k_done, c + 1)
                if reused(c, 2):
                    act.wait_ge(stored[par], 16 * outs * it)
                nc.scalar.activation(k_sb[par][:], ps_k[par][:], ACT.Identity, bias=bk[:, 0:1]).then_inc(k_ready, 1)

            pipeline(act, CHUNKS, 2, [(0, columns)] + ([(0, keys)] if first else []))


def attend(nc, k, layer):
    first = layer == 0
    HALF = P // 2
    LOAD = 4
    U = 2 * LOAD
    with ExitStack() as ctx:
        def sb(n, shape, dt=F32):
            return ctx.enter_context(nc.sbuf_tensor(f"at{layer}_{n}", shape, dt))

        def ps(n, shape):
            return ctx.enter_context(nc.psum_tensor(f"at{layer}_{n}", shape, F32))

        def sem(n):
            return ctx.enter_context(nc.semaphore(f"at{layer}_{n}"))

        q2 = [sb(f"q2{i}", [P, 2, LOAD, P]) for i in range(2)]
        k2 = [sb(f"k2{i}", [P, 2, LOAD, SEQ]) for i in range(2)]
        v2 = [sb(f"v2{i}", [P, LOAD, 2, D]) for i in range(2)]
        keys = [sb(f"keys{i}", [P, 2, 4, SEQ]) for i in range(2)]
        vals = [sb(f"vals{i}", [P, 8, 2, 2, DK + 1]) for i in range(2)]
        s_sb = [sb(f"s{i}", [P, HEADS, SEQ]) for i in range(2)]
        top = [sb(f"top{i}", [P, HEADS]) for i in range(2)]
        pt = [sb(f"pt{i}", [P, 8, P]) for i in range(2)]
        inv = [sb(f"inv{i}", [P, HEADS]) for i in range(2)]
        heads = [sb(f"heads{i}", [P, D]) for i in range(2)]
        ps_s = [ps(f"ps_s{i}", [P, 2, 512]) for i in range(2)]
        ps_p = ps("ps_p", [P, 8, P])
        ps_o = ps("ps_o", [P, 512])
        ps_w = ps("ps_w", [P, 512])
        sums = ps_o[:, 0:8 * 36].rearrange("p (u b r c) -> p u b r c", b=2, r=2, c=DK + 1)
        zeros = sb("zeros", [P, 8 * D])
        if first:
            wo = sb("wo", [P, D])
            ht = sb("ht", [P, P])
        loaded = [sem(f"loaded{i}") for i in range(2)]
        setup, cleared = sem("setup"), sem("cleared")
        sp_ticks, pool_ticks = sem("sp_ticks"), sem("pool_ticks")
        zeros_ready, filled = sem("zeros_ready"), sem("filled")
        keys_spread, vals_spread = sem("keys_spread"), sem("vals_spread")
        scored, masked, topped, shifted = sem("scored"), sem("masked"), sem("topped"), sem("shifted")
        exped, turned, turned_out, summed = sem("exped"), sem("turned"), sem("turned_out"), sem("summed")
        inverted, normalized = sem("inverted"), sem("normalized")
        heads_turned, ht_ready, projected, added = (
            sem("heads_turned"), sem("ht_ready"), sem("projected"), sem("added"))
        block = ctx.enter_context(nc.Block())

        DMAS = 8 + 8 + 2

        @block.sync
        def _(sp):
            if first:
                sp.dma_start(wo[:], k.wo).then_inc(setup, 16)
            sp.wait_ge(cleared, 8)
            qv = k.qt.rearrange("(G g f) (t b q) -> G b f g t q", G=2, g=2, b=2, q=SEQ)
            kv = (k.kt if first else k.ctxt_in).rearrange("(G g f) (t b q) -> G b f g t q", G=2, g=2, b=2, q=SEQ)
            vv = (k.v if first else k.ctx_in).rearrange("(t b q) d -> q t b d", b=2, q=SEQ)

            def load(it, par):
                s = 2 * it + par
                if reused(s, 2):
                    sp.wait_ge(scored, LOAD * (s - 1))
                    absorb(sp, sp_ticks)
                    sp.wait_ge(keys_spread, 2 * LOAD * (s - 1))
                    sp.wait_ge(vals_spread, 2 * LOAD * (s - 1))
                some = bass.ts(s, LOAD)
                for G in range(2):
                    for b in range(2):
                        rows = slice(HALF * G + 32 * b, HALF * G + 32 * b + 32)
                        for g in range(2):
                            sp.dma_start(k2[par][rows, g, :, :], kv[G, b, :, g, some, :]).then_inc(loaded[par], 16)
                for half in range(2):
                    sp.dma_start(v2[par][HALF * half:HALF * half + HALF, :, :, :],
                                 vv[:, some, :, :]).then_inc(loaded[par], 16)
                for G in range(2):
                    for b in range(2):
                        rows = slice(HALF * G + 32 * b, HALF * G + 32 * b + 32)
                        for g in range(2):
                            sp.dma_start(q2[par][rows, g, :, b * SEQ:(b + 1) * SEQ],
                                         qv[G, b, :, g, some, :]).then_inc(loaded[par], 16)

            pipeline(sp, TILES // LOAD, 2, [(0, load)])

        @block.gpsimd
        def _(pool):
            nc.gpsimd.memset(zeros[:], 0.0).then_inc(zeros_ready, 1)
            for i in range(2):
                nc.gpsimd.memset(q2[i][:], 0.0).then_inc(cleared, 1)
                nc.gpsimd.memset(vals[i][:], 0.0).then_inc(cleared, 1)
            pool.wait_ge(cleared, 4)
            for i in range(2):
                for r in range(2):
                    nc.gpsimd.memset(vals[i][HALF * r:HALF * r + HALF, :, :, r, DK:DK + 1], 1.0).then_inc(cleared, 1)
            head_of = k.const[:, C_HEAD:C_HEAD + 4]

            def spread_keys(it, kk):
                t, par, buf, tt = U * it + kk, kk % 2, kk // LOAD, kk % LOAD
                if tt == 0:
                    pool.wait_ge(loaded[buf], 16 * DMAS * (it + 1))
                if reused(t, 2):
                    pool.wait_ge(scored, t - 1)
                if reused(t, 1):
                    pool.wait_ge(vals_spread, 2 * t)
                for g in range(2):
                    nc.gpsimd.tensor_tensor(keys[par][:, g, :, :], spread(k2[buf][:, g, tt, :], 1, 4),
                                            spread(head_of, 2, SEQ), ALU.mult).then_inc(keys_spread, 1)

            def spread_values(it, kk):
                t, par, buf, tt = U * it + kk, kk % 2, kk // LOAD, kk % LOAD
                if reused(t, 2):
                    pool.wait_ge(summed, t - 1)
                for r in range(2):
                    if r:
                        pool.wait_ge(vals_spread, 2 * t + 1)
                    else:
                        pool.wait_ge(keys_spread, 2 * t + 2)
                    absorb(pool, pool_ticks)
                    rows = slice(HALF * r, HALF * r + HALF)
                    src = v2[buf][rows, tt, :, :].rearrange("p b (u r c) -> p u b r c", r=2, c=DK)[:, :, :, r, :]
                    nc.gpsimd.tensor_copy(vals[par][rows, :, :, r, 0:DK], src).then_inc(vals_spread, 1)

            pipeline(pool, TILES, U, [(0, spread_keys), (0, spread_values)], peeled=1)

        @block.tensor
        def _(pe):
            ident = k.const[:, C_IDENT:C_IDENT + P]

            def scores(it, kk):
                t, par, buf, tt = U * it + kk, kk % 2, kk // LOAD, kk % LOAD
                if tt == 0:
                    pe.wait_ge(loaded[buf], 16 * DMAS * (it + 1))
                pe.wait_ge(keys_spread, 2 * t + 2)
                if reused(t, 2):
                    pe.wait_ge(masked, 2 * t - 2)
                for g in range(2):
                    for G in range(2):
                        rows = slice(HALF * G, HALF * G + HALF)
                        last = nc.tensor.matmul(ps_s[par][:, G, 256 * g:256 * g + 256], q2[buf][rows, g, tt, :],
                                                keys[par][rows, g, :, :], start=True, stop=True)
                last.then_inc(scored, 1)

            def turn(it, kk):
                t, par = U * it + kk, kk % 2
                pe.wait_ge(exped, t + 1)
                if reused(t, 1):
                    pe.wait_ge(turned_out, 2 * t)
                for u in range(8):
                    last = nc.tensor.transpose(
                        ps_p[:, u, :], s_sb[par][:, 2 * u:2 * u + 2, :].rearrange("p h k -> p (h k)"), ident)
                last.then_inc(turned, 1)

            def weigh(it, kk):
                t, par = U * it + kk, kk % 2
                pe.wait_ge(turned_out, 2 * t + 2)
                pe.wait_ge(vals_spread, 2 * t + 2)
                if reused(t, 1):
                    pe.wait_ge(normalized, 2 * t)
                for u in range(8):
                    last = nc.tensor.matmul(ps_o[:, 36 * u:36 * u + 36], pt[par][:, u, :],
                                            vals[par][:, u, :, :, :].rearrange("p b r c -> p (b r c)"),
                                            start=True, stop=True)
                last.then_inc(summed, 1)

            def out(it, kk):
                t, par = U * it + kk, kk % 2
                if not reused(t, 1):
                    pe.wait_ge(setup, 16)
                pe.wait_ge(normalized, 2 * t + 2)
                if reused(t, 1):
                    pe.wait_ge(added, t)
                nc.tensor.transpose(ps_w[:, 0:P], heads[par][:], ident).then_inc(heads_turned, 1)
                pe.wait_ge(ht_ready, t + 1)
                nc.tensor.matmul(ps_w[:, P:2 * P], ht[:], wo[:], start=True, stop=True).then_inc(projected, 1)

            pipeline(pe, TILES, U, [(0, scores), (1, turn), (2, weigh)] + ([(3, out)] if first else []), peeled=1)

        @block.scalar
        def _(act):
            act.wait_ge(zeros_ready, 1)
            fills = SLOTS[layer] // 8
            for i in range(fills):
                act.dma_start(k.xs[layer][8 * P * i:8 * P * (i + 1), :].rearrange("(p r) d -> p (r d)", p=P),
                              zeros[:]).then_inc(filled, 16)

            def exponent(it, kk):
                t, par = U * it + kk, kk % 2
                act.wait_ge(shifted, t + 1)
                nc.scalar.activation(s_sb[par][:], s_sb[par][:], ACT.Exp).then_inc(exped, 1)

            def turn_out(it, kk):
                t, par = U * it + kk, kk % 2
                act.wait_ge(turned, t + 1)
                if reused(t, 2):
                    act.wait_ge(summed, t - 1)
                for h in range(2):
                    nc.scalar.activation(pt[par][:, 4 * h:4 * h + 4, :], ps_p[:, 4 * h:4 * h + 4, :],
                                         ACT.Copy).then_inc(turned_out, 1)

            def heads_out(it, kk):
                t = U * it + kk
                act.wait_ge(heads_turned, t + 1)
                nc.scalar.activation(ht[:], ps_w[:, 0:P], ACT.Copy).then_inc(ht_ready, 1)

            pipeline(act, TILES, U, [(0, exponent), (1, turn_out)] + ([(3, heads_out)] if first else []), peeled=1)
            act.wait_ge(filled, 16 * fills)

        @block.vector
        def _(dve):
            gate = k.gates[:, layer:layer + 1]

            def soften(it, kk):
                t, par = U * it + kk, kk % 2
                dve.wait_ge(scored, t + 1)
                if reused(t, 2):
                    dve.wait_ge(turned, t - 1)
                for G in range(2):
                    bias = k.bias0[:] if first else k.bias1[:, bass.ds(t, 1), :].rearrange("p a k -> p (a k)")
                    nc.vector.tensor_tensor(s_sb[par][:, 8 * G:8 * G + 8, :],
                                            ps_s[par][:, G, :].rearrange("p (h k) -> p h k", k=SEQ),
                                            spread(bias, 1, 8), ALU.add).then_inc(masked, 1)
                dve.wait_ge(masked, 2 * t + 2)
                nc.vector.tensor_reduce(top[par][:], s_sb[par][:], AX.X, ALU.max).then_inc(topped, 1)
                dve.wait_ge(topped, t + 1)
                nc.vector.tensor_tensor(s_sb[par][:], s_sb[par][:], spread(top[par][:], 2, SEQ),
                                        ALU.subtract).then_inc(shifted, 1)

            def divide(it, kk):
                t, par = U * it + kk, kk % 2
                dve.wait_ge(summed, t + 1)
                if first and reused(t, 2):
                    dve.wait_ge(heads_turned, t - 1)
                if not first and reused(t, 2):
                    dve.wait_ge(added, t - 1)
                for b in range(2):
                    rows = slice(HALF * b, HALF * b + HALF)
                    nc.vector.reciprocal(inv[par][rows, :].rearrange("p (u r) -> p u r", r=2),
                                         sums[rows, :, b, :, DK]).then_inc(inverted, 1)
                dve.wait_ge(inverted, 2 * t + 2)
                for b in range(2):
                    rows = slice(HALF * b, HALF * b + HALF)
                    nc.vector.tensor_tensor(
                        heads[par][rows, :].rearrange("p (u r c) -> p u r c", r=2, c=DK), sums[rows, :, b, :, 0:DK],
                        spread(inv[par][rows, :].rearrange("p (u r) -> p u r", r=2), 3, DK),
                        ALU.mult).then_inc(normalized, 1)

            def add(it, kk):
                t, par = U * it + kk, kk % 2
                if first:
                    dve.wait_ge(projected, t + 1)
                    src = ps_w[:, P:2 * P]
                else:
                    dve.wait_ge(normalized, 2 * t + 2)
                    src = heads[par][:]
                xt = k.x[:, bass.ds(t, 1), :].rearrange("p a d -> p (a d)")
                nc.vector.scalar_tensor_tensor(xt, src, gate, xt, ALU.mult, ALU.add).then_inc(added, 1)

            pipeline(dve, TILES, U, ([(4, add)] if first else [(3, add)]) + [(0, soften), (2, divide)], peeled=1)


def route(nc, k, layer):
    picks = layer + 1
    slots = SLOTS[layer]
    with ExitStack() as ctx:
        def sb(n, shape, dt=F32):
            return ctx.enter_context(nc.sbuf_tensor(f"ro{layer}_{n}", shape, dt))

        def ps(n):
            return ctx.enter_context(nc.psum_tensor(f"ro{layer}_{n}", [P, 512], F32))

        def sem(n):
            return ctx.enter_context(nc.semaphore(f"ro{layer}_{n}"))

        xn = [sb(f"xn{i}", [P, CHUNK, D]) for i in range(2)]
        xt = [sb(f"xt{i}", [P, CHUNK * P]) for i in range(2)]
        router = sb("router", [P, E])
        logits = sb("logits", [P, TILES, E])
        ps_t, ps_l = [ps(f"ps_t{i}") for i in range(2)], [ps(f"ps_l{i}") for i in range(2)]
        ps_c = [ps(f"ps_c{i}") for i in range(4)]
        work, prob = sb("work", [P, TILES, E]), sb("prob", [P, TILES, E])
        hot = [sb(f"hot{i}", [P, TILES, E]) for i in range(picks)]
        before = [sb(f"before{i}", [P, TILES, E]) for i in range(picks)]
        total = sb("total", [P, picks, E])
        m = [sb(f"m{i}", [P, TILES]) for i in range(picks)]
        col, inv_sum = sb("col", [P, TILES]), sb("inv_sum", [P, TILES])
        tiles_i, n_tiles = sb("tiles_i", [P, E], I32), sb("n_tiles", [P, E])
        ends, starts = sb("ends", [P, E]), sb("starts", [P, E])
        load_e = sb("load_e", [P, E])
        ge_end, row = sb("ge_end", [P, slots, E]), sb("row", [P, slots])

        setup, normed, transposed, xt_ready = sem("setup"), sem("normed"), sem("transposed"), sem("xt_ready")
        copied, logits_done, logits_out = sem("copied"), sem("logits_done"), sem("logits_out")
        steps, hot_ready, counted = sem("steps"), sem("hot_ready"), sem("counted")
        diff_ready, prob_ready = sem("diff_ready"), sem("prob_ready")
        block = ctx.enter_context(nc.Block())

        @block.sync
        def _(sp):
            sp.dma_start(router[:], k.routers[layer]).then_inc(setup, 16)

        @block.tensor
        def _(pe):
            ident = k.const[:, C_IDENT:C_IDENT + P]

            def transposes(it, par):
                c = 2 * it + par
                pe.wait_ge(normed, CHUNK * (c + 1))
                if reused(c, 2):
                    pe.wait_ge(xt_ready, c - 1)
                for j in range(CHUNK):
                    last = nc.tensor.transpose(ps_t[par][:, j * P:(j + 1) * P], xn[par][:, j, :], ident)
                last.then_inc(transposed, 1)

            def score(it, par):
                c = 2 * it + par
                if not reused(c, 1):
                    pe.wait_ge(setup, 16)
                pe.wait_ge(xt_ready, c + 1)
                if reused(c, 2):
                    pe.wait_ge(logits_out, c - 1)
                for j in range(CHUNK):
                    last = nc.tensor.matmul(ps_l[par][:, j * E:(j + 1) * E], xt[par][:, j * P:(j + 1) * P],
                                            router[:], start=True, stop=True)
                last.then_inc(logits_done, 1)

            pipeline(pe, CHUNKS, 2, [(0, transposes), (1, score)])
            for i in range(picks):
                pe.wait_ge(hot_ready, i + 1)
                chosen = hot[i][:].rearrange("p t e -> p (t e)")
                nc.tensor.matmul(ps_c[2 * i][:], k.const[:, C_TRI:C_TRI + P], chosen, start=True, stop=True)
                nc.tensor.matmul(ps_c[2 * i + 1][:], k.const[:, C_ONES:C_ONES + P], chosen,
                                 start=True, stop=True).then_inc(counted, 1)

        @block.scalar
        def _(act):
            def columns(it, par):
                c = 2 * it + par
                act.wait_ge(transposed, c + 1)
                if reused(c, 2):
                    act.wait_ge(logits_done, c - 1)
                    if not layer:
                        act.wait_ge(copied, c - 1)
                nc.scalar.activation(xt[par][:], ps_t[par][:], ACT.Copy).then_inc(xt_ready, 1)

            pipeline(act, CHUNKS, 2, [(0, columns)])
            act.wait_ge(diff_ready, 1)
            nc.scalar.activation(prob[:], work[:], ACT.Exp).then_inc(prob_ready, 1)

        @block.vector
        def _(dve):
            def norm(it, par):
                c = 2 * it + par
                if reused(c, 2):
                    dve.wait_ge(transposed, c - 1)
                for j in range(CHUNK):
                    normalize(nc, k, xn[par][:, j, :], c * CHUNK + j).then_inc(normed, 1)

            def keep_columns(it, par):
                c = 2 * it + par
                dve.wait_ge(xt_ready, c + 1)
                nc.vector.tensor_scalar(k.xnt[:, bass.ts(c, 512)], xt[par][:], 1.0, None,
                                        ALU.mult).then_inc(copied, 1)

            def keep_logits(it, par):
                c = 2 * it + par
                dve.wait_ge(logits_done, c + 1)
                nc.vector.tensor_scalar(logits[:, bass.ts(c, CHUNK), :],
                                        ps_l[par][:, 0:CHUNK * E].rearrange("p (t e) -> p t e", e=E),
                                        1.0, None, ALU.mult).then_inc(logits_out, 1)

            pipeline(dve, CHUNKS, 2, [(0, norm)] + ([] if layer else [(1, keep_columns)]) + [(2, keep_logits)])
            dve.wait_ge(logits_out, CHUNKS)
            do = Chain(dve, steps)
            first_of = spread(k.const[:, C_FIRST:C_FIRST + E], 1, TILES)

            def pick(i):
                do(nc.vector.tensor_reduce(m[i][:], logits[:], AX.X, ALU.max))
                do(nc.vector.tensor_tensor(work[:], logits[:], spread(m[i][:], 2, E), ALU.is_equal))
                do(nc.vector.tensor_tensor(work[:], work[:], first_of, ALU.mult))
                do(nc.vector.tensor_reduce(col[:], work[:], AX.X, ALU.max))
                nc.vector.tensor_tensor(hot[i][:], work[:], spread(col[:], 2, E), ALU.is_equal).then_inc(hot_ready, 1)
                dve.wait_ge(hot_ready, i + 1)

            pick(0)
            do(nc.vector.tensor_tensor(prob[:], logits[:], spread(m[0][:], 2, E), ALU.subtract))
            if picks == 2:
                do(nc.vector.scalar_tensor_tensor(logits[:], hot[0][:], -3.0e38, logits[:], ALU.mult, ALU.add))
                pick(1)
            nc.vector.tensor_copy(work[:], prob[:]).then_inc(diff_ready, 1)
            dve.wait_ge(prob_ready, 1)
            do(nc.vector.tensor_reduce(inv_sum[:], prob[:], AX.X, ALU.add))
            do(nc.vector.reciprocal(inv_sum[:], inv_sum[:]))

            for i in range(picks):
                dve.wait_ge(counted, i + 1)
                per_tile = ps_c[2 * i + 1][:].rearrange("p (t e) -> p t e", e=E)
                do(nc.vector.tensor_copy(work[:], per_tile))
                for e in range(E):
                    do(nc.vector.tensor_tensor_scan(before[i][:, :, e], k.const[:, C_ONES:C_ONES + TILES],
                                                    work[:, :, e], 0.0, ALU.mult, ALU.add))
                do(nc.vector.tensor_copy(total[:, i, :], before[i][:, TILES - 1, :]))
                do(nc.vector.tensor_tensor(before[i][:], before[i][:], work[:], ALU.subtract))
                do(nc.vector.tensor_tensor(before[i][:], before[i][:],
                                           ps_c[2 * i][:].rearrange("p (t e) -> p t e", e=E), ALU.add))

            def chosen(out, i, values):
                do(nc.vector.tensor_tensor(work[:], values, hot[i][:], ALU.mult))
                do(nc.vector.tensor_reduce(out, work[:], AX.X, ALU.add))

            if picks == 1:
                do(nc.vector.tensor_scalar(k.weight[0][:], inv_sum[:], 2.0, k.gates[:, 2:3], ALU.mult, ALU.mult))
                do(nc.vector.tensor_copy(load_e[:], total[:, 0, :]))
            else:
                gate1, gate2, denom = m[0], m[1], col
                do(nc.vector.tensor_copy(gate1[:], inv_sum[:]))
                chosen(gate2[:], 1, prob[:])
                do(nc.vector.tensor_tensor(gate2[:], gate2[:], inv_sum[:], ALU.mult))
                do(nc.vector.tensor_tensor(denom[:], gate1[:], gate2[:], ALU.add))
                do(nc.vector.tensor_scalar(denom[:], denom[:], 1e-9, None, ALU.add))
                do(nc.vector.reciprocal(denom[:], denom[:]))
                for i, gate in enumerate((gate1, gate2)):
                    do(nc.vector.tensor_tensor(gate[:], gate[:], denom[:], ALU.mult))
                    do(nc.vector.tensor_scalar(k.weight[i][:], gate[:], k.gates[:, 3:4], None, ALU.mult))
                chosen(gate1[:], 0, before[0][:])
                do(nc.vector.tensor_tensor(prob[:], before[1][:], spread(total[:, 0, :], 1, TILES), ALU.add))
                chosen(gate2[:], 1, prob[:])
                for i, pos in enumerate((gate1, gate2)):
                    do(nc.vector.tensor_scalar(pos[:], pos[:], float(CAP), None, ALU.is_lt))
                    do(nc.vector.tensor_tensor(k.weight[i][:], k.weight[i][:], pos[:], ALU.mult))
                do(nc.vector.tensor_tensor(load_e[:], total[:, 0, :], total[:, 1, :], ALU.add))
                do(nc.vector.tensor_tensor(before[0][:], before[0][:], before[1][:], ALU.add))

            do(nc.vector.tensor_scalar(n_tiles[:], load_e[:], P - 1.0, None, ALU.add))
            do(nc.vector.tensor_copy(tiles_i[:], n_tiles[:]))
            do(nc.vector.tensor_scalar(tiles_i[:], tiles_i[:], 7, None, ALU.arith_shift_right))
            do(nc.vector.tensor_copy(n_tiles[:], tiles_i[:]))
            do(nc.vector.tensor_scalar(n_tiles[:], n_tiles[:], float(P), None, ALU.mult))
            do(nc.vector.tensor_tensor_scan(ends[:], k.const[:, C_ONES:C_ONES + E], n_tiles[:], 0.0,
                                            ALU.mult, ALU.add))
            do(nc.vector.tensor_tensor(starts[:], ends[:], n_tiles[:], ALU.subtract))
            do(nc.vector.tensor_tensor(before[0][:], before[0][:], spread(starts[:], 1, TILES), ALU.add))
            for i in range(picks):
                chosen(col[:], i, before[0][:])
                do(nc.vector.tensor_copy(k.dest[i][:], col[:]))
            do(nc.vector.tensor_tensor(ge_end[:], spread(k.const[:, C_SLOT:C_SLOT + slots], 2, E),
                                       spread(ends[:], 1, slots), ALU.is_ge))
            do(nc.vector.tensor_reduce(row[:], ge_end[:], AX.X, ALU.add))
            do(nc.vector.tensor_scalar(row[:], row[:], E - 1.0, None, ALU.min))
            do(nc.vector.tensor_copy(k.slot_expert[:, 0:slots], row[:]))


def dispatch(nc, k, layer):
    picks = layer + 1
    shared = layer == 0
    with ExitStack() as ctx:
        def sb(n, shape, dt=F32):
            return ctx.enter_context(nc.sbuf_tensor(f"di{layer}_{n}", shape, dt))

        def ps(n):
            return ctx.enter_context(nc.psum_tensor(f"di{layer}_{n}", [P, 512], F32))

        def sem(n):
            return ctx.enter_context(nc.semaphore(f"di{layer}_{n}"))

        U = 8
        xn = [sb(f"xn{i}", [P, D]) for i in range(2)]
        to = [[sb(f"to{i}_{j}", [P, 1], I32) for i in range(2)] for j in range(picks)]
        if shared:
            wu, wg, wd = sb("wu", [P, F]), sb("wg", [P, F]), sb("wd", [P, FB, D])
            act_g = [sb(f"act_g{i}", [P, 512]) for i in range(2)]
            hid = [sb(f"hid{i}", [P, 512]) for i in range(8)]
            ps_u, ps_g, ps_y = ([ps(f"ps_{n}{i}") for i in range(2)] for n in "ugy")
        setup, ticks = sem("setup"), sem("ticks")
        normed, indexed = sem("normed"), sem("indexed")
        scattered = [sem(f"scattered{i}") for i in range(2)]
        projected, gated, multiplied, summed, added = (
            sem("projected"), sem("gated"), sem("multiplied"), sem("summed"), sem("added"))
        block = ctx.enter_context(nc.Block())

        @block.sync
        def _(sp):
            if shared:
                sp.dma_start(wu[:], k.shared_up).then_inc(setup, 16)
                sp.dma_start(wg[:], k.shared_gate).then_inc(setup, 16)
                sp.dma_start(wd[:], k.shared_down.rearrange("(c p) d -> p c d", p=P)).then_inc(setup, 16)

        @block.gpsimd
        def _(pool):
            def scatter(it, kk):
                t, par = U * it + kk, kk % 2
                n = U // 2 * it + kk // 2
                if reused(t, 2):
                    pool.wait_ge(scattered[par], 16 * picks * n)
                for i in range(picks):
                    nc.gpsimd.tensor_copy(to[i][par][:], k.dest[i][:, bass.ds(t, 1)]).then_inc(indexed, 1)
                pool.wait_ge(indexed, picks * (t + 1))
                pool.wait_ge(normed, t + 1)
                absorb(pool, ticks)
                for i in range(picks):
                    nc.gpsimd.indirect_dma_start(k.xs[layer], bass.IndirectOffsetOnAxis(ap=to[i][par][:, 0:1], axis=0),
                                                 xn[par][:], None).then_inc(scattered[par], 16)

            pipeline(pool, TILES, U, [(0, scatter)])
            for par in range(2):
                pool.wait_ge(scattered[par], 16 * picks * TILES // 2)

        @block.vector
        def _(dve):
            def norm(it, kk):
                t, par = U * it + kk, kk % 2
                if reused(t, 2):
                    dve.wait_ge(scattered[par], 16 * picks * (U // 2 * it + kk // 2))
                normalize(nc, k, xn[par][:], t).then_inc(normed, 1)

            def multiply(it, kk):
                w, par = U * it + kk, kk % 2
                dve.wait_ge(gated, w + 1)
                if reused(w, 8):
                    dve.wait_ge(summed, 2 * it + kk // 4 - 1)
                nc.vector.tensor_tensor(hid[kk][:], act_g[par][:], ps_u[par][:], ALU.mult).then_inc(multiplied, 1)

            def add(it, kk):
                if kk % CHUNK != CHUNK - 1:
                    return
                c = 2 * it + kk // CHUNK
                dve.wait_ge(summed, c + 1)
                dve.wait_ge(normed, CHUNK * (c + 1))
                xc = k.x[:, bass.ts(c, CHUNK), :]
                nc.vector.scalar_tensor_tensor(xc, ps_y[kk // CHUNK][:].rearrange("p (t d) -> p t d", d=D),
                                               k.gates[:, 2:3], xc, ALU.mult, ALU.add).then_inc(added, 1)

            pipeline(dve, TILES, U, [(0, norm)] + ([(0, multiply), (4, add)] if shared else []))

        if shared:
            @block.tensor
            def _(pe):
                def project_up(it, kk):
                    w, par, f = U * it + kk, kk % 2, kk % FB
                    if not reused(w, 1):
                        pe.wait_ge(setup, 16 * 3)
                    if reused(w, 2):
                        pe.wait_ge(multiplied, w - 1)
                    cols = k.xnt[:, bass.ts(2 * it + kk // CHUNK, 512)]
                    nc.tensor.matmul(ps_g[par][:], wg[:, f * P:(f + 1) * P], cols, start=True, stop=True)
                    nc.tensor.matmul(ps_u[par][:], wu[:, f * P:(f + 1) * P], cols,
                                     start=True, stop=True).then_inc(projected, 1)

                def project_down(it, kk):
                    if kk % CHUNK != CHUNK - 1:
                        return
                    c, par = 2 * it + kk // CHUNK, kk // CHUNK
                    pe.wait_ge(multiplied, CHUNK * (c + 1))
                    if reused(c, 2):
                        pe.wait_ge(added, c - 1)
                    for j in range(CHUNK):
                        for f in range(FB):
                            last = nc.tensor.matmul(ps_y[par][:, j * P:(j + 1) * P],
                                                    hid[4 * par + f][:, j * P:(j + 1) * P], wd[:, f, :],
                                                    start=f == 0, stop=f == FB - 1)
                    last.then_inc(summed, 1)

                pipeline(pe, TILES, U, [(0, project_up), (2, project_down)])

            @block.scalar
            def _(act):
                def gate(it, kk):
                    w, par = U * it + kk, kk % 2
                    act.wait_ge(projected, w + 1)
                    if reused(w, 2):
                        act.wait_ge(multiplied, w - 1)
                    nc.scalar.activation(act_g[par][:], ps_g[par][:], ACT.Silu).then_inc(gated, 1)

                pipeline(act, TILES, U, [(0, gate)])


def experts(nc, k, layer):
    slots = SLOTS[layer]
    swiglu = layer == 0
    with ExitStack() as ctx:
        def sb(n, shape, dt=F32):
            return ctx.enter_context(nc.sbuf_tensor(f"ex{layer}_{n}", shape, dt))

        def ps(n):
            return ctx.enter_context(nc.psum_tensor(f"ex{layer}_{n}", [P, 512], F32))

        def sem(n):
            return ctx.enter_context(nc.semaphore(f"ex{layer}_{n}"))

        U = 4
        w_in = sb("w_in", [P, E * F])
        w_out = sb("w_out", [P, E * FB * D])
        if swiglu:
            w_gate = sb("w_gate", [P, E * F])
            act_g = [sb(f"act_g{i}", [P, F]) for i in range(2)]
        else:
            b1, b2 = sb("b1", [P, E * F]), sb("b2", [P, E * D])
        xs = [sb(f"xs{i}", [P, D]) for i in range(4)]
        xt = [sb(f"xt{i}", [P, P]) for i in range(2)]
        hid = [sb(f"hid{i}", [P, F]) for i in range(2)]
        ht = [sb(f"ht{i}", [P, FB, P]) for i in range(2)]
        y = [sb(f"y{i}", [P, D]) for i in range(2)]
        ps_x, ps_y = ps("ps_x"), ps("ps_y")
        ps_u, ps_h = [ps(f"ps_u{i}") for i in range(2)], [ps(f"ps_h{i}") for i in range(2)]
        ps_g = [ps(f"ps_g{i}") for i in range(2)] if swiglu else None
        setup, cleared = sem("setup"), sem("cleared")
        rows_in = [sem(f"rows_in{i}") for i in range(4)]
        x_turned, xt_ready, projected, gated = sem("x_turned"), sem("xt_ready"), sem("projected"), sem("gated")
        hid_ready, h_turned, ht_ready, summed, y_ready = (
            sem("hid_ready"), sem("h_turned"), sem("ht_ready"), sem("summed"), sem("y_ready"))
        stored = [sem(f"stored{i}") for i in range(2)]
        given = E - 1 if swiglu else E
        loads = 3 if swiglu else 4
        block = ctx.enter_context(nc.Block())

        def expert_of(eng, s):
            return eng.value_load(k.slot_expert[0:1, bass.ds(s, 1)], min_val=0, max_val=E - 1)

        @block.sync
        def _(sp):
            w1, wd = (k.up, k.down) if swiglu else (k.w1, k.w2)
            sp.dma_start(w_in[:, 0:given * F].rearrange("p (e f) -> p e f", e=given),
                         w1.rearrange("e p f -> p e f")).then_inc(setup, 16)
            if swiglu:
                sp.dma_start(w_gate[:, 0:given * F].rearrange("p (e f) -> p e f", e=given),
                             k.gate.rearrange("e p f -> p e f")).then_inc(setup, 16)
            else:
                sp.dma_start(b1[:], k.b1.rearrange("e f -> (e f)").partition_broadcast(P)).then_inc(setup, 16)
                sp.dma_start(b2[:], k.b2.rearrange("e d -> (e d)").partition_broadcast(P)).then_inc(setup, 16)
            sp.dma_start(w_out[:, 0:given * FB * D].rearrange("p (e c d) -> p e c d", e=given, c=FB),
                         wd.rearrange("e (c p) d -> p e c d", p=P)).then_inc(setup, 16)

            def load(it, kk):
                s = U * it + kk
                if reused(s, 4):
                    sp.wait_ge(x_turned, s - 3)
                sp.dma_start(xs[kk][:], k.xs[layer][bass.ts(s, P), :]).then_inc(rows_in[kk], 16)

            pipeline(sp, slots, U, [(0, load)])

        @block.gpsimd
        def _(pool):
            if swiglu:
                nc.gpsimd.memset(w_in[:, given * F:], 0.0).then_inc(cleared, 1)
                nc.gpsimd.memset(w_gate[:, given * F:], 0.0).then_inc(cleared, 1)
                nc.gpsimd.memset(w_out[:, given * FB * D:], 0.0).then_inc(cleared, 1)

            def store(it, kk):
                s, par = U * it + kk, kk % 2
                pool.wait_ge(y_ready, s + 1)
                pool.dma_start(k.ys[layer][bass.ts(s, P), :], y[par][:]).then_inc(stored[par], 16)

            pipeline(pool, slots, U, [(0, store)])
            for par in range(2):
                pool.wait_ge(stored[par], 16 * slots // 2)

        @block.tensor
        def _(pe):
            ident = k.const[:, C_IDENT:C_IDENT + P]
            pe.wait_ge(setup, 16 * loads)
            if swiglu:
                pe.wait_ge(cleared, 3)

            def turn_x(it, kk):
                s, par = U * it + kk, kk % 2
                pe.wait_ge(rows_in[kk], 16 * (it + 1))
                if reused(s, 1):
                    pe.wait_ge(xt_ready, s)
                nc.tensor.transpose(ps_x[:, 0:P], xs[kk][:], ident).then_inc(x_turned, 1)

            def project_in(it, kk):
                s, par = U * it + kk, kk % 2
                e = expert_of(pe, s)
                pe.wait_ge(xt_ready, s + 1)
                if reused(s, 2):
                    pe.wait_ge(hid_ready, s - 1)
                if swiglu:
                    nc.tensor.matmul(ps_g[par][:], xt[par][:], w_gate[:, bass.ts(e, F)], start=True, stop=True)
                nc.tensor.matmul(ps_u[par][:], xt[par][:], w_in[:, bass.ts(e, F)],
                                 start=True, stop=True).then_inc(projected, 1)

            def turn_h(it, kk):
                s, par = U * it + kk, kk % 2
                pe.wait_ge(hid_ready, s + 1)
                if reused(s, 2):
                    pe.wait_ge(ht_ready, s - 1)
                for c in range(FB):
                    last = nc.tensor.transpose(ps_h[par][:, c * P:(c + 1) * P], hid[par][:, c * P:(c + 1) * P], ident)
                last.then_inc(h_turned, 1)

            def project_out(it, kk):
                s, par = U * it + kk, kk % 2
                e = expert_of(pe, s)
                pe.wait_ge(ht_ready, s + 1)
                if reused(s, 1):
                    pe.wait_ge(y_ready, s)
                for c in range(FB):
                    last = nc.tensor.matmul(ps_y[:, 0:D], ht[par][:, c, :],
                                            w_out[:, bass.ds(e * (FB * D) + c * D, D)],
                                            start=c == 0, stop=c == FB - 1)
                last.then_inc(summed, 1)

            pipeline(pe, slots, U, [(0, turn_x), (1, project_in), (2, turn_h), (3, project_out)])

        @block.scalar
        def _(act):
            def x_out(it, kk):
                s, par = U * it + kk, kk % 2
                act.wait_ge(x_turned, s + 1)
                if reused(s, 2):
                    act.wait_ge(projected, s - 1)
                nc.scalar.activation(xt[par][:], ps_x[:, 0:P], ACT.Copy).then_inc(xt_ready, 1)

            def gate(it, kk):
                s, par = U * it + kk, kk % 2
                act.wait_ge(projected, s + 1)
                if reused(s, 2):
                    act.wait_ge(hid_ready, s - 1)
                nc.scalar.activation(act_g[par][:], ps_g[par][:], ACT.Silu).then_inc(gated, 1)

            def h_out(it, kk):
                s, par = U * it + kk, kk % 2
                act.wait_ge(h_turned, s + 1)
                if reused(s, 2):
                    act.wait_ge(summed, s - 1)
                nc.scalar.activation(ht[par][:].rearrange("p c t -> p (c t)"), ps_h[par][:],
                                     ACT.Copy if swiglu else ACT.Gelu).then_inc(ht_ready, 1)

            pipeline(act, slots, U, [(0, x_out)] + ([(1, gate)] if swiglu else []) + [(2, h_out)])

        @block.vector
        def _(dve):
            if not swiglu:
                dve.wait_ge(setup, 16 * loads)

            def hidden(it, kk):
                s, par = U * it + kk, kk % 2
                if swiglu:
                    dve.wait_ge(gated, s + 1)
                else:
                    e = expert_of(dve, s)
                    dve.wait_ge(projected, s + 1)
                if reused(s, 2):
                    dve.wait_ge(h_turned, s - 1)
                other = act_g[par][:] if swiglu else b1[:, bass.ts(e, F)]
                nc.vector.tensor_tensor(hid[par][:], ps_u[par][:], other,
                                        ALU.mult if swiglu else ALU.add).then_inc(hid_ready, 1)

            def output(it, kk):
                s, par = U * it + kk, kk % 2
                if not swiglu:
                    e = expert_of(dve, s)
                dve.wait_ge(summed, s + 1)
                if reused(s, 2):
                    dve.wait_ge(stored[par], 16 * (2 * it + kk // 2))
                if swiglu:
                    nc.vector.tensor_copy(y[par][:], ps_y[:, 0:D]).then_inc(y_ready, 1)
                else:
                    nc.vector.tensor_tensor(y[par][:], ps_y[:, 0:D], b2[:, bass.ts(e, D)],
                                            ALU.add).then_inc(y_ready, 1)

            pipeline(dve, slots, U, [(1, hidden), (3, output)])


def combine(nc, k, layer):
    picks = layer + 1
    with ExitStack() as ctx:
        def sem(n):
            return ctx.enter_context(nc.semaphore(f"co{layer}_{n}"))

        U = 4
        rows = [[ctx.enter_context(nc.sbuf_tensor(f"co{layer}_rows{i}_{j}", [P, D], F32)) for i in range(U)]
                for j in range(picks)]
        at = [[ctx.enter_context(nc.sbuf_tensor(f"co{layer}_at{i}_{j}", [P, 1], I32)) for i in range(U)]
              for j in range(picks)]
        indexed, added, stored, ticks = sem("indexed"), sem("added"), sem("stored"), sem("ticks")
        gathered = [sem(f"gathered{i}") for i in range(U)]
        block = ctx.enter_context(nc.Block())

        @block.gpsimd
        def _(pool):
            def gather(it, kk):
                t = U * it + kk
                if reused(t, U):
                    pool.wait_ge(added, picks * (t - U + 1))
                for i in range(picks):
                    nc.gpsimd.tensor_copy(at[i][kk][:], k.dest[i][:, bass.ds(t, 1)]).then_inc(indexed, 1)
                pool.wait_ge(indexed, picks * (t + 1))
                absorb(pool, ticks)
                for i in range(picks):
                    nc.gpsimd.indirect_dma_start(rows[i][kk][:], None, k.ys[layer],
                                                 bass.IndirectOffsetOnAxis(ap=at[i][kk][:, 0:1], axis=0)
                                                 ).then_inc(gathered[kk], 16)

            pipeline(pool, TILES, U, [(0, gather)])

        @block.vector
        def _(dve):
            def add(it, kk):
                t = U * it + kk
                xt = k.x[:, bass.ds(t, 1), :].rearrange("p a d -> p (a d)")
                dve.wait_ge(gathered[kk], 16 * picks * (it + 1))
                for i in range(picks):
                    if i:
                        dve.wait_ge(added, picks * t + i)
                    nc.vector.scalar_tensor_tensor(xt, rows[i][kk][:], k.weight[i][:, bass.ds(t, 1)], xt,
                                                   ALU.mult, ALU.add).then_inc(added, 1)

            pipeline(dve, TILES, U, [(0, add)])

        if layer:
            @block.sync
            def _(sp):
                ov = k.out.rearrange("(t p) d -> p t d", p=P)

                def store(it, par):
                    c = 2 * it + par
                    sp.wait_ge(added, picks * CHUNK * (c + 1))
                    sp.dma_start(ov[:, bass.ts(c, CHUNK), :], k.x[:, bass.ts(c, CHUNK), :]).then_inc(stored, 16)

                pipeline(sp, CHUNKS, 2, [(0, store)])
                sp.wait_ge(stored, 16 * CHUNKS)


def clear_semaphores(nc, numbers):
    with nc.Block() as block:
        @block.gpsimd
        def _(pool):
            pool.sem_clear(numbers)


class Tensors:
    pass


def build(nc, tensors):
    k = tensors
    k.qt = nc.dram_tensor("qt", (D, TOKENS), F32).ap()
    k.kt = nc.dram_tensor("kt", (D, TOKENS), F32).ap()
    k.v = nc.dram_tensor("v", (TOKENS, D), F32).ap()
    k.xs = [nc.dram_tensor(f"slot_x{i}", (SLOTS[i] * P, D), F32).ap() for i in range(2)]
    k.ys = [nc.dram_tensor(f"slot_y{i}", (SLOTS[i] * P, D), F32).ap() for i in range(2)]
    with ExitStack() as ctx:
        def sb(n, shape, dt=F32):
            return ctx.enter_context(nc.sbuf_tensor(n, shape, dt))

        k.x = sb("x", [P, TILES, D])
        k.const = sb("const", [P, C_ALL])
        k.gates = sb("gates", [P, 4])
        k.mean, k.rstd = sb("mean", [P, TILES]), sb("rstd", [P, TILES])
        k.weight = [sb(f"weight{i}", [P, TILES]) for i in range(2)]
        k.dest = [sb(f"dest{i}", [P, TILES], I32) for i in range(2)]
        k.slot_expert = sb("slot_expert", [P, MAX_SLOTS], I32)
        numbers = range(min(nc.free_semaphores), max(nc.free_semaphores) + 1)
        load_inputs(nc, k)
        for layer in range(2):
            if layer:
                clear_semaphores(nc, numbers)
            with ExitStack() as own:
                if layer == 0:
                    k.mask0 = own.enter_context(nc.sbuf_tensor("mask0", [P, SEQ], I32))
                    k.bias0 = own.enter_context(nc.sbuf_tensor("bias0", [P, SEQ], F32))
                else:
                    k.mask1 = own.enter_context(nc.sbuf_tensor("mask1", [P, TILES, SEQ], I32))
                    k.bias1 = own.enter_context(nc.sbuf_tensor("bias1", [P, TILES, SEQ], F32))
                layer_stats(nc, k, f"lnq{layer}")
                project(nc, k, layer)
                attend(nc, k, layer)
            with ExitStack() as own:
                layer_stats(nc, k, f"lnf{layer}")
                if layer == 0:
                    k.xnt = own.enter_context(nc.sbuf_tensor("xnt", [P, TOKENS], F32))
                route(nc, k, layer)
                dispatch(nc, k, layer)
            experts(nc, k, layer)
            combine(nc, k, layer)


def kernel(**inputs):
    import concourse.bacc as bacc
    from concourse.bass_utils import run_bass_kernel_spmd

    a = {n: np.asarray(v) for n, v in inputs.items()}
    ctx = a["ctx_1024"].reshape(TOKENS, D)
    given = {
        "x_in": a["x"].reshape(TOKENS, D),
        "ctx_in": ctx,
        "ctxt_in": ctx.T,
        "mask0_in": a["mask_1x1xSxS2_ik0"].reshape(SEQ, SEQ),
        "mask1_in": a["mask_BxSxS2_ik1"],
        "g_xattn": a["g_xattn"],
        "g_ffn": a["g_ffn"],
        "wq": a["L0_xattn_wq_w"].T,
        "wk": a["L0_xattn_wk_w"].T,
        "wv": a["L0_xattn_wv_w"].T,
        "wo": a["L0_xattn_wo_w"].T,
        "bq": a["L0_xattn_wq_b"].reshape(D, 1),
        "bk": a["L0_xattn_wk_b"].reshape(D, 1),
        "bv": a["L0_xattn_wv_b"],
        "bo": a["L0_xattn_wo_b"],
        "router0": a["L0_ffn_Wr"],
        "router1": a["L1_ffn_Wg"],
        "up": a["L0_ffn_Wu"],
        "gate": a["L0_ffn_Wg"],
        "down": a["L0_ffn_Wd"],
        "shared_up": a["L0_ffn_Wu_s"],
        "shared_gate": a["L0_ffn_Wg_s"],
        "shared_down": a["L0_ffn_Wd_s"],
        "w1": a["L1_ffn_W1"],
        "b1": a["L1_ffn_b1"],
        "w2": a["L1_ffn_W2"],
        "b2": a["L1_ffn_b2"],
        "const_in": constants(),
    }
    given = {n: np.ascontiguousarray(v) for n, v in given.items()}
    nc = bacc.Bacc("TRN2", target_bir_lowering=False, num_devices=1)
    t = Tensors()
    for n, v in given.items():
        t.__dict__[n] = nc.dram_tensor(n, v.shape, mybir.dt.from_np(v.dtype), kind="ExternalInput").ap()
    t.out = nc.dram_tensor("out", (TOKENS, D), F32, kind="ExternalOutput").ap()
    t.routers = [t.router0, t.router1]
    build(nc, t)
    result = run_bass_kernel_spmd(nc, [given], core_ids=[0])
    return result.results[0]["out"].reshape(BATCH, SEQ, D)
```

```python
from contextlib import ExitStack

import numpy as np

import concourse.bass as bass
from concourse import mybir

F32 = mybir.dt.float32
I32 = mybir.dt.int32
ALU = mybir.AluOpType
ACT = mybir.ActivationFunctionType
AX = mybir.AxisListType

P = 128
SEQ = 64
BATCH = 128
D = 128
HEADS = 16
DK = D // HEADS
TOKENS = BATCH * SEQ
TILES = TOKENS // P
CHUNK = 4
CHUNKS = TILES // CHUNK
E = 8
F = 512
FB = F // P
NEG = 1.0e9
EPS = 1e-5
CAP = 2 * 2 * TOKENS // E
SLOTS = (TOKENS // P + E, 2 * TOKENS // P + E)
MAX_SLOTS = max(SLOTS)

C_IDENT, C_TRI, C_ONES = 0, P, 2 * P
C_HEAD = 3 * P
C_HALF = C_HEAD + 4
C_FIRST = C_HALF + 2
C_EXPERT = C_FIRST + E
C_SLOT = C_EXPERT + E
C_ALL = C_SLOT + MAX_SLOTS


def constants():
    c = np.zeros((P, C_ALL), np.float32)
    c[:, C_IDENT:C_IDENT + P] = np.eye(P)
    c[:, C_TRI:C_TRI + P] = np.triu(np.ones((P, P)), 1)
    c[:, C_ONES:C_ONES + P] = 1.0
    c[:, C_HEAD:C_HEAD + 4] = (np.arange(P)[:, None] % 32) // DK == np.arange(4)
    c[:, C_HALF:C_HALF + 2] = np.arange(P)[:, None] // (P // 2) == np.arange(2)
    c[:, C_FIRST:C_FIRST + E] = E - np.arange(E)
    c[:, C_EXPERT:C_EXPERT + E] = np.arange(E)
    c[:, C_SLOT:C_SLOT + MAX_SLOTS] = P * np.arange(MAX_SLOTS)
    return c


def spread(ap, dim, n):
    ap = ap.unsqueeze(dim)
    shape = list(ap.shape)
    shape[dim] = n
    return ap.broadcast_to(shape)


def pipeline(eng, tiles, unroll, stages, peeled=2):
    last = max(lag for lag, _ in stages)
    assert last <= unroll and tiles % unroll == 0

    def step(it, k, t):
        for lag, f in stages:
            if t is None or 0 <= t - lag < tiles:
                q, r = divmod(k - lag, unroll)
                f(it + q, r)

    for t in range(peeled * unroll):
        step(t // unroll, t % unroll, t)
    with eng.Fori(peeled, tiles // unroll) as it:
        for k in range(unroll):
            step(it, k, None)
    for k in range(last):
        step(tiles // unroll, k, tiles + k)


def reused(t, buffers):
    return not isinstance(t, int) or t >= buffers


def absorb(eng, ticks):
    eng.sem_inc(ticks, 1)


class Chain:

    def __init__(self, eng, sem):
        self.eng, self.sem, self.n = eng, sem, 0

    def __call__(self, instruction):
        self.n += 1
        instruction.then_inc(self.sem, 1)
        self.eng.wait_ge(self.sem, self.n)


def load_inputs(nc, k):
    with ExitStack() as ctx:
        arrived = ctx.enter_context(nc.semaphore("inputs_arrived"))
        ready = ctx.enter_context(nc.semaphore("gates_ready"))
        counted = ctx.enter_context(nc.semaphore("inputs_counted"))
        block = ctx.enter_context(nc.Block())

        @block.sync
        def _(sp):
            n = 0
            xv = k.x_in.rearrange("(t p) d -> p t d", p=P)
            for a in range(0, TILES, TILES // 4):
                sp.dma_start(k.x[:, a:a + TILES // 4, :], xv[:, a:a + TILES // 4, :]).then_inc(arrived, 16)
                n += 1
            sp.dma_start(k.const[:], k.const_in).then_inc(arrived, 16)
            sp.dma_start(k.gates[:, 0:2], k.g_xattn.partition_broadcast(P)).then_inc(arrived, 16)
            sp.dma_start(k.gates[:, 2:4], k.g_ffn.partition_broadcast(P)).then_inc(arrived, 16)
            sp.wait_ge(arrived, 16 * (n + 3))

        @block.vector
        def _(dve):
            dve.wait_ge(arrived, 16 * 7)
            with dve.Fori(0, TILES // 16) as it:
                for i in range(16):
                    gather_stats(nc, k, 16 * it + i).then_inc(counted, 1)
            dve.wait_ge(counted, TILES)

        @block.scalar
        def _(act):
            act.wait_ge(arrived, 16 * 7)
            nc.scalar.activation(k.gates[:], k.gates[:], ACT.Tanh).then_inc(ready, 1)


def gather_stats(nc, k, t):
    return nc.vector.bn_stats(k.stats[:, bass.ds(t, 1), :].rearrange("p a s -> p (a s)"),
                              k.x[:, bass.ds(t, 1), :].rearrange("p a s -> p (a s)"))


def layer_stats(nc, k, name):
    with ExitStack() as ctx:
        def sb(n, shape):
            return ctx.enter_context(nc.sbuf_tensor(f"{name}_{n}", shape, F32))

        stats = k.stats
        a, b, c, v = (sb(n, [P, TILES]) for n in ("a", "b", "c", "v"))
        steps = ctx.enter_context(nc.semaphore(f"{name}_steps"))
        var_ready = ctx.enter_context(nc.semaphore(f"{name}_var_ready"))
        root_ready = ctx.enter_context(nc.semaphore(f"{name}_root_ready"))
        block = ctx.enter_context(nc.Block())

        @block.vector
        def _(dve):
            do = Chain(dve, steps)
            mean_e, m2_e, mean_o, m2_o = (stats[:, :, i] for i in (1, 2, 4, 5))
            do(nc.vector.tensor_tensor(a[:], mean_e, mean_o, ALU.add))
            do(nc.vector.tensor_tensor(b[:], mean_e, mean_o, ALU.subtract))
            do(nc.vector.tensor_tensor(c[:], m2_e, m2_o, ALU.add))
            do(nc.vector.tensor_scalar(k.mean[:], a[:], 0.5, None, ALU.mult))
            do(nc.vector.tensor_tensor(b[:], b[:], b[:], ALU.mult))
            do(nc.vector.scalar_tensor_tensor(v[:], b[:], D / 4.0, c[:], ALU.mult, ALU.add))
            nc.vector.tensor_scalar(v[:], v[:], 1.0 / D, EPS, ALU.mult, ALU.add).then_inc(var_ready, 1)
            dve.wait_ge(root_ready, 1)
            do(nc.vector.reciprocal(a[:], a[:]))
            do(nc.vector.tensor_tensor(b[:], a[:], a[:], ALU.mult))
            do(nc.vector.tensor_tensor(b[:], b[:], v[:], ALU.mult))
            do(nc.vector.tensor_scalar(b[:], b[:], -0.5, 1.5, ALU.mult, ALU.add))
            do(nc.vector.tensor_tensor(k.rstd[:], a[:], b[:], ALU.mult))

        @block.scalar
        def _(act):
            act.wait_ge(var_ready, 1)
            nc.scalar.activation(a[:], v[:], ACT.Sqrt).then_inc(root_ready, 1)


def normalize(nc, k, out, t):
    return nc.vector.tensor_scalar(out, k.x[:, bass.ds(t, 1), :].rearrange("p a d -> p (a d)"),
                                   k.mean[:, bass.ds(t, 1)], k.rstd[:, bass.ds(t, 1)],
                                   ALU.subtract, ALU.mult)


def project(nc, k, layer):
    first = layer == 0
    with ExitStack() as ctx:
        def sb(n, shape, dt=F32):
            return ctx.enter_context(nc.sbuf_tensor(f"pj{layer}_{n}", shape, dt))

        def ps(n):
            return ctx.enter_context(nc.psum_tensor(f"pj{layer}_{n}", [P, 512], F32))

        def sem(n):
            return ctx.enter_context(nc.semaphore(f"pj{layer}_{n}"))

        xn = [sb(f"xn{i}", [P, CHUNK, D]) for i in range(2)]
        xt = [sb(f"xt{i}", [P, CHUNK * P]) for i in range(2)]
        q_sb = [sb(f"q{i}", [P, CHUNK * P]) for i in range(2)]
        ps_t = [ps(f"ps_t{i}") for i in range(2)]
        if first:
            ctxt = [sb(f"ctxt{i}", [P, CHUNK * P]) for i in range(2)]
            k_sb = [sb(f"k{i}", [P, CHUNK * P]) for i in range(2)]
            v_sb = [sb(f"v{i}", [P, CHUNK, D]) for i in range(2)]
            ps_q, ps_k, ps_v = ([ps(f"ps_{n}{i}") for i in range(2)] for n in "qkv")
            wq, wk, wv = (sb(f"w{n}", [P, D]) for n in "qkv")
            bq, bk = sb("bq", [P, 1]), sb("bk", [P, 1])
            bv, bo = sb("bv", [P, D]), sb("bo", [P, D])
            mask01 = sb("mask01", [P, SEQ])
            keep_col = sb("keep_col", [P, 1])
            keep = sb("keep", [P, SEQ])

        setup = sem("setup")
        steps = sem("steps")
        keep_col_ready, keep_summed = sem("keep_col_ready"), sem("keep_summed")
        ctx_in = [sem(f"ctx_in{i}") for i in range(2)]
        biased = sem("biased")
        normed, transposed, xt_ready = sem("normed"), sem("transposed"), sem("xt_ready")
        q_done, k_done, v_done = sem("q_done"), sem("k_done"), sem("v_done")
        q_ready, k_ready, v_ready = sem("q_ready"), sem("k_ready"), sem("v_ready")
        stored = [sem(f"stored{i}") for i in range(2)]
        outs = 3 if first else 1
        block = ctx.enter_context(nc.Block())

        @block.sync
        def _(sp):
            if first:
                for dst, src in ((wq, k.wq), (wk, k.wk), (wv, k.wv), (bq, k.bq), (bk, k.bk)):
                    sp.dma_start(dst[:], src).then_inc(setup, 16)
                sp.dma_start(bv[:], k.bv.partition_broadcast(P)).then_inc(setup, 16)
                sp.dma_start(bo[:], k.bo.partition_broadcast(P)).then_inc(setup, 16)
                for b in range(2):
                    sp.dma_start(k.mask0[b * SEQ:(b + 1) * SEQ, :], k.mask0_in).then_inc(setup, 16)
            else:
                sp.dma_start(k.mask1[:], k.mask1_in.rearrange("(t b) q k -> (b q) t k", b=2)).then_inc(setup, 16)

            def load(it, par):
                c = 2 * it + par
                if reused(c, 2):
                    sp.wait_ge(v_done, c - 1)
                sp.dma_start(ctxt[par][:], k.ctxt_in[:, bass.ts(c, 512)]).then_inc(ctx_in[par], 16)

            def store(it, par):
                c = 2 * it + par
                sp.wait_ge(q_ready, c + 1)
                sp.dma_start(k.qt[:, bass.ts(c, 512)], q_sb[par][:]).then_inc(stored[par], 16)
                if first:
                    sp.wait_ge(k_ready, c + 1)
                    sp.dma_start(k.kt[:, bass.ts(c, 512)], k_sb[par][:]).then_inc(stored[par], 16)
                    sp.wait_ge(v_ready, c + 1)
                    sp.dma_start(k.v.rearrange("(t p) d -> p t d", p=P)[:, bass.ts(c, CHUNK), :],
                                 v_sb[par][:]).then_inc(stored[par], 16)

            pipeline(sp, CHUNKS, 2, ([(0, load)] if first else []) + [(1, store)])
            for par in range(2):
                sp.wait_ge(stored[par], 16 * outs * CHUNKS // 2)

        @block.vector
        def _(dve):
            do = Chain(dve, steps)
            if first:
                dve.wait_ge(setup, 16 * 9)
                do(nc.vector.tensor_scalar(mask01[:], k.mask0[:], 0.0, None, ALU.not_equal))
                nc.vector.tensor_reduce(keep_col[:], mask01[:], AX.X, ALU.max).then_inc(keep_col_ready, 1)
                do(nc.vector.tensor_scalar(k.bias0[:], mask01[:], -1.0, NEG, ALU.add, ALU.mult))
                do(nc.vector.tensor_scalar(bo[:], bo[:], k.gates[:, 0:1], None, ALU.mult))
                dve.wait_ge(keep_summed, 1)
                do(nc.vector.tensor_scalar(keep[:], ps_k[0][:, 0:SEQ], DK ** -0.5, None, ALU.mult))
            else:
                dve.wait_ge(setup, 16)
                do(nc.vector.tensor_scalar(k.bias1[:], k.mask1[:], -1.0, NEG, ALU.add, ALU.mult))

            def norm(it, par):
                c = 2 * it + par
                if reused(c, 2):
                    dve.wait_ge(transposed, c - 1)
                for j in range(CHUNK):
                    normalize(nc, k, xn[par][:, j, :], c * CHUNK + j).then_inc(normed, 1)

            def queries(it, par):
                c = 2 * it + par
                dve.wait_ge(q_done, c + 1)
                if reused(c, 2):
                    dve.wait_ge(stored[par], 16 * outs * it)
                nc.vector.scalar_tensor_tensor(
                    q_sb[par][:].rearrange("p (s q) -> p s q", q=SEQ),
                    ps_q[par][:].rearrange("p (s q) -> p s q", q=SEQ), bq[:, 0:1],
                    spread(keep[:], 1, 2 * CHUNK), ALU.add, ALU.mult).then_inc(q_ready, 1)

            def values(it, par):
                c = 2 * it + par
                dve.wait_ge(v_done, c + 1)
                if reused(c, 2):
                    dve.wait_ge(stored[par], 16 * outs * it)
                nc.vector.tensor_tensor(v_sb[par][:], ps_v[par][:].rearrange("p (t d) -> p t d", d=D),
                                        spread(bv[:], 1, CHUNK), ALU.add).then_inc(v_ready, 1)

            def out_bias(it, par):
                c = 2 * it + par
                dve.wait_ge(normed, CHUNK * (c + 1))
                xc = k.x[:, bass.ts(c, CHUNK), :]
                nc.vector.tensor_tensor(xc, xc, spread(bo[:], 1, CHUNK), ALU.add).then_inc(biased, 1)

            pipeline(dve, CHUNKS, 2, [(0, norm)] + ([(0, out_bias), (1, queries), (1, values)] if first else []))

        @block.tensor
        def _(pe):
            ident = k.const[:, C_IDENT:C_IDENT + P]
            if first:
                pe.wait_ge(keep_col_ready, 1)
                nc.tensor.matmul(ps_k[0][:, 0:SEQ], keep_col[0:SEQ, 0:1].broadcast_to([SEQ, P]),
                                 ident[0:SEQ, 0:SEQ], start=True, stop=True).then_inc(keep_summed, 1)

            def transposes(it, par):
                c = 2 * it + par
                pe.wait_ge(normed, CHUNK * (c + 1))
                if reused(c, 2):
                    pe.wait_ge(xt_ready if first else q_ready, c - 1)
                for j in range(CHUNK):
                    last = nc.tensor.transpose(ps_t[par][:, j * P:(j + 1) * P], xn[par][:, j, :], ident)
                last.then_inc(transposed, 1)

            def products(it, par):
                c = 2 * it + par
                if not reused(c, 1):
                    pe.wait_ge(setup, 16 * 9)
                    pe.wait_ge(steps, 4)
                pe.wait_ge(ctx_in[par], 16 * (it + 1))
                if reused(c, 2):
                    pe.wait_ge(k_ready, c - 1)
                nc.tensor.matmul(ps_k[par][:], wk[:], ctxt[par][:], start=True, stop=True).then_inc(k_done, 1)
                if reused(c, 2):
                    pe.wait_ge(v_ready, c - 1)
                for j in range(CHUNK):
                    last = nc.tensor.matmul(ps_v[par][:, j * P:(j + 1) * P], ctxt[par][:, j * P:(j + 1) * P],
                                            wv[:], start=True, stop=True)
                last.then_inc(v_done, 1)
                pe.wait_ge(xt_ready, c + 1)
                if reused(c, 2):
                    pe.wait_ge(q_ready, c - 1)
                nc.tensor.matmul(ps_q[par][:], wq[:], xt[par][:], start=True, stop=True).then_inc(q_done, 1)

            pipeline(pe, CHUNKS, 2, [(0, transposes)] + ([(0, products)] if first else []))

        @block.scalar
        def _(act):
            def columns(it, par):
                c = 2 * it + par
                act.wait_ge(transposed, c + 1)
                if first:
                    if reused(c, 2):
                        act.wait_ge(q_done, c - 1)
                    nc.scalar.activation(xt[par][:], ps_t[par][:], ACT.Copy).then_inc(xt_ready, 1)
                else:
                    if reused(c, 2):
                        act.wait_ge(stored[par], 16 * it)
                    nc.scalar.activation(q_sb[par][:], ps_t[par][:], ACT.Copy, scale=DK ** -0.5).then_inc(q_ready, 1)

            def keys(it, par):
                c = 2 * it + par
                if not reused(c, 1):
                    act.wait_ge(setup, 16 * 9)
                act.wait_ge(k_done, c + 1)
                if reused(c, 2):
                    act.wait_ge(stored[par], 16 * outs * it)
                nc.scalar.activation(k_sb[par][:], ps_k[par][:], ACT.Identity, bias=bk[:, 0:1]).then_inc(k_ready, 1)

            pipeline(act, CHUNKS, 2, [(0, columns)] + ([(0, keys)] if first else []))


def attend(nc, k, layer):
    first = layer == 0
    HALF = P // 2
    LOAD = 4
    U = 2 * LOAD
    with ExitStack() as ctx:
        def sb(n, shape, dt=F32):
            return ctx.enter_context(nc.sbuf_tensor(f"at{layer}_{n}", shape, dt))

        def ps(n, shape):
            return ctx.enter_context(nc.psum_tensor(f"at{layer}_{n}", shape, F32))

        def sem(n):
            return ctx.enter_context(nc.semaphore(f"at{layer}_{n}"))

        q2 = [sb(f"q2{i}", [P, 2, 2, LOAD, P]) for i in range(2)]
        k2 = [sb(f"k2{i}", [P, 2, LOAD, SEQ]) for i in range(2)]
        v2 = [sb(f"v2{i}", [P, LOAD, 2, D]) for i in range(2)]
        keys = [sb(f"keys{i}", [P, 2 if first else 1, 4, 2, LOAD, SEQ]) for i in range(2)]
        vals = [sb(f"vals{i}", [P, LOAD, 2, 8, 2, DK + 1]) for i in range(2)]
        s_sb = [sb(f"s{i}", [P, HEADS, SEQ]) for i in range(4)]
        top = [sb(f"top{i}", [P, HEADS]) for i in range(2)]
        pt = [sb(f"pt{i}", [P, 8, P]) for i in range(2)]
        inv = [sb(f"inv{i}", [P, HEADS]) for i in range(2)]
        heads = [sb(f"heads{i}", [P, D]) for i in range(4)]
        ps_s = [ps(f"ps_s{i}", [P, 2, 512]) for i in range(2)]
        ps_p = ps("ps_p", [P, 8, P])
        ps_o = ps("ps_o", [P, 512])
        ps_w = ps("ps_w", [P, 512])
        sums = ps_o[:, 0:8 * 36].rearrange("p (u b r c) -> p u b r c", b=2, r=2, c=DK + 1)
        zeros = sb("zeros", [P, 8 * D])
        if first:
            wo = sb("wo", [P, D])
            ht = sb("ht", [P, P])
        sums_sb = [sb(f"sums{i}", [P, HEADS, DK + 1]) for i in range(4)]
        loaded = [sem(f"loaded{i}") for i in range(2)]
        setup, cleared = sem("setup"), sem("cleared")
        sp_ticks, pool_ticks, dve_ticks = sem("sp_ticks"), sem("pool_ticks"), sem("dve_ticks")
        marked, counted = sem("marked"), sem("counted")
        zeros_ready, filled = sem("zeros_ready"), sem("filled")
        keys_spread, vals_spread = sem("keys_spread"), sem("vals_spread")
        scored, masked, topped, shifted = sem("scored"), sem("masked"), sem("topped"), sem("shifted")
        exped, turned, turned_out, summed = sem("exped"), sem("turned"), sem("turned_out"), sem("summed")
        inverted, normalized, sums_out = sem("inverted"), sem("normalized"), sem("sums_out")
        heads_turned, ht_ready, projected, added = (
            sem("heads_turned"), sem("ht_ready"), sem("projected"), sem("added"))
        block = ctx.enter_context(nc.Block())

        DMAS = 8 + 8 + 2
        MARKS = 10 if first else 2
        SPREADS = 2 if first else 1

        @block.sync
        def _(sp):
            if first:
                sp.dma_start(wo[:], k.wo).then_inc(setup, 16)
            sp.wait_ge(marked, MARKS)
            qv = k.qt.rearrange("(G g f) (t b q) -> G b f g t q", G=2, g=2, b=2, q=SEQ)
            kv = (k.kt if first else k.ctxt_in).rearrange("(G g f) (t b q) -> G b f g t q", G=2, g=2, b=2, q=SEQ)
            vv = (k.v if first else k.ctx_in).rearrange("(t b q) d -> q t b d", b=2, q=SEQ)

            def load(it, par):
                s = 2 * it + par
                if reused(s, 2):
                    sp.wait_ge(scored, LOAD * (s - 1))
                    absorb(sp, sp_ticks)
                    sp.wait_ge(keys_spread, SPREADS * (s - 1))
                    absorb(sp, sp_ticks)
                    sp.wait_ge(vals_spread, 2 * (s - 1))
                    absorb(sp, sp_ticks)
                some = bass.ts(s, LOAD)
                for G in range(2):
                    for b in range(2):
                        rows = slice(HALF * G + 32 * b, HALF * G + 32 * b + 32)
                        for g in range(2):
                            sp.dma_start(k2[par][rows, g, :, :], kv[G, b, :, g, some, :]).then_inc(loaded[par], 16)
                for half in range(2):
                    sp.dma_start(v2[par][HALF * half:HALF * half + HALF, :, :, :],
                                 vv[:, some, :, :]).then_inc(loaded[par], 16)
                for G in range(2):
                    for b in range(2):
                        rows = slice(HALF * G + 32 * b, HALF * G + 32 * b + 32)
                        for g in range(2):
                            sp.dma_start(q2[par][rows, G, g, :, b * SEQ:(b + 1) * SEQ],
                                         qv[G, b, :, g, some, :]).then_inc(loaded[par], 16)

            pipeline(sp, TILES // LOAD, 2, [(0, load)])

        @block.gpsimd
        def _(pool):
            nc.gpsimd.memset(zeros[:], 0.0).then_inc(zeros_ready, 1)
            for i in range(2):
                nc.gpsimd.memset(vals[i][:], 0.0).then_inc(cleared, 1)
            pool.wait_ge(cleared, 2)
            for i in range(2):
                for r in range(2):
                    nc.gpsimd.memset(vals[i][HALF * r:HALF * r + HALF, :, :, :, r, DK:DK + 1],
                                     1.0).then_inc(cleared, 1)
            pool.wait_ge(cleared, 6)
            head_of = k.const[:, C_HEAD:C_HEAD + 4]

            def spread_keys(it, buf):
                s = 2 * it + buf
                pool.wait_ge(loaded[buf], 16 * DMAS * (it + 1))
                if reused(s, 2):
                    pool.wait_ge(scored, LOAD * (s - 1))
                    absorb(pool, pool_ticks)
                for G in range(SPREADS):
                    rows = slice(HALF * G, HALF * G + HALF) if first else slice(0, P)
                    if G:
                        pool.wait_ge(keys_spread, SPREADS * s + 1)
                        absorb(pool, pool_ticks)
                    nc.gpsimd.tensor_tensor(
                        keys[buf][rows, G, :, :, :, :].rearrange("p h g t k -> p h (g t k)"),
                        spread(k2[buf][rows, :, :, :].rearrange("p g t k -> p (g t k)"), 1, 4),
                        spread(head_of[rows, :], 2, 2 * LOAD * SEQ), ALU.mult).then_inc(keys_spread, 1)

            def spread_values(it, buf):
                s = 2 * it + buf
                if reused(s, 2):
                    pool.wait_ge(summed, LOAD * (s - 1))
                    absorb(pool, pool_ticks)
                if first:
                    pool.wait_ge(keys_spread, SPREADS * (s + 1))
                    absorb(pool, pool_ticks)
                for r in range(2):
                    nc.gpsimd.tensor_tensor(
                        vals[buf][:, :, :, :, r, 0:DK].rearrange("p t b u c -> p (t b) u c"),
                        v2[buf][:].rearrange("p t b (u r c) -> p (t b) u r c", r=2, c=DK)[:, :, :, r, :],
                        spread(spread(k.const[:, C_HALF + r:C_HALF + r + 1].broadcast_to([P, DK]), 1, 8),
                               1, 2 * LOAD),
                        ALU.mult).then_inc(vals_spread, 1)

            def spread_ahead(it, kk):
                if kk % LOAD == 0:
                    spread_keys(it, kk // LOAD)

            def spread_behind(it, kk):
                if kk % LOAD == 0:
                    spread_values(it, kk // LOAD)

            pipeline(pool, TILES, U, [(0, spread_ahead), (2, spread_behind)], peeled=1)

        @block.tensor
        def _(pe):
            ident = k.const[:, C_IDENT:C_IDENT + P]

            def scores(it, kk):
                t, par, buf, tt = U * it + kk, kk % 2, kk // LOAD, kk % LOAD
                if not reused(t, 1):
                    pe.wait_ge(marked, MARKS)
                if tt == 0:
                    pe.wait_ge(loaded[buf], 16 * DMAS * (it + 1))
                    pe.wait_ge(keys_spread, SPREADS * (2 * it + buf + 1))
                if reused(t, 2):
                    pe.wait_ge(shifted if first else masked, t - 1 if first else 2 * t - 2)
                for g in range(2):
                    for G in range(2):
                        last = nc.tensor.matmul(ps_s[par][:, G, 256 * g:256 * g + 256], q2[buf][:, G, g, tt, :],
                                                keys[buf][:, G if first else 0, :, g, tt, :],
                                                start=True, stop=True)
                last.then_inc(scored, 1)

            def turn(it, kk):
                t = U * it + kk
                pe.wait_ge(exped, t + 1)
                if reused(t, 1):
                    pe.wait_ge(turned_out, 2 * t)
                for u in range(8):
                    last = nc.tensor.transpose(
                        ps_p[:, u, :], s_sb[kk % 4][:, 2 * u:2 * u + 2, :].rearrange("p h k -> p (h k)"), ident)
                last.then_inc(turned, 1)

            def weigh(it, kk):
                t, par, buf, tt = U * it + kk, kk % 2, kk // LOAD, kk % LOAD
                pe.wait_ge(turned_out, 2 * t + 2)
                if tt == 0:
                    pe.wait_ge(vals_spread, 2 * (2 * it + buf + 1))
                if reused(t, 1):
                    pe.wait_ge(sums_out, 2 * t)
                for u in range(8):
                    last = nc.tensor.matmul(ps_o[:, 36 * u:36 * u + 36], pt[par][:, u, :],
                                            vals[buf][:, tt, :, u, :, :].rearrange("p b r c -> p b (r c)"),
                                            start=True, stop=True)
                last.then_inc(summed, 1)

            def turn_heads(it, kk):
                t = U * it + kk
                pe.wait_ge(normalized, t + 1)
                if reused(t, 1):
                    pe.wait_ge(added, t)
                nc.tensor.transpose(ps_w[:, 0:P], heads[kk % 4][:], ident).then_inc(heads_turned, 1)

            def project_heads(it, kk):
                t = U * it + kk
                if not reused(t, 1):
                    pe.wait_ge(setup, 16)
                pe.wait_ge(ht_ready, t + 1)
                nc.tensor.matmul(ps_w[:, P:2 * P], ht[:], wo[:], start=True, stop=True).then_inc(projected, 1)

            pipeline(pe, TILES, U, [(0, scores)] + ([(5, turn_heads)] if first else []) + [(2, turn), (3, weigh)]
                     + ([(5, project_heads)] if first else []), peeled=1)

        @block.scalar
        def _(act):
            act.wait_ge(zeros_ready, 1)
            fills = SLOTS[layer] // 8
            for i in range(fills):
                act.dma_start(k.xs[layer][8 * P * i:8 * P * (i + 1), :].rearrange("(p r) d -> p (r d)", p=P),
                              zeros[:]).then_inc(filled, 16)

            def exponent(it, kk):
                t, buf = U * it + kk, kk % 4
                act.wait_ge(shifted, t + 1)
                nc.scalar.activation(s_sb[buf][:], s_sb[buf][:], ACT.Exp).then_inc(exped, 1)

            def turn_out(it, kk):
                t, par = U * it + kk, kk % 2
                act.wait_ge(turned, t + 1)
                if reused(t, 2):
                    act.wait_ge(summed, t - 1)
                for h in range(2):
                    nc.scalar.activation(pt[par][:, 4 * h:4 * h + 4, :], ps_p[:, 4 * h:4 * h + 4, :],
                                         ACT.Copy).then_inc(turned_out, 1)

            def sums_away(it, kk):
                t, buf = U * it + kk, kk % 4
                act.wait_ge(summed, t + 1)
                if reused(t, 4):
                    act.wait_ge(normalized, t - 3)
                for b in range(2):
                    rows = slice(HALF * b, HALF * b + HALF)
                    nc.scalar.activation(sums_sb[buf][rows, :, :].rearrange("p (u r) c -> p u r c", r=2),
                                         sums[rows, :, b, :, :], ACT.Copy).then_inc(sums_out, 1)

            def heads_out(it, kk):
                t = U * it + kk
                act.wait_ge(heads_turned, t + 1)
                nc.scalar.activation(ht[:], ps_w[:, 0:P], ACT.Copy).then_inc(ht_ready, 1)

            pipeline(act, TILES, U, ([(5, heads_out)] if first else []) + [(4, sums_away), (2, turn_out), (0, exponent)],
                     peeled=1)
            act.wait_ge(filled, 16 * fills)

        @block.vector
        def _(dve):
            gate = k.gates[:, layer:layer + 1]

            def soften(it, kk):
                t, par, s = U * it + kk, kk % 2, s_sb[kk % 4]
                dve.wait_ge(scored, t + 1)
                if reused(t, 4):
                    dve.wait_ge(turned, t - 3)
                if first:
                    src = ps_s[par][:].rearrange("p G (h k) -> p (G h) k", k=SEQ)
                else:
                    bias = k.bias1[:, bass.ds(t, 1), :].rearrange("p a k -> p (a k)")
                    for G in range(2):
                        nc.vector.tensor_tensor(s[:, 8 * G:8 * G + 8, :],
                                                ps_s[par][:, G, :].rearrange("p (h k) -> p h k", k=SEQ),
                                                spread(bias, 1, 8), ALU.add).then_inc(masked, 1)
                    dve.wait_ge(masked, 2 * t + 2)
                    src = s[:]
                nc.vector.tensor_reduce(top[par][:], src, AX.X, ALU.max).then_inc(topped, 1)
                dve.wait_ge(topped, t + 1)
                nc.vector.tensor_tensor(s[:], src, spread(top[par][:], 2, SEQ), ALU.subtract).then_inc(shifted, 1)

            def divide(it, kk):
                t, par, buf = U * it + kk, kk % 2, kk % 4
                dve.wait_ge(sums_out, 2 * t + 2)
                nc.vector.reciprocal(inv[par][:], sums_sb[buf][:, :, DK]).then_inc(inverted, 1)
                if reused(t, 4):
                    dve.wait_ge(added, t - 3)
                dve.wait_ge(inverted, t + 1)
                nc.vector.tensor_tensor(heads[buf][:].rearrange("p (h c) -> p h c", c=DK), sums_sb[buf][:, :, 0:DK],
                                        spread(inv[par][:], 2, DK), ALU.mult).then_inc(normalized, 1)

            def add(it, kk):
                t = U * it + kk
                if first:
                    dve.wait_ge(projected, t + 1)
                    src = ps_w[:, P:2 * P]
                else:
                    dve.wait_ge(normalized, t + 1)
                    src = heads[kk % 4][:]
                xt = k.x[:, bass.ds(t, 1), :].rearrange("p a d -> p (a d)")
                nc.vector.scalar_tensor_tensor(xt, src, gate, xt, ALU.mult, ALU.add).then_inc(added, 1)

            def count(it, kk):
                t = U * it + kk
                dve.wait_ge(added, t + 1)
                absorb(dve, dve_ticks)
                gather_stats(nc, k, t).then_inc(counted, 1)

            for i in range(2):
                nc.vector.memset(q2[i][:], 0.0).then_inc(marked, 1)
            if first:
                ident = k.const[:, C_IDENT:C_IDENT + P]
                dve.wait_ge(marked, 2)
                for i in range(2):
                    for G in range(2):
                        rows = slice(HALF * (1 - G), HALF * (1 - G) + HALF)
                        nc.vector.tensor_copy(q2[i][rows, G, :, :, :].rearrange("p g t (b q) -> p (g t b) q", b=2),
                                              spread(ident[rows, rows], 1, 4 * LOAD)).then_inc(marked, 1)
                        nc.vector.tensor_copy(keys[i][rows, G, :, :, :, :].rearrange("p h g t k -> p (h g t) k"),
                                              spread(k.bias0[rows, :], 1, 8 * LOAD)).then_inc(marked, 1)

            if first:
                pipeline(dve, TILES, U, [(6, add), (0, soften), (4, divide), (7, count)], peeled=1)
            else:
                pipeline(dve, TILES, U, [(5, add), (0, soften), (4, divide), (6, count)], peeled=1)
            dve.wait_ge(counted, TILES)


def route(nc, k, layer):
    picks = layer + 1
    slots = SLOTS[layer]
    with ExitStack() as ctx:
        def sb(n, shape, dt=F32):
            return ctx.enter_context(nc.sbuf_tensor(f"ro{layer}_{n}", shape, dt))

        def ps(n):
            return ctx.enter_context(nc.psum_tensor(f"ro{layer}_{n}", [P, 512], F32))

        def sem(n):
            return ctx.enter_context(nc.semaphore(f"ro{layer}_{n}"))

        xn = [sb(f"xn{i}", [P, CHUNK, D]) for i in range(2)]
        xt = [sb(f"xt{i}", [P, CHUNK * P]) for i in range(2)]
        router = sb("router", [P, E])
        logits = sb("logits", [P, TILES, E])
        ps_t, ps_l = [ps(f"ps_t{i}") for i in range(2)], [ps(f"ps_l{i}") for i in range(2)]
        ps_c = [ps(f"ps_c{i}") for i in range(4)]
        work, prob = sb("work", [P, TILES, E]), sb("prob", [P, TILES, E])
        hot = [sb(f"hot{i}", [P, TILES, E]) for i in range(picks)]
        before = [sb(f"before{i}", [P, TILES, E]) for i in range(picks)]
        total = sb("total", [P, picks, E])
        m = [sb(f"m{i}", [P, TILES]) for i in range(picks)]
        col, inv_sum = sb("col", [P, TILES]), sb("inv_sum", [P, TILES])
        tiles_i, n_tiles = sb("tiles_i", [P, E], I32), sb("n_tiles", [P, E])
        ends, starts = sb("ends", [P, E]), sb("starts", [P, E])
        load_e = sb("load_e", [P, E])
        ge_end, row = sb("ge_end", [P, slots, E]), sb("row", [P, slots])

        setup, normed, transposed, xt_ready = sem("setup"), sem("normed"), sem("transposed"), sem("xt_ready")
        copied, logits_done, logits_out = sem("copied"), sem("logits_done"), sem("logits_out")
        steps, hot_ready, counted = sem("steps"), sem("hot_ready"), sem("counted")
        diff_ready, prob_ready = sem("diff_ready"), sem("prob_ready")
        block = ctx.enter_context(nc.Block())

        @block.sync
        def _(sp):
            sp.dma_start(router[:], k.routers[layer]).then_inc(setup, 16)

        @block.tensor
        def _(pe):
            ident = k.const[:, C_IDENT:C_IDENT + P]

            def transposes(it, par):
                c = 2 * it + par
                pe.wait_ge(normed, CHUNK * (c + 1))
                if reused(c, 2):
                    pe.wait_ge(xt_ready, c - 1)
                for j in range(CHUNK):
                    last = nc.tensor.transpose(ps_t[par][:, j * P:(j + 1) * P], xn[par][:, j, :], ident)
                last.then_inc(transposed, 1)

            def score(it, par):
                c = 2 * it + par
                if not reused(c, 1):
                    pe.wait_ge(setup, 16)
                pe.wait_ge(xt_ready, c + 1)
                if reused(c, 2):
                    pe.wait_ge(logits_out, c - 1)
                for j in range(CHUNK):
                    last = nc.tensor.matmul(ps_l[par][:, j * E:(j + 1) * E], xt[par][:, j * P:(j + 1) * P],
                                            router[:], start=True, stop=True)
                last.then_inc(logits_done, 1)

            pipeline(pe, CHUNKS, 2, [(0, transposes), (1, score)])
            for i in range(picks):
                pe.wait_ge(hot_ready, i + 1)
                chosen = hot[i][:].rearrange("p t e -> p (t e)")
                nc.tensor.matmul(ps_c[2 * i][:], k.const[:, C_TRI:C_TRI + P], chosen, start=True, stop=True)
                nc.tensor.matmul(ps_c[2 * i + 1][:], k.const[:, C_ONES:C_ONES + P], chosen,
                                 start=True, stop=True).then_inc(counted, 1)

        @block.scalar
        def _(act):
            def columns(it, par):
                c = 2 * it + par
                act.wait_ge(transposed, c + 1)
                if reused(c, 2):
                    act.wait_ge(logits_done, c - 1)
                    if not layer:
                        act.wait_ge(copied, c - 1)
                nc.scalar.activation(xt[par][:], ps_t[par][:], ACT.Copy).then_inc(xt_ready, 1)

            pipeline(act, CHUNKS, 2, [(0, columns)])
            act.wait_ge(diff_ready, 1)
            nc.scalar.activation(prob[:], work[:], ACT.Exp).then_inc(prob_ready, 1)

        @block.vector
        def _(dve):
            def norm(it, par):
                c = 2 * it + par
                if reused(c, 2):
                    dve.wait_ge(transposed, c - 1)
                for j in range(CHUNK):
                    normalize(nc, k, xn[par][:, j, :], c * CHUNK + j).then_inc(normed, 1)

            def keep_columns(it, par):
                c = 2 * it + par
                dve.wait_ge(xt_ready, c + 1)
                nc.vector.tensor_scalar(k.xnt[:, bass.ts(c, 512)], xt[par][:], 1.0, None,
                                        ALU.mult).then_inc(copied, 1)

            def keep_logits(it, par):
                c = 2 * it + par
                dve.wait_ge(logits_done, c + 1)
                nc.vector.tensor_scalar(logits[:, bass.ts(c, CHUNK), :],
                                        ps_l[par][:, 0:CHUNK * E].rearrange("p (t e) -> p t e", e=E),
                                        1.0, None, ALU.mult).then_inc(logits_out, 1)

            pipeline(dve, CHUNKS, 2, [(0, norm)] + ([] if layer else [(1, keep_columns)]) + [(2, keep_logits)])
            dve.wait_ge(logits_out, CHUNKS)
            do = Chain(dve, steps)
            first_of = spread(k.const[:, C_FIRST:C_FIRST + E], 1, TILES)

            def pick(i):
                do(nc.vector.tensor_reduce(m[i][:], logits[:], AX.X, ALU.max))
                do(nc.vector.tensor_tensor(work[:], logits[:], spread(m[i][:], 2, E), ALU.is_equal))
                do(nc.vector.tensor_tensor(work[:], work[:], first_of, ALU.mult))
                do(nc.vector.tensor_reduce(col[:], work[:], AX.X, ALU.max))
                nc.vector.tensor_tensor(hot[i][:], work[:], spread(col[:], 2, E), ALU.is_equal).then_inc(hot_ready, 1)
                dve.wait_ge(hot_ready, i + 1)

            pick(0)
            do(nc.vector.tensor_tensor(prob[:], logits[:], spread(m[0][:], 2, E), ALU.subtract))
            if picks == 2:
                do(nc.vector.scalar_tensor_tensor(logits[:], hot[0][:], -3.0e38, logits[:], ALU.mult, ALU.add))
                pick(1)
            nc.vector.tensor_copy(work[:], prob[:]).then_inc(diff_ready, 1)
            dve.wait_ge(prob_ready, 1)
            do(nc.vector.tensor_reduce(inv_sum[:], prob[:], AX.X, ALU.add))
            do(nc.vector.reciprocal(inv_sum[:], inv_sum[:]))

            for i in range(picks):
                dve.wait_ge(counted, i + 1)
                per_tile = ps_c[2 * i + 1][:].rearrange("p (t e) -> p t e", e=E)
                do(nc.vector.tensor_copy(work[:], per_tile))
                for e in range(E):
                    do(nc.vector.tensor_tensor_scan(before[i][:, :, e], k.const[:, C_ONES:C_ONES + TILES],
                                                    work[:, :, e], 0.0, ALU.mult, ALU.add))
                do(nc.vector.tensor_copy(total[:, i, :], before[i][:, TILES - 1, :]))
                do(nc.vector.tensor_tensor(before[i][:], before[i][:], work[:], ALU.subtract))
                do(nc.vector.tensor_tensor(before[i][:], before[i][:],
                                           ps_c[2 * i][:].rearrange("p (t e) -> p t e", e=E), ALU.add))

            def chosen(out, i, values):
                do(nc.vector.tensor_tensor(work[:], values, hot[i][:], ALU.mult))
                do(nc.vector.tensor_reduce(out, work[:], AX.X, ALU.add))

            if picks == 1:
                do(nc.vector.tensor_scalar(k.weight[0][:], inv_sum[:], 2.0, k.gates[:, 2:3], ALU.mult, ALU.mult))
                do(nc.vector.tensor_copy(load_e[:], total[:, 0, :]))
            else:
                gate1, gate2, denom = m[0], m[1], col
                do(nc.vector.tensor_copy(gate1[:], inv_sum[:]))
                chosen(gate2[:], 1, prob[:])
                do(nc.vector.tensor_tensor(gate2[:], gate2[:], inv_sum[:], ALU.mult))
                do(nc.vector.tensor_tensor(denom[:], gate1[:], gate2[:], ALU.add))
                do(nc.vector.tensor_scalar(denom[:], denom[:], 1e-9, None, ALU.add))
                do(nc.vector.reciprocal(denom[:], denom[:]))
                for i, gate in enumerate((gate1, gate2)):
                    do(nc.vector.tensor_tensor(gate[:], gate[:], denom[:], ALU.mult))
                    do(nc.vector.tensor_scalar(k.weight[i][:], gate[:], k.gates[:, 3:4], None, ALU.mult))
                chosen(gate1[:], 0, before[0][:])
                do(nc.vector.tensor_tensor(prob[:], before[1][:], spread(total[:, 0, :], 1, TILES), ALU.add))
                chosen(gate2[:], 1, prob[:])
                for i, pos in enumerate((gate1, gate2)):
                    do(nc.vector.tensor_scalar(pos[:], pos[:], float(CAP), None, ALU.is_lt))
                    do(nc.vector.tensor_tensor(k.weight[i][:], k.weight[i][:], pos[:], ALU.mult))
                do(nc.vector.tensor_tensor(load_e[:], total[:, 0, :], total[:, 1, :], ALU.add))
                do(nc.vector.tensor_tensor(before[0][:], before[0][:], before[1][:], ALU.add))

            do(nc.vector.tensor_scalar(n_tiles[:], load_e[:], P - 1.0, None, ALU.add))
            do(nc.vector.tensor_copy(tiles_i[:], n_tiles[:]))
            do(nc.vector.tensor_scalar(tiles_i[:], tiles_i[:], 7, None, ALU.arith_shift_right))
            do(nc.vector.tensor_copy(n_tiles[:], tiles_i[:]))
            do(nc.vector.tensor_scalar(n_tiles[:], n_tiles[:], float(P), None, ALU.mult))
            do(nc.vector.tensor_tensor_scan(ends[:], k.const[:, C_ONES:C_ONES + E], n_tiles[:], 0.0,
                                            ALU.mult, ALU.add))
            do(nc.vector.tensor_tensor(starts[:], ends[:], n_tiles[:], ALU.subtract))
            do(nc.vector.tensor_tensor(before[0][:], before[0][:], spread(starts[:], 1, TILES), ALU.add))
            for i in range(picks):
                chosen(col[:], i, before[0][:])
                do(nc.vector.tensor_copy(k.dest[i][:], col[:]))
            do(nc.vector.tensor_tensor(ge_end[:], spread(k.const[:, C_SLOT:C_SLOT + slots], 2, E),
                                       spread(ends[:], 1, slots), ALU.is_ge))
            do(nc.vector.tensor_reduce(row[:], ge_end[:], AX.X, ALU.add))
            do(nc.vector.tensor_scalar(row[:], row[:], E - 1.0, None, ALU.min))
            do(nc.vector.tensor_copy(k.slot_expert[:, 0:slots], row[:]))


def dispatch(nc, k, layer):
    picks = layer + 1
    shared = layer == 0
    with ExitStack() as ctx:
        def sb(n, shape, dt=F32):
            return ctx.enter_context(nc.sbuf_tensor(f"di{layer}_{n}", shape, dt))

        def ps(n):
            return ctx.enter_context(nc.psum_tensor(f"di{layer}_{n}", [P, 512], F32))

        def sem(n):
            return ctx.enter_context(nc.semaphore(f"di{layer}_{n}"))

        U = 8
        xn = [sb(f"xn{i}", [P, D]) for i in range(2)]
        to = [[sb(f"to{i}_{j}", [P, 1], I32) for i in range(2)] for j in range(picks)]
        if shared:
            wu, wg, wd = sb("wu", [P, F]), sb("wg", [P, F]), sb("wd", [P, FB, D])
            act_g = [sb(f"act_g{i}", [P, 512]) for i in range(2)]
            hid = [sb(f"hid{i}", [P, 512]) for i in range(8)]
            ps_u, ps_g, ps_y = ([ps(f"ps_{n}{i}") for i in range(2)] for n in "ugy")
        setup, ticks = sem("setup"), sem("ticks")
        normed, indexed = sem("normed"), sem("indexed")
        scattered = [sem(f"scattered{i}") for i in range(2)]
        projected, gated, multiplied, summed, added = (
            sem("projected"), sem("gated"), sem("multiplied"), sem("summed"), sem("added"))
        block = ctx.enter_context(nc.Block())

        @block.sync
        def _(sp):
            if shared:
                sp.dma_start(wu[:], k.shared_up).then_inc(setup, 16)
                sp.dma_start(wg[:], k.shared_gate).then_inc(setup, 16)
                sp.dma_start(wd[:], k.shared_down.rearrange("(c p) d -> p c d", p=P)).then_inc(setup, 16)

        @block.gpsimd
        def _(pool):
            def scatter(it, kk):
                t, par = U * it + kk, kk % 2
                n = U // 2 * it + kk // 2
                if reused(t, 2):
                    pool.wait_ge(scattered[par], 16 * picks * n)
                for i in range(picks):
                    nc.gpsimd.tensor_copy(to[i][par][:], k.dest[i][:, bass.ds(t, 1)]).then_inc(indexed, 1)
                pool.wait_ge(indexed, picks * (t + 1))
                pool.wait_ge(normed, t + 1)
                absorb(pool, ticks)
                for i in range(picks):
                    nc.gpsimd.indirect_dma_start(k.xs[layer], bass.IndirectOffsetOnAxis(ap=to[i][par][:, 0:1], axis=0),
                                                 xn[par][:], None).then_inc(scattered[par], 16)

            pipeline(pool, TILES, U, [(0, scatter)])
            for par in range(2):
                pool.wait_ge(scattered[par], 16 * picks * TILES // 2)

        @block.vector
        def _(dve):
            def norm(it, kk):
                t, par = U * it + kk, kk % 2
                if reused(t, 2):
                    dve.wait_ge(scattered[par], 16 * picks * (U // 2 * it + kk // 2))
                normalize(nc, k, xn[par][:], t).then_inc(normed, 1)

            def multiply(it, kk):
                w, par = U * it + kk, kk % 2
                dve.wait_ge(gated, w + 1)
                if reused(w, 8):
                    dve.wait_ge(summed, 2 * it + kk // 4 - 1)
                nc.vector.tensor_tensor(hid[kk][:], act_g[par][:], ps_u[par][:], ALU.mult).then_inc(multiplied, 1)

            def add(it, kk):
                if kk % CHUNK != CHUNK - 1:
                    return
                c = 2 * it + kk // CHUNK
                dve.wait_ge(summed, c + 1)
                dve.wait_ge(normed, CHUNK * (c + 1))
                xc = k.x[:, bass.ts(c, CHUNK), :]
                nc.vector.scalar_tensor_tensor(xc, ps_y[kk // CHUNK][:].rearrange("p (t d) -> p t d", d=D),
                                               k.gates[:, 2:3], xc, ALU.mult, ALU.add).then_inc(added, 1)

            pipeline(dve, TILES, U, [(0, norm)] + ([(0, multiply), (4, add)] if shared else []))

        if shared:
            @block.tensor
            def _(pe):
                def project_up(it, kk):
                    w, par, f = U * it + kk, kk % 2, kk % FB
                    if not reused(w, 1):
                        pe.wait_ge(setup, 16 * 3)
                    if reused(w, 2):
                        pe.wait_ge(multiplied, w - 1)
                    cols = k.xnt[:, bass.ts(2 * it + kk // CHUNK, 512)]
                    nc.tensor.matmul(ps_g[par][:], wg[:, f * P:(f + 1) * P], cols, start=True, stop=True)
                    nc.tensor.matmul(ps_u[par][:], wu[:, f * P:(f + 1) * P], cols,
                                     start=True, stop=True).then_inc(projected, 1)

                def project_down(it, kk):
                    if kk % CHUNK != CHUNK - 1:
                        return
                    c, par = 2 * it + kk // CHUNK, kk // CHUNK
                    pe.wait_ge(multiplied, CHUNK * (c + 1))
                    if reused(c, 2):
                        pe.wait_ge(added, c - 1)
                    for j in range(CHUNK):
                        for f in range(FB):
                            last = nc.tensor.matmul(ps_y[par][:, j * P:(j + 1) * P],
                                                    hid[4 * par + f][:, j * P:(j + 1) * P], wd[:, f, :],
                                                    start=f == 0, stop=f == FB - 1)
                    last.then_inc(summed, 1)

                pipeline(pe, TILES, U, [(0, project_up), (2, project_down)])

            @block.scalar
            def _(act):
                def gate(it, kk):
                    w, par = U * it + kk, kk % 2
                    act.wait_ge(projected, w + 1)
                    if reused(w, 2):
                        act.wait_ge(multiplied, w - 1)
                    nc.scalar.activation(act_g[par][:], ps_g[par][:], ACT.Silu).then_inc(gated, 1)

                pipeline(act, TILES, U, [(0, gate)])


def experts(nc, k, layer):
    slots = SLOTS[layer]
    swiglu = layer == 0
    with ExitStack() as ctx:
        def sb(n, shape, dt=F32):
            return ctx.enter_context(nc.sbuf_tensor(f"ex{layer}_{n}", shape, dt))

        def ps(n):
            return ctx.enter_context(nc.psum_tensor(f"ex{layer}_{n}", [P, 512], F32))

        def sem(n):
            return ctx.enter_context(nc.semaphore(f"ex{layer}_{n}"))

        U = 4
        w_in = sb("w_in", [P, E * F])
        w_out = sb("w_out", [P, E * FB * D])
        if swiglu:
            w_gate = sb("w_gate", [P, E * F])
            act_g = [sb(f"act_g{i}", [P, F]) for i in range(2)]
        else:
            b1, b2 = sb("b1", [P, E * F]), sb("b2", [P, E * D])
        xs = [sb(f"xs{i}", [P, D]) for i in range(4)]
        xt = [sb(f"xt{i}", [P, P]) for i in range(2)]
        hid = [sb(f"hid{i}", [P, F]) for i in range(2)]
        ht = [sb(f"ht{i}", [P, FB, P]) for i in range(2)]
        y = [sb(f"y{i}", [P, D]) for i in range(2)]
        ps_x, ps_y = ps("ps_x"), ps("ps_y")
        ps_u, ps_h = [ps(f"ps_u{i}") for i in range(2)], [ps(f"ps_h{i}") for i in range(2)]
        ps_g = [ps(f"ps_g{i}") for i in range(2)] if swiglu else None
        setup, cleared = sem("setup"), sem("cleared")
        rows_in = [sem(f"rows_in{i}") for i in range(4)]
        x_turned, xt_ready, projected, gated = sem("x_turned"), sem("xt_ready"), sem("projected"), sem("gated")
        hid_ready, h_turned, ht_ready, summed, y_ready = (
            sem("hid_ready"), sem("h_turned"), sem("ht_ready"), sem("summed"), sem("y_ready"))
        stored = [sem(f"stored{i}") for i in range(2)]
        given = E - 1 if swiglu else E
        loads = 3 if swiglu else 4
        block = ctx.enter_context(nc.Block())

        def expert_of(eng, s):
            return eng.value_load(k.slot_expert[0:1, bass.ds(s, 1)], min_val=0, max_val=E - 1)

        @block.sync
        def _(sp):
            w1, wd = (k.up, k.down) if swiglu else (k.w1, k.w2)
            sp.dma_start(w_in[:, 0:given * F].rearrange("p (e f) -> p e f", e=given),
                         w1.rearrange("e p f -> p e f")).then_inc(setup, 16)
            if swiglu:
                sp.dma_start(w_gate[:, 0:given * F].rearrange("p (e f) -> p e f", e=given),
                             k.gate.rearrange("e p f -> p e f")).then_inc(setup, 16)
            else:
                sp.dma_start(b1[:], k.b1.rearrange("e f -> (e f)").partition_broadcast(P)).then_inc(setup, 16)
                sp.dma_start(b2[:], k.b2.rearrange("e d -> (e d)").partition_broadcast(P)).then_inc(setup, 16)
            sp.dma_start(w_out[:, 0:given * FB * D].rearrange("p (e c d) -> p e c d", e=given, c=FB),
                         wd.rearrange("e (c p) d -> p e c d", p=P)).then_inc(setup, 16)

            def load(it, kk):
                s = U * it + kk
                if reused(s, 4):
                    sp.wait_ge(x_turned, s - 3)
                sp.dma_start(xs[kk][:], k.xs[layer][bass.ts(s, P), :]).then_inc(rows_in[kk], 16)

            pipeline(sp, slots, U, [(0, load)])

        @block.gpsimd
        def _(pool):
            if swiglu:
                nc.gpsimd.memset(w_in[:, given * F:], 0.0).then_inc(cleared, 1)
                nc.gpsimd.memset(w_gate[:, given * F:], 0.0).then_inc(cleared, 1)
                nc.gpsimd.memset(w_out[:, given * FB * D:], 0.0).then_inc(cleared, 1)

            def store(it, kk):
                s, par = U * it + kk, kk % 2
                pool.wait_ge(y_ready, s + 1)
                pool.dma_start(k.ys[layer][bass.ts(s, P), :], y[par][:]).then_inc(stored[par], 16)

            pipeline(pool, slots, U, [(0, store)])
            for par in range(2):
                pool.wait_ge(stored[par], 16 * slots // 2)

        @block.tensor
        def _(pe):
            ident = k.const[:, C_IDENT:C_IDENT + P]
            pe.wait_ge(setup, 16 * loads)
            if swiglu:
                pe.wait_ge(cleared, 3)

            def turn_x(it, kk):
                s, par = U * it + kk, kk % 2
                pe.wait_ge(rows_in[kk], 16 * (it + 1))
                if reused(s, 1):
                    pe.wait_ge(xt_ready, s)
                nc.tensor.transpose(ps_x[:, 0:P], xs[kk][:], ident).then_inc(x_turned, 1)

            def project_in(it, kk):
                s, par = U * it + kk, kk % 2
                e = expert_of(pe, s)
                pe.wait_ge(xt_ready, s + 1)
                if reused(s, 2):
                    pe.wait_ge(hid_ready, s - 1)
                if swiglu:
                    nc.tensor.matmul(ps_g[par][:], xt[par][:], w_gate[:, bass.ts(e, F)], start=True, stop=True)
                nc.tensor.matmul(ps_u[par][:], xt[par][:], w_in[:, bass.ts(e, F)],
                                 start=True, stop=True).then_inc(projected, 1)

            def turn_h(it, kk):
                s, par = U * it + kk, kk % 2
                pe.wait_ge(hid_ready, s + 1)
                if reused(s, 2):
                    pe.wait_ge(ht_ready, s - 1)
                for c in range(FB):
                    last = nc.tensor.transpose(ps_h[par][:, c * P:(c + 1) * P], hid[par][:, c * P:(c + 1) * P], ident)
                last.then_inc(h_turned, 1)

            def project_out(it, kk):
                s, par = U * it + kk, kk % 2
                e = expert_of(pe, s)
                pe.wait_ge(ht_ready, s + 1)
                if reused(s, 1):
                    pe.wait_ge(y_ready, s)
                for c in range(FB):
                    last = nc.tensor.matmul(ps_y[:, 0:D], ht[par][:, c, :],
                                            w_out[:, bass.ds(e * (FB * D) + c * D, D)],
                                            start=c == 0, stop=c == FB - 1)
                last.then_inc(summed, 1)

            pipeline(pe, slots, U, [(0, turn_x), (1, project_in), (2, turn_h), (3, project_out)])

        @block.scalar
        def _(act):
            def x_out(it, kk):
                s, par = U * it + kk, kk % 2
                act.wait_ge(x_turned, s + 1)
                if reused(s, 2):
                    act.wait_ge(projected, s - 1)
                nc.scalar.activation(xt[par][:], ps_x[:, 0:P], ACT.Copy).then_inc(xt_ready, 1)

            def gate(it, kk):
                s, par = U * it + kk, kk % 2
                act.wait_ge(projected, s + 1)
                if reused(s, 2):
                    act.wait_ge(hid_ready, s - 1)
                nc.scalar.activation(act_g[par][:], ps_g[par][:], ACT.Silu).then_inc(gated, 1)

            def h_out(it, kk):
                s, par = U * it + kk, kk % 2
                act.wait_ge(h_turned, s + 1)
                if reused(s, 2):
                    act.wait_ge(summed, s - 1)
                nc.scalar.activation(ht[par][:].rearrange("p c t -> p (c t)"), ps_h[par][:],
                                     ACT.Copy if swiglu else ACT.Gelu).then_inc(ht_ready, 1)

            pipeline(act, slots, U, [(0, x_out)] + ([(1, gate)] if swiglu else []) + [(2, h_out)])

        @block.vector
        def _(dve):
            if not swiglu:
                dve.wait_ge(setup, 16 * loads)

            def hidden(it, kk):
                s, par = U * it + kk, kk % 2
                if swiglu:
                    dve.wait_ge(gated, s + 1)
                else:
                    e = expert_of(dve, s)
                    dve.wait_ge(projected, s + 1)
                if reused(s, 2):
                    dve.wait_ge(h_turned, s - 1)
                other = act_g[par][:] if swiglu else b1[:, bass.ts(e, F)]
                nc.vector.tensor_tensor(hid[par][:], ps_u[par][:], other,
                                        ALU.mult if swiglu else ALU.add).then_inc(hid_ready, 1)

            def output(it, kk):
                s, par = U * it + kk, kk % 2
                if not swiglu:
                    e = expert_of(dve, s)
                dve.wait_ge(summed, s + 1)
                if reused(s, 2):
                    dve.wait_ge(stored[par], 16 * (2 * it + kk // 2))
                if swiglu:
                    nc.vector.tensor_copy(y[par][:], ps_y[:, 0:D]).then_inc(y_ready, 1)
                else:
                    nc.vector.tensor_tensor(y[par][:], ps_y[:, 0:D], b2[:, bass.ts(e, D)],
                                            ALU.add).then_inc(y_ready, 1)

            pipeline(dve, slots, U, [(1, hidden), (3, output)])


def combine(nc, k, layer):
    picks = layer + 1
    with ExitStack() as ctx:
        def sem(n):
            return ctx.enter_context(nc.semaphore(f"co{layer}_{n}"))

        U = 4
        rows = [[ctx.enter_context(nc.sbuf_tensor(f"co{layer}_rows{i}_{j}", [P, D], F32)) for i in range(U)]
                for j in range(picks)]
        at = [[ctx.enter_context(nc.sbuf_tensor(f"co{layer}_at{i}_{j}", [P, 1], I32)) for i in range(U)]
              for j in range(picks)]
        indexed, added, stored, ticks = sem("indexed"), sem("added"), sem("stored"), sem("ticks")
        counted, dve_ticks = sem("counted"), sem("dve_ticks")
        gathered = [sem(f"gathered{i}") for i in range(U)]
        block = ctx.enter_context(nc.Block())

        @block.gpsimd
        def _(pool):
            def gather(it, kk):
                t = U * it + kk
                if reused(t, U):
                    pool.wait_ge(added, picks * (t - U + 1))
                for i in range(picks):
                    nc.gpsimd.tensor_copy(at[i][kk][:], k.dest[i][:, bass.ds(t, 1)]).then_inc(indexed, 1)
                pool.wait_ge(indexed, picks * (t + 1))
                absorb(pool, ticks)
                for i in range(picks):
                    nc.gpsimd.indirect_dma_start(rows[i][kk][:], None, k.ys[layer],
                                                 bass.IndirectOffsetOnAxis(ap=at[i][kk][:, 0:1], axis=0)
                                                 ).then_inc(gathered[kk], 16)

            pipeline(pool, TILES, U, [(0, gather)])

        @block.vector
        def _(dve):
            def add(it, kk):
                t = U * it + kk
                xt = k.x[:, bass.ds(t, 1), :].rearrange("p a d -> p (a d)")
                dve.wait_ge(gathered[kk], 16 * picks * (it + 1))
                for i in range(picks):
                    if i:
                        dve.wait_ge(added, picks * t + i)
                    nc.vector.scalar_tensor_tensor(xt, rows[i][kk][:], k.weight[i][:, bass.ds(t, 1)], xt,
                                                   ALU.mult, ALU.add).then_inc(added, 1)
                if not layer:
                    dve.wait_ge(added, picks * (t + 1))
                    absorb(dve, dve_ticks)
                    gather_stats(nc, k, t).then_inc(counted, 1)

            pipeline(dve, TILES, U, [(0, add)])
            if not layer:
                dve.wait_ge(counted, TILES)

        if layer:
            @block.sync
            def _(sp):
                ov = k.out.rearrange("(t p) d -> p t d", p=P)

                def store(it, par):
                    c = 2 * it + par
                    sp.wait_ge(added, picks * CHUNK * (c + 1))
                    sp.dma_start(ov[:, bass.ts(c, CHUNK), :], k.x[:, bass.ts(c, CHUNK), :]).then_inc(stored, 16)

                pipeline(sp, CHUNKS, 2, [(0, store)])
                sp.wait_ge(stored, 16 * CHUNKS)


def clear_semaphores(nc, numbers):
    with nc.Block() as block:
        @block.gpsimd
        def _(pool):
            pool.sem_clear(numbers)


class Tensors:
    pass


def build(nc, tensors):
    k = tensors
    k.qt = nc.dram_tensor("qt", (D, TOKENS), F32).ap()
    k.kt = nc.dram_tensor("kt", (D, TOKENS), F32).ap()
    k.v = nc.dram_tensor("v", (TOKENS, D), F32).ap()
    k.xs = [nc.dram_tensor(f"slot_x{i}", (SLOTS[i] * P, D), F32).ap() for i in range(2)]
    k.ys = [nc.dram_tensor(f"slot_y{i}", (SLOTS[i] * P, D), F32).ap() for i in range(2)]
    with ExitStack() as ctx:
        def sb(n, shape, dt=F32):
            return ctx.enter_context(nc.sbuf_tensor(n, shape, dt))

        k.x = sb("x", [P, TILES, D])
        k.const = sb("const", [P, C_ALL])
        k.gates = sb("gates", [P, 4])
        k.stats = sb("stats", [P, TILES, 6])
        k.mean, k.rstd = sb("mean", [P, TILES]), sb("rstd", [P, TILES])
        k.weight = [sb(f"weight{i}", [P, TILES]) for i in range(2)]
        k.dest = [sb(f"dest{i}", [P, TILES], I32) for i in range(2)]
        k.slot_expert = sb("slot_expert", [P, MAX_SLOTS], I32)
        numbers = range(min(nc.free_semaphores), max(nc.free_semaphores) + 1)
        load_inputs(nc, k)
        for layer in range(2):
            if layer:
                clear_semaphores(nc, numbers)
            with ExitStack() as own:
                if layer == 0:
                    k.mask0 = own.enter_context(nc.sbuf_tensor("mask0", [P, SEQ], I32))
                    k.bias0 = own.enter_context(nc.sbuf_tensor("bias0", [P, SEQ], F32))
                else:
                    k.mask1 = own.enter_context(nc.sbuf_tensor("mask1", [P, TILES, SEQ], I32))
                    k.bias1 = own.enter_context(nc.sbuf_tensor("bias1", [P, TILES, SEQ], F32))
                layer_stats(nc, k, f"lnq{layer}")
                project(nc, k, layer)
                attend(nc, k, layer)
            with ExitStack() as own:
                layer_stats(nc, k, f"lnf{layer}")
                if layer == 0:
                    k.xnt = own.enter_context(nc.sbuf_tensor("xnt", [P, TOKENS], F32))
                route(nc, k, layer)
                dispatch(nc, k, layer)
            experts(nc, k, layer)
            combine(nc, k, layer)


def kernel(**inputs):
    import concourse.bacc as bacc
    from concourse.bass_utils import run_bass_kernel_spmd

    a = {n: np.asarray(v) for n, v in inputs.items()}
    ctx = a["ctx_1024"].reshape(TOKENS, D)
    given = {
        "x_in": a["x"].reshape(TOKENS, D),
        "ctx_in": ctx,
        "ctxt_in": ctx.T,
        "mask0_in": a["mask_1x1xSxS2_ik0"].reshape(SEQ, SEQ),
        "mask1_in": a["mask_BxSxS2_ik1"],
        "g_xattn": a["g_xattn"],
        "g_ffn": a["g_ffn"],
        "wq": a["L0_xattn_wq_w"].T,
        "wk": a["L0_xattn_wk_w"].T,
        "wv": a["L0_xattn_wv_w"].T,
        "wo": a["L0_xattn_wo_w"].T,
        "bq": a["L0_xattn_wq_b"].reshape(D, 1),
        "bk": a["L0_xattn_wk_b"].reshape(D, 1),
        "bv": a["L0_xattn_wv_b"],
        "bo": a["L0_xattn_wo_b"],
        "router0": a["L0_ffn_Wr"],
        "router1": a["L1_ffn_Wg"],
        "up": a["L0_ffn_Wu"],
        "gate": a["L0_ffn_Wg"],
        "down": a["L0_ffn_Wd"],
        "shared_up": a["L0_ffn_Wu_s"],
        "shared_gate": a["L0_ffn_Wg_s"],
        "shared_down": a["L0_ffn_Wd_s"],
        "w1": a["L1_ffn_W1"],
        "b1": a["L1_ffn_b1"],
        "w2": a["L1_ffn_W2"],
        "b2": a["L1_ffn_b2"],
        "const_in": constants(),
    }
    given = {n: np.ascontiguousarray(v) for n, v in given.items()}
    nc = bacc.Bacc("TRN2", target_bir_lowering=False, num_devices=1)
    t = Tensors()
    for n, v in given.items():
        t.__dict__[n] = nc.dram_tensor(n, v.shape, mybir.dt.from_np(v.dtype), kind="ExternalInput").ap()
    t.out = nc.dram_tensor("out", (TOKENS, D), F32, kind="ExternalOutput").ap()
    t.routers = [t.router0, t.router1]
    build(nc, t)
    result = run_bass_kernel_spmd(nc, [given], core_ids=[0])
    return result.results[0]["out"].reshape(BATCH, SEQ, D)
```

```python
from contextlib import ExitStack

import numpy as np

import concourse.bass as bass
from concourse import mybir

F32 = mybir.dt.float32
I32 = mybir.dt.int32
ALU = mybir.AluOpType
ACT = mybir.ActivationFunctionType
AX = mybir.AxisListType

P = 128
SEQ = 64
BATCH = 128
D = 128
HEADS = 16
DK = D // HEADS
TOKENS = BATCH * SEQ
TILES = TOKENS // P
CHUNK = 4
CHUNKS = TILES // CHUNK
E = 8
F = 512
FB = F // P
NEG = 1.0e9
EPS = 1e-5
CAP = 2 * 2 * TOKENS // E
SLOTS = (TOKENS // P + E, 2 * TOKENS // P + E)
MAX_SLOTS = max(SLOTS)
LANES = 8

C_IDENT, C_TRI, C_ONES = 0, P, 2 * P
C_HEAD = 3 * P
C_HALF = C_HEAD + 4
C_FIRST = C_HALF + 2
C_EXPERT = C_FIRST + E
C_SLOT = C_EXPERT + E
C_LANE = C_SLOT + MAX_SLOTS
C_TOKEN = C_LANE + P
C_ALL = C_TOKEN + TILES


def constants():
    c = np.zeros((P, C_ALL), np.float32)
    c[:, C_IDENT:C_IDENT + P] = np.eye(P)
    c[:, C_TRI:C_TRI + P] = np.triu(np.ones((P, P)), 1)
    c[:, C_ONES:C_ONES + P] = 1.0
    c[:, C_HEAD:C_HEAD + 4] = (np.arange(P)[:, None] % 32) // DK == np.arange(4)
    c[:, C_HALF:C_HALF + 2] = np.arange(P)[:, None] // (P // 2) == np.arange(2)
    c[:, C_FIRST:C_FIRST + E] = E - np.arange(E)
    c[:, C_EXPERT:C_EXPERT + E] = np.arange(E)
    c[:, C_SLOT:C_SLOT + MAX_SLOTS] = P * np.arange(MAX_SLOTS)
    c[:, C_LANE:C_LANE + P] = np.arange(P)
    c[:, C_TOKEN:C_TOKEN + TILES] = 1 + np.arange(P)[:, None] + P * np.arange(TILES)
    return c


def spread(ap, dim, n):
    ap = ap.unsqueeze(dim)
    shape = list(ap.shape)
    shape[dim] = n
    return ap.broadcast_to(shape)


def pipeline(eng, tiles, unroll, stages, peeled=2):
    last = max(lag for lag, _ in stages)
    assert last <= unroll and tiles % unroll == 0

    def step(it, k, t):
        for lag, f in stages:
            if t is None or 0 <= t - lag < tiles:
                q, r = divmod(k - lag, unroll)
                f(it + q, r)

    for t in range(peeled * unroll):
        step(t // unroll, t % unroll, t)
    with eng.Fori(peeled, tiles // unroll) as it:
        for k in range(unroll):
            step(it, k, None)
    for k in range(last):
        step(tiles // unroll, k, tiles + k)


def reused(t, buffers):
    return not isinstance(t, int) or t >= buffers


def absorb(eng, ticks):
    eng.sem_inc(ticks, 1)


class Chain:

    def __init__(self, eng, sem):
        self.eng, self.sem, self.n = eng, sem, 0

    def __call__(self, instruction):
        self.n += 1
        instruction.then_inc(self.sem, 1)
        self.eng.wait_ge(self.sem, self.n)


def load_inputs(nc, k):
    with ExitStack() as ctx:
        arrived = ctx.enter_context(nc.semaphore("inputs_arrived"))
        ready = ctx.enter_context(nc.semaphore("gates_ready"))
        awake = ctx.enter_context(nc.semaphore("pool_awake"))
        counted = ctx.enter_context(nc.semaphore("inputs_counted"))
        block = ctx.enter_context(nc.Block())

        @block.sync
        def _(sp):
            n = 0
            xv = k.x_in.rearrange("(t p) d -> p t d", p=P)
            for a in range(0, TILES, TILES // 4):
                sp.dma_start(k.x[:, a:a + TILES // 4, :], xv[:, a:a + TILES // 4, :]).then_inc(arrived, 16)
                n += 1
            sp.dma_start(k.const[:], k.const_in).then_inc(arrived, 16)
            sp.dma_start(k.gates[:, 0:2], k.g_xattn.partition_broadcast(P)).then_inc(arrived, 16)
            sp.dma_start(k.gates[:, 2:4], k.g_ffn.partition_broadcast(P)).then_inc(arrived, 16)
            sp.wait_ge(arrived, 16 * (n + 3))

        @block.gpsimd
        def _(pool):
            nc.gpsimd.memset(k.scratch[:], 0.0).then_inc(awake, 1)
            pool.wait_ge(awake, 1)
            wake_pool(nc, k).then_inc(awake, 1)

        @block.vector
        def _(dve):
            dve.wait_ge(arrived, 16 * 7)
            with dve.Fori(0, TILES // 16) as it:
                for i in range(16):
                    gather_stats(nc, k, 16 * it + i).then_inc(counted, 1)
            dve.wait_ge(counted, TILES)

        @block.scalar
        def _(act):
            act.wait_ge(arrived, 16 * 7)
            nc.scalar.activation(k.gates[:], k.gates[:], ACT.Tanh).then_inc(ready, 1)


def gather_stats(nc, k, t):
    return nc.vector.bn_stats(k.stats[:, bass.ds(t, 1), :].rearrange("p a s -> p (a s)"),
                              k.x[:, bass.ds(t, 1), :].rearrange("p a s -> p (a s)"))


def layer_stats(nc, k, name):
    with ExitStack() as ctx:
        def sb(n, shape):
            return ctx.enter_context(nc.sbuf_tensor(f"{name}_{n}", shape, F32))

        stats = k.stats
        a, b, c, v = (sb(n, [P, TILES]) for n in ("a", "b", "c", "v"))
        steps = ctx.enter_context(nc.semaphore(f"{name}_steps"))
        var_ready = ctx.enter_context(nc.semaphore(f"{name}_var_ready"))
        root_ready = ctx.enter_context(nc.semaphore(f"{name}_root_ready"))
        block = ctx.enter_context(nc.Block())

        @block.vector
        def _(dve):
            do = Chain(dve, steps)
            mean_e, m2_e, mean_o, m2_o = (stats[:, :, i] for i in (1, 2, 4, 5))
            do(nc.vector.tensor_tensor(a[:], mean_e, mean_o, ALU.add))
            do(nc.vector.tensor_tensor(b[:], mean_e, mean_o, ALU.subtract))
            do(nc.vector.tensor_tensor(c[:], m2_e, m2_o, ALU.add))
            do(nc.vector.tensor_scalar(k.mean[:], a[:], 0.5, None, ALU.mult))
            do(nc.vector.tensor_tensor(b[:], b[:], b[:], ALU.mult))
            do(nc.vector.scalar_tensor_tensor(v[:], b[:], D / 4.0, c[:], ALU.mult, ALU.add))
            nc.vector.tensor_scalar(v[:], v[:], 1.0 / D, EPS, ALU.mult, ALU.add).then_inc(var_ready, 1)
            dve.wait_ge(root_ready, 1)
            do(nc.vector.reciprocal(a[:], a[:]))
            do(nc.vector.tensor_tensor(b[:], a[:], a[:], ALU.mult))
            do(nc.vector.tensor_tensor(b[:], b[:], v[:], ALU.mult))
            do(nc.vector.tensor_scalar(b[:], b[:], -0.5, 1.5, ALU.mult, ALU.add))
            do(nc.vector.tensor_tensor(k.rstd[:], a[:], b[:], ALU.mult))

        @block.scalar
        def _(act):
            act.wait_ge(var_ready, 1)
            nc.scalar.activation(a[:], v[:], ACT.Sqrt).then_inc(root_ready, 1)


def wake_pool(nc, k):
    return nc.gpsimd.tensor_scalar(k.scratch[:], k.scratch[:], 1.0, None, ALU.mult)


def normalize(nc, k, out, t):
    return nc.vector.tensor_scalar(out, k.x[:, bass.ds(t, 1), :].rearrange("p a d -> p (a d)"),
                                   k.mean[:, bass.ds(t, 1)], k.rstd[:, bass.ds(t, 1)],
                                   ALU.subtract, ALU.mult)


def project(nc, k, layer):
    first = layer == 0
    with ExitStack() as ctx:
        def sb(n, shape, dt=F32):
            return ctx.enter_context(nc.sbuf_tensor(f"pj{layer}_{n}", shape, dt))

        def ps(n):
            return ctx.enter_context(nc.psum_tensor(f"pj{layer}_{n}", [P, 512], F32))

        def sem(n):
            return ctx.enter_context(nc.semaphore(f"pj{layer}_{n}"))

        U = 4
        xn = [sb(f"xn{i}", [P, CHUNK, D]) for i in range(2)]
        xt = [sb(f"xt{i}", [P, CHUNK * P]) for i in range(2)]
        q_sb = [sb(f"q{i}", [P, CHUNK * P]) for i in range(U)]
        ps_t = [ps(f"ps_t{i}") for i in range(2)]
        if first:
            ctxt = [sb(f"ctxt{i}", [P, CHUNK * P]) for i in range(U)]
            k_sb = [sb(f"k{i}", [P, CHUNK * P]) for i in range(U)]
            v_sb = [sb(f"v{i}", [P, CHUNK, D]) for i in range(U)]
            ps_q, ps_k, ps_v = ([ps(f"ps_{n}{i}") for i in range(2)] for n in "qkv")
            wq, wk, wv = (sb(f"w{n}", [P, D]) for n in "qkv")
            bq, bk = sb("bq", [P, 1]), sb("bk", [P, 1])
            bv, bo = sb("bv", [P, D]), sb("bo", [P, D])
            mask01 = sb("mask01", [P, SEQ])
            keep_col = sb("keep_col", [P, 1])
            keep = sb("keep", [P, SEQ])

        setup = sem("setup")
        steps = sem("steps")
        keep_col_ready, keep_summed = sem("keep_col_ready"), sem("keep_summed")
        ctx_in = [sem(f"ctx_in{i}") for i in range(U)]
        biased = sem("biased")
        normed, transposed, xt_ready = sem("normed"), sem("transposed"), sem("xt_ready")
        q_done, k_done, v_done = sem("q_done"), sem("k_done"), sem("v_done")
        q_ready, k_ready, v_ready = sem("q_ready"), sem("k_ready"), sem("v_ready")
        stored = [sem(f"stored{i}") for i in range(U)]
        outs = 3 if first else 1
        block = ctx.enter_context(nc.Block())

        @block.sync
        def _(sp):
            if first:
                for dst, src in ((wq, k.wq), (wk, k.wk), (wv, k.wv), (bq, k.bq), (bk, k.bk)):
                    sp.dma_start(dst[:], src).then_inc(setup, 16)
                sp.dma_start(bv[:], k.bv.partition_broadcast(P)).then_inc(setup, 16)
                sp.dma_start(bo[:], k.bo.partition_broadcast(P)).then_inc(setup, 16)
                for b in range(2):
                    sp.dma_start(k.mask0[b * SEQ:(b + 1) * SEQ, :], k.mask0_in).then_inc(setup, 16)
            else:
                sp.dma_start(k.mask1[:], k.mask1_in.rearrange("(t b) q k -> (b q) t k", b=2)).then_inc(setup, 16)

            def load(it, kk):
                c, par = U * it + kk, kk % 2
                if reused(c, U):
                    sp.wait_ge(v_done, c - U + 1)
                sp.dma_start(ctxt[kk][:], k.ctxt_in[:, bass.ts(c, 512)]).then_inc(ctx_in[kk], 16)

            def store(it, kk):
                c, par = U * it + kk, kk % 2
                sp.wait_ge(q_ready, c + 1)
                sp.dma_start(k.qt[:, bass.ts(c, 512)], q_sb[kk][:]).then_inc(stored[kk], 16)
                if first:
                    sp.wait_ge(k_ready, c + 1)
                    sp.dma_start(k.kt[:, bass.ts(c, 512)], k_sb[kk][:]).then_inc(stored[kk], 16)
                    sp.wait_ge(v_ready, c + 1)
                    sp.dma_start(k.v.rearrange("(t p) d -> p t d", p=P)[:, bass.ts(c, CHUNK), :],
                                 v_sb[kk][:]).then_inc(stored[kk], 16)

            pipeline(sp, CHUNKS, U, ([(0, load)] if first else []) + [(3, store)])
            for n in range(U):
                sp.wait_ge(stored[n], 16 * outs * CHUNKS // U)

        @block.vector
        def _(dve):
            do = Chain(dve, steps)
            if first:
                dve.wait_ge(setup, 16 * 9)
                do(nc.vector.tensor_scalar(mask01[:], k.mask0[:], 0.0, None, ALU.not_equal))
                nc.vector.tensor_reduce(keep_col[:], mask01[:], AX.X, ALU.max).then_inc(keep_col_ready, 1)
                do(nc.vector.tensor_scalar(k.bias0[:], mask01[:], -1.0, NEG, ALU.add, ALU.mult))
                do(nc.vector.tensor_scalar(bo[:], bo[:], k.gates[:, 0:1], None, ALU.mult))
                dve.wait_ge(keep_summed, 1)
                do(nc.vector.tensor_scalar(keep[:], ps_k[0][:, 0:SEQ], DK ** -0.5, None, ALU.mult))
            else:
                dve.wait_ge(setup, 16)
                do(nc.vector.tensor_scalar(k.bias1[:], k.mask1[:], -1.0, NEG, ALU.add, ALU.mult))

            def norm(it, kk):
                c, par = U * it + kk, kk % 2
                if reused(c, 2):
                    dve.wait_ge(transposed, c - 1)
                for j in range(CHUNK):
                    normalize(nc, k, xn[par][:, j, :], c * CHUNK + j).then_inc(normed, 1)

            def queries(it, kk):
                c, par = U * it + kk, kk % 2
                dve.wait_ge(q_done, c + 1)
                if reused(c, U):
                    dve.wait_ge(stored[kk], 16 * outs * it)
                nc.vector.scalar_tensor_tensor(
                    q_sb[kk][:].rearrange("p (s q) -> p s q", q=SEQ),
                    ps_q[par][:].rearrange("p (s q) -> p s q", q=SEQ), bq[:, 0:1],
                    spread(keep[:], 1, 2 * CHUNK), ALU.add, ALU.mult).then_inc(q_ready, 1)

            def values(it, kk):
                c, par = U * it + kk, kk % 2
                dve.wait_ge(v_done, c + 1)
                if reused(c, U):
                    dve.wait_ge(stored[kk], 16 * outs * it)
                nc.vector.tensor_tensor(v_sb[kk][:], ps_v[par][:].rearrange("p (t d) -> p t d", d=D),
                                        spread(bv[:], 1, CHUNK), ALU.add).then_inc(v_ready, 1)

            def out_bias(it, kk):
                c = U * it + kk
                dve.wait_ge(normed, CHUNK * (c + 1))
                xc = k.x[:, bass.ts(c, CHUNK), :]
                nc.vector.tensor_tensor(xc, xc, spread(bo[:], 1, CHUNK), ALU.add).then_inc(biased, 1)

            pipeline(dve, CHUNKS, U, [(0, norm)] + ([(0, out_bias), (2, queries), (2, values)] if first else []))

        @block.tensor
        def _(pe):
            ident = k.const[:, C_IDENT:C_IDENT + P]
            if first:
                pe.wait_ge(keep_col_ready, 1)
                nc.tensor.matmul(ps_k[0][:, 0:SEQ], keep_col[0:SEQ, 0:1].broadcast_to([SEQ, P]),
                                 ident[0:SEQ, 0:SEQ], start=True, stop=True).then_inc(keep_summed, 1)

            def transposes(it, kk):
                c, par = U * it + kk, kk % 2
                pe.wait_ge(normed, CHUNK * (c + 1))
                if reused(c, 2):
                    pe.wait_ge(xt_ready if first else q_ready, c - 1)
                for j in range(CHUNK):
                    last = nc.tensor.transpose(ps_t[par][:, j * P:(j + 1) * P], xn[par][:, j, :], ident)
                last.then_inc(transposed, 1)

            def products(it, kk):
                c, par = U * it + kk, kk % 2
                if not reused(c, 1):
                    pe.wait_ge(setup, 16 * 9)
                    pe.wait_ge(steps, 4)
                pe.wait_ge(ctx_in[kk], 16 * (it + 1))
                if reused(c, 2):
                    pe.wait_ge(k_ready, c - 1)
                nc.tensor.matmul(ps_k[par][:], wk[:], ctxt[kk][:], start=True, stop=True).then_inc(k_done, 1)
                if reused(c, 2):
                    pe.wait_ge(v_ready, c - 1)
                for j in range(CHUNK):
                    last = nc.tensor.matmul(ps_v[par][:, j * P:(j + 1) * P], ctxt[kk][:, j * P:(j + 1) * P],
                                            wv[:], start=True, stop=True)
                last.then_inc(v_done, 1)
                pe.wait_ge(xt_ready, c + 1)
                if reused(c, 2):
                    pe.wait_ge(q_ready, c - 1)
                nc.tensor.matmul(ps_q[par][:], wq[:], xt[par][:], start=True, stop=True).then_inc(q_done, 1)

            pipeline(pe, CHUNKS, U, [(0, transposes)] + ([(1, products)] if first else []))

        @block.scalar
        def _(act):
            def columns(it, kk):
                c, par = U * it + kk, kk % 2
                act.wait_ge(transposed, c + 1)
                if first:
                    if reused(c, 2):
                        act.wait_ge(q_done, c - 1)
                    nc.scalar.activation(xt[par][:], ps_t[par][:], ACT.Copy).then_inc(xt_ready, 1)
                else:
                    if reused(c, U):
                        act.wait_ge(stored[kk], 16 * it)
                    nc.scalar.activation(q_sb[kk][:], ps_t[par][:], ACT.Copy, scale=DK ** -0.5).then_inc(q_ready, 1)

            def keys(it, kk):
                c, par = U * it + kk, kk % 2
                if not reused(c, 1):
                    act.wait_ge(setup, 16 * 9)
                act.wait_ge(k_done, c + 1)
                if reused(c, U):
                    act.wait_ge(stored[kk], 16 * outs * it)
                nc.scalar.activation(k_sb[kk][:], ps_k[par][:], ACT.Identity, bias=bk[:, 0:1]).then_inc(k_ready, 1)

            pipeline(act, CHUNKS, U, [(0, columns)] + ([(1, keys)] if first else []))


def attend(nc, k, layer):
    first = layer == 0
    HALF = P // 2
    LOAD = 4
    U = 2 * LOAD
    with ExitStack() as ctx:
        def sb(n, shape, dt=F32):
            return ctx.enter_context(nc.sbuf_tensor(f"at{layer}_{n}", shape, dt))

        def ps(n, shape):
            return ctx.enter_context(nc.psum_tensor(f"at{layer}_{n}", shape, F32))

        def sem(n):
            return ctx.enter_context(nc.semaphore(f"at{layer}_{n}"))

        q2 = [sb(f"q2{i}", [P, 2, 2, LOAD, P]) for i in range(2)]
        k2 = [sb(f"k2{i}", [P, 2, LOAD, SEQ]) for i in range(2)]
        v2 = [sb(f"v2{i}", [P, LOAD, 2, D]) for i in range(2)]
        keys = [sb(f"keys{i}", [P, 2 if first else 1, 4, 2, LOAD, SEQ]) for i in range(2)]
        vals = [sb(f"vals{i}", [P, LOAD, 2, 8, 2, DK + 1]) for i in range(2)]
        s_sb = [sb(f"s{i}", [P, HEADS, SEQ]) for i in range(4)]
        top = [sb(f"top{i}", [P, HEADS]) for i in range(2)]
        pt = [sb(f"pt{i}", [P, 8, P]) for i in range(2)]
        inv = [sb(f"inv{i}", [P, HEADS]) for i in range(2)]
        heads = [sb(f"heads{i}", [P, D]) for i in range(4)]
        ps_s = [ps(f"ps_s{i}", [P, 2, 512]) for i in range(2)]
        ps_p = ps("ps_p", [P, 8, P])
        ps_o = ps("ps_o", [P, 512])
        ps_w = ps("ps_w", [P, 512])
        sums = ps_o[:, 0:8 * 36].rearrange("p (u b r c) -> p u b r c", b=2, r=2, c=DK + 1)
        if first:
            wo = sb("wo", [P, D])
            ht = sb("ht", [P, P])
        sums_sb = [sb(f"sums{i}", [P, HEADS, DK + 1]) for i in range(4)]
        kv_loaded, q_loaded = ([sem(f"{n}_loaded{i}") for i in range(2)] for n in ("kv", "q"))
        setup, cleared = sem("setup"), sem("cleared")
        sp_ticks, pool_ticks, dve_ticks = sem("sp_ticks"), sem("pool_ticks"), sem("dve_ticks")
        marked, counted = sem("marked"), sem("counted")
        keys_spread, vals_spread = sem("keys_spread"), sem("vals_spread")
        scored, masked, topped, shifted = sem("scored"), sem("masked"), sem("topped"), sem("shifted")
        exped, turned, turned_out, summed = sem("exped"), sem("turned"), sem("turned_out"), sem("summed")
        inverted, normalized, sums_out = sem("inverted"), sem("normalized"), sem("sums_out")
        heads_turned, ht_ready, projected, added = (
            sem("heads_turned"), sem("ht_ready"), sem("projected"), sem("added"))
        block = ctx.enter_context(nc.Block())

        KV_DMAS, Q_DMAS = 8 + 2, 8
        MARKS = 5 if first else 1
        SPREADS = 2 if first else 1

        @block.sync
        def _(sp):
            if first:
                sp.dma_start(wo[:], k.wo).then_inc(setup, 16)
            qv = k.qt.rearrange("(G g f) (t b q) -> G b f g t q", G=2, g=2, b=2, q=SEQ)
            kv = (k.kt if first else k.ctxt_in).rearrange("(G g f) (t b q) -> G b f g t q", G=2, g=2, b=2, q=SEQ)
            vv = (k.v if first else k.ctx_in).rearrange("(t b q) d -> q t b d", b=2, q=SEQ)

            def load(it, par):
                s = 2 * it + par
                if reused(s, 2):
                    sp.wait_ge(scored, LOAD * (s - 1))
                    absorb(sp, sp_ticks)
                    sp.wait_ge(keys_spread, SPREADS * (s - 1))
                    absorb(sp, sp_ticks)
                    sp.wait_ge(vals_spread, 2 * (s - 1))
                    absorb(sp, sp_ticks)
                some = bass.ts(s, LOAD)
                for G in range(2):
                    for b in range(2):
                        rows = slice(HALF * G + 32 * b, HALF * G + 32 * b + 32)
                        for g in range(2):
                            sp.dma_start(k2[par][rows, g, :, :], kv[G, b, :, g, some, :]).then_inc(kv_loaded[par], 16)
                for half in range(2):
                    sp.dma_start(v2[par][HALF * half:HALF * half + HALF, :, :, :],
                                 vv[:, some, :, :]).then_inc(kv_loaded[par], 16)
                if not reused(s, 2):
                    sp.wait_ge(marked, MARKS * (s + 1))
                for G in range(2):
                    for b in range(2):
                        rows = slice(HALF * G + 32 * b, HALF * G + 32 * b + 32)
                        for g in range(2):
                            sp.dma_start(q2[par][rows, G, g, :, b * SEQ:(b + 1) * SEQ],
                                         qv[G, b, :, g, some, :]).then_inc(q_loaded[par], 16)

            pipeline(sp, TILES // LOAD, 2, [(0, load)])

        @block.gpsimd
        def _(pool):
            for i in range(2):
                nc.gpsimd.memset(vals[i][:], 0.0).then_inc(cleared, 1)
            pool.wait_ge(cleared, 2)
            for i in range(2):
                for r in range(2):
                    nc.gpsimd.memset(vals[i][HALF * r:HALF * r + HALF, :, :, :, r, DK:DK + 1],
                                     1.0).then_inc(cleared, 1)
            pool.wait_ge(cleared, 6)
            head_of = k.const[:, C_HEAD:C_HEAD + 4]

            def spread_keys(it, buf):
                s = 2 * it + buf
                pool.wait_ge(kv_loaded[buf], 16 * KV_DMAS * (it + 1))
                if reused(s, 2):
                    pool.wait_ge(scored, LOAD * (s - 1))
                    absorb(pool, pool_ticks)
                for G in range(SPREADS):
                    rows = slice(HALF * G, HALF * G + HALF) if first else slice(0, P)
                    if G:
                        pool.wait_ge(keys_spread, SPREADS * s + 1)
                        absorb(pool, pool_ticks)
                    nc.gpsimd.tensor_tensor(
                        keys[buf][rows, G, :, :, :, :].rearrange("p h g t k -> p h (g t k)"),
                        spread(k2[buf][rows, :, :, :].rearrange("p g t k -> p (g t k)"), 1, 4),
                        spread(head_of[rows, :], 2, 2 * LOAD * SEQ), ALU.mult).then_inc(keys_spread, 1)

            def spread_values(it, buf):
                s = 2 * it + buf
                if reused(s, 2):
                    pool.wait_ge(summed, LOAD * (s - 1))
                    absorb(pool, pool_ticks)
                if first:
                    pool.wait_ge(keys_spread, SPREADS * (s + 1))
                    absorb(pool, pool_ticks)
                for r in range(2):
                    nc.gpsimd.tensor_tensor(
                        vals[buf][:, :, :, :, r, 0:DK].rearrange("p t b u c -> p (t b) u c"),
                        v2[buf][:].rearrange("p t b (u r c) -> p (t b) u r c", r=2, c=DK)[:, :, :, r, :],
                        spread(spread(k.const[:, C_HALF + r:C_HALF + r + 1].broadcast_to([P, DK]), 1, 8),
                               1, 2 * LOAD),
                        ALU.mult).then_inc(vals_spread, 1)

            def spread_ahead(it, kk):
                if kk % LOAD == 0:
                    spread_keys(it, kk // LOAD)

            def spread_behind(it, kk):
                if kk % LOAD == 0:
                    spread_values(it, kk // LOAD)

            pipeline(pool, TILES, U, [(0, spread_ahead), (2, spread_behind)], peeled=1)

        @block.tensor
        def _(pe):
            ident = k.const[:, C_IDENT:C_IDENT + P]

            def scores(it, kk):
                t, par, buf, tt = U * it + kk, kk % 2, kk // LOAD, kk % LOAD
                if not reused(t, U) and tt == 0:
                    pe.wait_ge(marked, MARKS * (buf + 1))
                if tt == 0:
                    pe.wait_ge(q_loaded[buf], 16 * Q_DMAS * (it + 1))
                    pe.wait_ge(keys_spread, SPREADS * (2 * it + buf + 1))
                if reused(t, 2):
                    pe.wait_ge(shifted if first else masked, t - 1 if first else 2 * t - 2)
                for g in range(2):
                    for G in range(2):
                        last = nc.tensor.matmul(ps_s[par][:, G, 256 * g:256 * g + 256], q2[buf][:, G, g, tt, :],
                                                keys[buf][:, G if first else 0, :, g, tt, :],
                                                start=True, stop=True)
                last.then_inc(scored, 1)

            def turn(it, kk):
                t = U * it + kk
                pe.wait_ge(exped, t + 1)
                if reused(t, 1):
                    pe.wait_ge(turned_out, 2 * t)
                for u in range(8):
                    last = nc.tensor.transpose(
                        ps_p[:, u, :], s_sb[kk % 4][:, 2 * u:2 * u + 2, :].rearrange("p h k -> p (h k)"), ident)
                last.then_inc(turned, 1)

            def weigh(it, kk):
                t, par, buf, tt = U * it + kk, kk % 2, kk // LOAD, kk % LOAD
                pe.wait_ge(turned_out, 2 * t + 2)
                if tt == 0:
                    pe.wait_ge(vals_spread, 2 * (2 * it + buf + 1))
                if reused(t, 1):
                    pe.wait_ge(sums_out, 2 * t)
                for u in range(8):
                    last = nc.tensor.matmul(ps_o[:, 36 * u:36 * u + 36], pt[par][:, u, :],
                                            vals[buf][:, tt, :, u, :, :].rearrange("p b r c -> p b (r c)"),
                                            start=True, stop=True)
                last.then_inc(summed, 1)

            def turn_heads(it, kk):
                t = U * it + kk
                pe.wait_ge(normalized, t + 1)
                if reused(t, 1):
                    pe.wait_ge(added, t)
                nc.tensor.transpose(ps_w[:, 0:P], heads[kk % 4][:], ident).then_inc(heads_turned, 1)

            def project_heads(it, kk):
                t = U * it + kk
                if not reused(t, 1):
                    pe.wait_ge(setup, 16)
                pe.wait_ge(ht_ready, t + 1)
                nc.tensor.matmul(ps_w[:, P:2 * P], ht[:], wo[:], start=True, stop=True).then_inc(projected, 1)

            pipeline(pe, TILES, U, [(0, scores)] + ([(5, turn_heads)] if first else []) + [(2, turn), (3, weigh)]
                     + ([(5, project_heads)] if first else []), peeled=1)

        @block.scalar
        def _(act):
            def exponent(it, kk):
                t, buf = U * it + kk, kk % 4
                act.wait_ge(shifted, t + 1)
                nc.scalar.activation(s_sb[buf][:], s_sb[buf][:], ACT.Exp).then_inc(exped, 1)

            def turn_out(it, kk):
                t, par = U * it + kk, kk % 2
                act.wait_ge(turned, t + 1)
                if reused(t, 2):
                    act.wait_ge(summed, t - 1)
                for h in range(2):
                    nc.scalar.activation(pt[par][:, 4 * h:4 * h + 4, :], ps_p[:, 4 * h:4 * h + 4, :],
                                         ACT.Copy).then_inc(turned_out, 1)

            def sums_away(it, kk):
                t, buf = U * it + kk, kk % 4
                act.wait_ge(summed, t + 1)
                if reused(t, 4):
                    act.wait_ge(normalized, t - 3)
                for b in range(2):
                    rows = slice(HALF * b, HALF * b + HALF)
                    nc.scalar.activation(sums_sb[buf][rows, :, :].rearrange("p (u r) c -> p u r c", r=2),
                                         sums[rows, :, b, :, :], ACT.Copy).then_inc(sums_out, 1)

            def heads_out(it, kk):
                t = U * it + kk
                act.wait_ge(heads_turned, t + 1)
                nc.scalar.activation(ht[:], ps_w[:, 0:P], ACT.Copy).then_inc(ht_ready, 1)

            pipeline(act, TILES, U, [(4, sums_away)] + ([(5, heads_out)] if first else []) + [(2, turn_out), (1, exponent)],
                     peeled=1)

        @block.vector
        def _(dve):
            gate = k.gates[:, layer:layer + 1]

            def scores_of(it, kk):
                if not first:
                    return s_sb[kk % 4][:]
                return ps_s[kk % 2][:].rearrange("p G (h k) -> p (G h) k", k=SEQ)

            def mask(it, kk):
                t, par, s = U * it + kk, kk % 2, s_sb[kk % 4]
                dve.wait_ge(scored, t + 1)
                if reused(t, 4):
                    dve.wait_ge(turned, t - 3)
                bias = k.bias1[:, bass.ds(t, 1), :].rearrange("p a k -> p (a k)")
                for G in range(2):
                    nc.vector.tensor_tensor(s[:, 8 * G:8 * G + 8, :],
                                            ps_s[par][:, G, :].rearrange("p (h k) -> p h k", k=SEQ),
                                            spread(bias, 1, 8), ALU.add).then_inc(masked, 1)

            def find_top(it, kk):
                t, par = U * it + kk, kk % 2
                if first:
                    dve.wait_ge(scored, t + 1)
                else:
                    dve.wait_ge(masked, 2 * t + 2)
                nc.vector.tensor_reduce(top[par][:], scores_of(it, kk), AX.X, ALU.max).then_inc(topped, 1)

            def shift(it, kk):
                t, par, s = U * it + kk, kk % 2, s_sb[kk % 4]
                if first and reused(t, 4):
                    dve.wait_ge(turned, t - 3)
                dve.wait_ge(topped, t + 1)
                nc.vector.tensor_tensor(s[:], scores_of(it, kk), spread(top[par][:], 2, SEQ),
                                        ALU.subtract).then_inc(shifted, 1)

            def invert(it, kk):
                t, par, buf = U * it + kk, kk % 2, kk % 4
                dve.wait_ge(sums_out, 2 * t + 2)
                nc.vector.reciprocal(inv[par][:], sums_sb[buf][:, :, DK]).then_inc(inverted, 1)

            def divide(it, kk):
                t, par, buf = U * it + kk, kk % 2, kk % 4
                if reused(t, 4):
                    dve.wait_ge(added, t - 3)
                dve.wait_ge(inverted, t + 1)
                nc.vector.tensor_tensor(heads[buf][:].rearrange("p (h c) -> p h c", c=DK), sums_sb[buf][:, :, 0:DK],
                                        spread(inv[par][:], 2, DK), ALU.mult).then_inc(normalized, 1)

            def add(it, kk):
                t = U * it + kk
                if first:
                    dve.wait_ge(projected, t + 1)
                    src = ps_w[:, P:2 * P]
                else:
                    dve.wait_ge(normalized, t + 1)
                    src = heads[kk % 4][:]
                xt = k.x[:, bass.ds(t, 1), :].rearrange("p a d -> p (a d)")
                nc.vector.scalar_tensor_tensor(xt, src, gate, xt, ALU.mult, ALU.add).then_inc(added, 1)

            def count(it, kk):
                t = U * it + kk
                dve.wait_ge(added, t + 1)
                absorb(dve, dve_ticks)
                gather_stats(nc, k, t).then_inc(counted, 1)

            for i in range(2):
                nc.vector.memset(q2[i][:], 0.0).then_inc(marked, 1)
                if first:
                    ident = k.const[:, C_IDENT:C_IDENT + P]
                    dve.wait_ge(marked, MARKS * i + 1)
                    for G in range(2):
                        rows = slice(HALF * (1 - G), HALF * (1 - G) + HALF)
                        nc.vector.tensor_copy(q2[i][rows, G, :, :, :].rearrange("p g t (b q) -> p (g t b) q", b=2),
                                              spread(ident[rows, rows], 1, 4 * LOAD)).then_inc(marked, 1)
                        nc.vector.tensor_copy(keys[i][rows, G, :, :, :, :].rearrange("p h g t k -> p (h g t) k"),
                                              spread(k.bias0[rows, :], 1, 8 * LOAD)).then_inc(marked, 1)

            if first:
                pipeline(dve, TILES, U, [(6, add), (0, find_top), (4, invert), (0, shift), (4, divide), (7, count)],
                         peeled=1)
            else:
                pipeline(dve, TILES, U, [(0, mask), (4, invert), (0, find_top), (4, divide), (0, shift), (4, add),
                                         (5, count)], peeled=1)
            dve.wait_ge(counted, TILES)


def load_experts(sp, k, layer):
    given = E - 1 if layer == 0 else E
    w1, wd = (k.up, k.down) if layer == 0 else (k.w1, k.w2)
    sp.dma_start(k.w_in[:, 0:given * F].rearrange("p (e f) -> p e f", e=given),
                 w1.rearrange("e p f -> p e f")).then_inc(k.weights_in, 16)
    if layer == 0:
        sp.dma_start(k.w_gate[:, 0:given * F].rearrange("p (e f) -> p e f", e=given),
                     k.gate.rearrange("e p f -> p e f")).then_inc(k.weights_in, 16)
    else:
        sp.dma_start(k.b1_all[:], k.b1.rearrange("e f -> (e f)").partition_broadcast(P)).then_inc(k.weights_in, 16)
        sp.dma_start(k.b2_all[:], k.b2.rearrange("e d -> (e d)").partition_broadcast(P)).then_inc(k.weights_in, 16)
    sp.dma_start(k.w_out[:, 0:given * FB * D].rearrange("p (e c d) -> p e c d", e=given, c=FB),
                 wd.rearrange("e (c p) d -> p e c d", p=P)).then_inc(k.weights_in, 16)


def route(nc, k, layer):
    picks = layer + 1
    slots = SLOTS[layer]
    with ExitStack() as ctx:
        def sb(n, shape, dt=F32):
            return ctx.enter_context(nc.sbuf_tensor(f"ro{layer}_{n}", shape, dt))

        def ps(n):
            return ctx.enter_context(nc.psum_tensor(f"ro{layer}_{n}", [P, 512], F32))

        def sem(n):
            return ctx.enter_context(nc.semaphore(f"ro{layer}_{n}"))

        U = 4
        xn = [sb(f"xn{i}", [P, CHUNK, D]) for i in range(U)]
        xt = [sb(f"xt{i}", [P, CHUNK * P]) for i in range(U)]
        router = sb("router", [P, E])
        logits = sb("logits", [P, TILES, E])
        ps_t, ps_l = [ps(f"ps_t{i}") for i in range(2)], [ps(f"ps_l{i}") for i in range(2)]
        ps_c = [ps(f"ps_c{i}") for i in range(4)]
        work, prob = sb("work", [P, TILES, E]), sb("prob", [P, TILES, E])
        hot = [sb(f"hot{i}", [P, TILES, E]) for i in range(picks)]
        before = [sb(f"before{i}", [P, TILES, E]) for i in range(picks)]
        total = sb("total", [P, picks, E])
        m = [sb(f"m{i}", [P, TILES]) for i in range(picks)]
        col, inv_sum = sb("col", [P, TILES]), sb("inv_sum", [P, TILES])
        tiles_i, n_tiles = sb("tiles_i", [P, E], I32), sb("n_tiles", [P, E])
        ends, starts = sb("ends", [P, E]), sb("starts", [P, E])
        load_e, slot_i = sb("load_e", [P, E]), sb("slot_i", [P, TILES], I32)
        ge_end, row = sb("ge_end", [P, slots, E]), sb("row", [P, slots])

        setup, normed, transposed, xt_ready = sem("setup"), sem("normed"), sem("transposed"), sem("xt_ready")
        shared_in = sem("shared_in")
        kept = [sem(f"kept{i}") for i in range(U)]
        copied, logits_done, logits_out = sem("copied"), sem("logits_done"), sem("logits_out")
        steps, hot_ready, counted = sem("steps"), sem("hot_ready"), sem("counted")
        diff_ready, prob_ready = sem("diff_ready"), sem("prob_ready")
        block = ctx.enter_context(nc.Block())

        @block.sync
        def _(sp):
            sp.dma_start(router[:], k.routers[layer]).then_inc(setup, 16)

            def keep_rows(it, kk):
                c, par = U * it + kk, kk % 2
                sp.wait_ge(normed, CHUNK * (c + 1))
                sp.dma_start(k.xn.rearrange("(t p) d -> p t d", p=P)[:, bass.ts(c, CHUNK), :],
                             xn[kk][:]).then_inc(kept[kk], 16)

            pipeline(sp, CHUNKS, U, [(0, keep_rows)])
            if not layer:
                wu, wg, wd = k.shared_w
                sp.dma_start(wu[:], k.shared_up).then_inc(shared_in, 16)
                sp.dma_start(wg[:], k.shared_gate).then_inc(shared_in, 16)
                sp.dma_start(wd[:], k.shared_down.rearrange("(c p) d -> p c d", p=P)).then_inc(shared_in, 16)
                sp.wait_ge(shared_in, 16 * 3)
            load_experts(sp, k, layer)
            for n in range(U):
                sp.wait_ge(kept[n], 16 * CHUNKS // U)

        @block.tensor
        def _(pe):
            ident = k.const[:, C_IDENT:C_IDENT + P]

            def transposes(it, kk):
                c, par = U * it + kk, kk % 2
                pe.wait_ge(normed, CHUNK * (c + 1))
                if reused(c, 2):
                    pe.wait_ge(xt_ready, c - 1)
                for j in range(CHUNK):
                    last = nc.tensor.transpose(ps_t[par][:, j * P:(j + 1) * P], xn[kk][:, j, :], ident)
                last.then_inc(transposed, 1)

            def score(it, kk):
                c, par = U * it + kk, kk % 2
                if not reused(c, 1):
                    pe.wait_ge(setup, 16)
                pe.wait_ge(xt_ready, c + 1)
                if reused(c, 2):
                    pe.wait_ge(logits_out, c - 1)
                for j in range(CHUNK):
                    last = nc.tensor.matmul(ps_l[par][:, j * E:(j + 1) * E], xt[kk][:, j * P:(j + 1) * P],
                                            router[:], start=True, stop=True)
                last.then_inc(logits_done, 1)

            pipeline(pe, CHUNKS, U, [(0, transposes), (2, score)])
            for i in range(picks):
                pe.wait_ge(hot_ready, i + 1)
                chosen = hot[i][:].rearrange("p t e -> p (t e)")
                nc.tensor.matmul(ps_c[2 * i][:], k.const[:, C_TRI:C_TRI + P], chosen, start=True, stop=True)
                nc.tensor.matmul(ps_c[2 * i + 1][:], k.const[:, C_ONES:C_ONES + P], chosen,
                                 start=True, stop=True).then_inc(counted, 1)

        @block.scalar
        def _(act):
            def columns(it, kk):
                c, par = U * it + kk, kk % 2
                act.wait_ge(transposed, c + 1)
                if reused(c, U):
                    act.wait_ge(logits_done, c - U + 1)
                    if not layer:
                        act.wait_ge(copied, c - U + 1)
                nc.scalar.activation(xt[kk][:], ps_t[par][:], ACT.Copy).then_inc(xt_ready, 1)

            pipeline(act, CHUNKS, U, [(0, columns)])
            act.wait_ge(diff_ready, 1)
            nc.scalar.activation(prob[:], work[:], ACT.Exp).then_inc(prob_ready, 1)

        @block.vector
        def _(dve):
            def norm(it, kk):
                c, par = U * it + kk, kk % 2
                if reused(c, U):
                    dve.wait_ge(transposed, c - U + 1)
                    dve.wait_ge(kept[kk], 16 * it)
                for j in range(CHUNK):
                    normalize(nc, k, xn[kk][:, j, :], c * CHUNK + j).then_inc(normed, 1)

            def keep_columns(it, kk):
                c, par = U * it + kk, kk % 2
                dve.wait_ge(xt_ready, c + 1)
                nc.vector.tensor_scalar(k.xnt[:, bass.ts(c, 512)], xt[kk][:], 1.0, None,
                                        ALU.mult).then_inc(copied, 1)

            def keep_logits(it, kk):
                c, par = U * it + kk, kk % 2
                dve.wait_ge(logits_done, c + 1)
                nc.vector.tensor_scalar(logits[:, bass.ts(c, CHUNK), :],
                                        ps_l[par][:, 0:CHUNK * E].rearrange("p (t e) -> p t e", e=E),
                                        1.0, None, ALU.mult).then_inc(logits_out, 1)

            pipeline(dve, CHUNKS, U, [(0, norm)] + ([] if layer else [(2, keep_columns)]) + [(3, keep_logits)])
            dve.wait_ge(logits_out, CHUNKS)
            do = Chain(dve, steps)
            first_of = spread(k.const[:, C_FIRST:C_FIRST + E], 1, TILES)

            def pick(i):
                do(nc.vector.tensor_reduce(m[i][:], logits[:], AX.X, ALU.max))
                do(nc.vector.tensor_tensor(work[:], logits[:], spread(m[i][:], 2, E), ALU.is_equal))
                do(nc.vector.tensor_tensor(work[:], work[:], first_of, ALU.mult))
                do(nc.vector.tensor_reduce(col[:], work[:], AX.X, ALU.max))
                nc.vector.tensor_tensor(hot[i][:], work[:], spread(col[:], 2, E), ALU.is_equal).then_inc(hot_ready, 1)
                dve.wait_ge(hot_ready, i + 1)

            pick(0)
            do(nc.vector.tensor_tensor(prob[:], logits[:], spread(m[0][:], 2, E), ALU.subtract))
            if picks == 2:
                do(nc.vector.scalar_tensor_tensor(logits[:], hot[0][:], -3.0e38, logits[:], ALU.mult, ALU.add))
                pick(1)
            nc.vector.tensor_copy(work[:], prob[:]).then_inc(diff_ready, 1)
            dve.wait_ge(prob_ready, 1)
            do(nc.vector.tensor_reduce(inv_sum[:], prob[:], AX.X, ALU.add))
            do(nc.vector.reciprocal(inv_sum[:], inv_sum[:]))

            for i in range(picks):
                dve.wait_ge(counted, i + 1)
                per_tile = ps_c[2 * i + 1][:].rearrange("p (t e) -> p t e", e=E)
                do(nc.vector.tensor_copy(work[:], per_tile))
                for e in range(E):
                    do(nc.vector.tensor_tensor_scan(before[i][:, :, e], k.const[:, C_ONES:C_ONES + TILES],
                                                    work[:, :, e], 0.0, ALU.mult, ALU.add))
                do(nc.vector.tensor_copy(total[:, i, :], before[i][:, TILES - 1, :]))
                do(nc.vector.tensor_tensor(before[i][:], before[i][:], work[:], ALU.subtract))
                do(nc.vector.tensor_tensor(before[i][:], before[i][:],
                                           ps_c[2 * i][:].rearrange("p (t e) -> p t e", e=E), ALU.add))

            def chosen(out, i, values):
                do(nc.vector.tensor_tensor(work[:], values, hot[i][:], ALU.mult))
                do(nc.vector.tensor_reduce(out, work[:], AX.X, ALU.add))

            if picks == 1:
                do(nc.vector.tensor_scalar(k.weight[0][:], inv_sum[:], 2.0, k.gates[:, 2:3], ALU.mult, ALU.mult))
                do(nc.vector.tensor_copy(load_e[:], total[:, 0, :]))
            else:
                gate1, gate2, denom = m[0], m[1], col
                do(nc.vector.tensor_copy(gate1[:], inv_sum[:]))
                chosen(gate2[:], 1, prob[:])
                do(nc.vector.tensor_tensor(gate2[:], gate2[:], inv_sum[:], ALU.mult))
                do(nc.vector.tensor_tensor(denom[:], gate1[:], gate2[:], ALU.add))
                do(nc.vector.tensor_scalar(denom[:], denom[:], 1e-9, None, ALU.add))
                do(nc.vector.reciprocal(denom[:], denom[:]))
                for i, gate in enumerate((gate1, gate2)):
                    do(nc.vector.tensor_tensor(gate[:], gate[:], denom[:], ALU.mult))
                    do(nc.vector.tensor_scalar(k.weight[i][:], gate[:], k.gates[:, 3:4], None, ALU.mult))
                chosen(gate1[:], 0, before[0][:])
                do(nc.vector.tensor_tensor(prob[:], before[1][:], spread(total[:, 0, :], 1, TILES), ALU.add))
                chosen(gate2[:], 1, prob[:])
                for i, pos in enumerate((gate1, gate2)):
                    do(nc.vector.tensor_scalar(pos[:], pos[:], float(CAP), None, ALU.is_lt))
                    do(nc.vector.tensor_tensor(k.weight[i][:], k.weight[i][:], pos[:], ALU.mult))
                do(nc.vector.tensor_tensor(load_e[:], total[:, 0, :], total[:, 1, :], ALU.add))
                do(nc.vector.tensor_tensor(before[0][:], before[0][:], before[1][:], ALU.add))

            do(nc.vector.tensor_scalar(n_tiles[:], load_e[:], P - 1.0, None, ALU.add))
            do(nc.vector.tensor_copy(tiles_i[:], n_tiles[:]))
            do(nc.vector.tensor_scalar(tiles_i[:], tiles_i[:], 7, None, ALU.arith_shift_right))
            do(nc.vector.tensor_copy(n_tiles[:], tiles_i[:]))
            do(nc.vector.tensor_scalar(n_tiles[:], n_tiles[:], float(P), None, ALU.mult))
            do(nc.vector.tensor_tensor_scan(ends[:], k.const[:, C_ONES:C_ONES + E], n_tiles[:], 0.0,
                                            ALU.mult, ALU.add))
            do(nc.vector.tensor_tensor(starts[:], ends[:], n_tiles[:], ALU.subtract))
            do(nc.vector.tensor_tensor(before[0][:], before[0][:], spread(starts[:], 1, TILES), ALU.add))
            for i in range(picks):
                chosen(col[:], i, before[0][:])
                do(nc.vector.tensor_copy(slot_i[:], col[:]))
                do(nc.vector.tensor_scalar(slot_i[:], slot_i[:], 7, None, ALU.arith_shift_right))
                do(nc.vector.tensor_copy(k.tile_at[i][:], slot_i[:]))
                do(nc.vector.tensor_scalar(k.tile_at[i][:], k.tile_at[i][:], float(P), None, ALU.mult))
                do(nc.vector.tensor_tensor(k.lane[i][:], col[:], k.tile_at[i][:], ALU.subtract))
            do(nc.vector.tensor_tensor(ge_end[:], spread(k.const[:, C_SLOT:C_SLOT + slots], 2, E),
                                       spread(ends[:], 1, slots), ALU.is_ge))
            do(nc.vector.tensor_reduce(row[:], ge_end[:], AX.X, ALU.add))
            do(nc.vector.tensor_scalar(row[:], row[:], E - 1.0, None, ALU.min))
            do(nc.vector.tensor_copy(k.slot_expert[:, 0:slots], row[:]))


def place(nc, k, layer):
    picks = layer + 1
    slots = SLOTS[layer]
    shared = layer == 0
    with ExitStack() as ctx:
        def sb(n, shape, dt=F32):
            return ctx.enter_context(nc.sbuf_tensor(f"pl{layer}_{n}", shape, dt))

        def ps(n):
            return ctx.enter_context(nc.psum_tensor(f"pl{layer}_{n}", [P, 512], F32))

        def sem(n):
            return ctx.enter_context(nc.semaphore(f"pl{layer}_{n}"))

        U = 8
        in_lane = [[sb(f"in_lane{i}_{j}", [P, P]) for i in range(2)] for j in range(picks)]
        in_tile = [[sb(f"in_tile{i}_{j}", [P, slots]) for i in range(2)] for j in range(picks)]
        number = [k.const[:, C_TOKEN:C_TOKEN + TILES]]
        if not shared:
            later = sb("later", [P, TILES])
            number.append(later[:])
        holds, empty, over = sb("holds", [P, slots]), sb("empty", [P, slots]), sb("over", [P, slots])
        spare = sb("spare", [P, slots])
        ps_m = ps("ps_m")
        if shared:
            wu, wg, wd = k.shared_w
            act_g = [sb(f"act_g{i}", [P, 512]) for i in range(2)]
            hid = [sb(f"hid{i}", [P, 512]) for i in range(8)]
            ps_u, ps_g, ps_y = ([ps(f"ps_{n}{i}") for i in range(2)] for n in "ugy")
        steps = sem("steps")
        marked, placed = sem("marked"), sem("placed")
        projected, gated, multiplied, summed, added = (
            sem("projected"), sem("gated"), sem("multiplied"), sem("summed"), sem("added"))
        block = ctx.enter_context(nc.Block())

        @block.vector
        def _(dve):
            do = Chain(dve, steps)
            if not shared:
                do(nc.vector.tensor_scalar(later[:], number[0], float(TOKENS), None, ALU.add))

            def mark(it, kk):
                t, par = U * it + kk, kk % 2
                if reused(t, 2):
                    dve.wait_ge(placed, t - 1)
                for i in range(picks):
                    nc.vector.tensor_scalar(in_lane[i][par][:], k.const[:, C_LANE:C_LANE + P],
                                            k.lane[i][:, bass.ds(t, 1)], None, ALU.is_equal).then_inc(marked, 1)
                    nc.vector.tensor_scalar(in_tile[i][par][:], k.const[:, C_SLOT:C_SLOT + slots],
                                            k.tile_at[i][:, bass.ds(t, 1)], number[i][:, bass.ds(t, 1)],
                                            ALU.is_equal, ALU.mult).then_inc(marked, 1)

            def multiply(it, kk):
                w, par = U * it + kk, kk % 2
                dve.wait_ge(gated, w + 1)
                if reused(w, 8):
                    dve.wait_ge(summed, 2 * it + kk // 4 - 1)
                nc.vector.tensor_tensor(hid[kk][:], act_g[par][:], ps_u[par][:], ALU.mult).then_inc(multiplied, 1)

            def add(it, kk):
                if kk % CHUNK != CHUNK - 1:
                    return
                c = 2 * it + kk // CHUNK
                dve.wait_ge(summed, c + 1)
                xc = k.x[:, bass.ts(c, CHUNK), :]
                nc.vector.scalar_tensor_tensor(xc, ps_y[kk // CHUNK][:].rearrange("p (t d) -> p t d", d=D),
                                               k.gates[:, 2:3], xc, ALU.mult, ALU.add).then_inc(added, 1)

            pipeline(dve, TILES, U, [(0, mark)] + ([(0, multiply), (4, add)] if shared else []))
            dve.wait_ge(placed, TILES)
            do(nc.vector.tensor_copy(holds[:], ps_m[:, 0:slots]))
            do(nc.vector.tensor_scalar(spare[:], k.const[:, C_SLOT:C_SLOT + slots], number[0][:, 0:1],
                                       float(picks * TOKENS), ALU.add, ALU.add))
            do(nc.vector.scalar_tensor_tensor(empty[:], holds[:], 0.0, spare[:], ALU.is_equal, ALU.mult))
            do(nc.vector.tensor_tensor(empty[:], empty[:], holds[:], ALU.add))
            do(nc.vector.tensor_scalar(k.slot_rows[:, 1, 0:slots], empty[:], -1.0, None, ALU.add))
            do(nc.vector.tensor_scalar(over[:], holds[:], TOKENS + 0.5, -float(TOKENS), ALU.is_ge, ALU.mult))
            do(nc.vector.tensor_scalar(holds[:], holds[:], -1.0, 0.0, ALU.add, ALU.max))
            do(nc.vector.tensor_tensor(k.slot_rows[:, 0, 0:slots], holds[:], over[:], ALU.add))

        @block.tensor
        def _(pe):
            def fill(it, kk):
                t, par = U * it + kk, kk % 2
                pe.wait_ge(marked, 2 * picks * (t + 1))
                for i in range(picks):
                    last = nc.tensor.matmul(ps_m[:, 0:slots], in_lane[i][par][:], in_tile[i][par][:],
                                            start=not reused(t, 1) and i == 0,
                                            stop=isinstance(t, int) and t == TILES - 1 and i == picks - 1)
                last.then_inc(placed, 1)

            def project_up(it, kk):
                w, par, f = U * it + kk, kk % 2, kk % FB
                if reused(w, 2):
                    pe.wait_ge(multiplied, w - 1)
                cols = k.xnt[:, bass.ts(2 * it + kk // CHUNK, 512)]
                nc.tensor.matmul(ps_g[par][:], wg[:, f * P:(f + 1) * P], cols, start=True, stop=True)
                nc.tensor.matmul(ps_u[par][:], wu[:, f * P:(f + 1) * P], cols,
                                 start=True, stop=True).then_inc(projected, 1)

            def project_down(it, kk):
                if kk % CHUNK != CHUNK - 1:
                    return
                c, par = 2 * it + kk // CHUNK, kk // CHUNK
                pe.wait_ge(multiplied, CHUNK * (c + 1))
                if reused(c, 2):
                    pe.wait_ge(added, c - 1)
                for j in range(CHUNK):
                    for f in range(FB):
                        last = nc.tensor.matmul(ps_y[par][:, j * P:(j + 1) * P],
                                                hid[4 * par + f][:, j * P:(j + 1) * P], wd[:, f, :],
                                                start=f == 0, stop=f == FB - 1)
                last.then_inc(summed, 1)

            pipeline(pe, TILES, U, [(1, fill)] + ([(0, project_up), (2, project_down)] if shared else []))

        if shared:
            @block.scalar
            def _(act):
                def gate(it, kk):
                    w, par = U * it + kk, kk % 2
                    act.wait_ge(projected, w + 1)
                    if reused(w, 2):
                        act.wait_ge(multiplied, w - 1)
                    nc.scalar.activation(act_g[par][:], ps_g[par][:], ACT.Silu).then_inc(gated, 1)

                pipeline(act, TILES, U, [(0, gate)])


def experts(nc, k, layer):
    slots = SLOTS[layer]
    swiglu = layer == 0
    with ExitStack() as ctx:
        def sb(n, shape, dt=F32):
            return ctx.enter_context(nc.sbuf_tensor(f"ex{layer}_{n}", shape, dt))

        def ps(n):
            return ctx.enter_context(nc.psum_tensor(f"ex{layer}_{n}", [P, 512], F32))

        def sem(n):
            return ctx.enter_context(nc.semaphore(f"ex{layer}_{n}"))

        U = LANES
        w_in, w_out = k.w_in, k.w_out
        if swiglu:
            w_gate = k.w_gate
            act_g = [sb(f"act_g{i}", [P, F]) for i in range(2)]
        else:
            b1, b2 = k.b1_all, k.b2_all
        rows_from, rows_to = ([sb(f"{n}{i}", [P, 1], I32) for i in range(U)] for n in ("from", "to"))
        xs = [sb(f"xs{i}", [P, D]) for i in range(U)]
        xt = [sb(f"xt{i}", [P, P]) for i in range(2)]
        hid = [sb(f"hid{i}", [P, F]) for i in range(2)]
        ht = [sb(f"ht{i}", [P, FB, P]) for i in range(2)]
        y = [sb(f"y{i}", [P, D]) for i in range(U)]
        ps_x, ps_y = ps("ps_x"), ps("ps_y")
        ps_u, ps_h = [ps(f"ps_u{i}") for i in range(2)], [ps(f"ps_h{i}") for i in range(2)]
        ps_g = [ps(f"ps_g{i}") for i in range(2)] if swiglu else None
        cleared, from_ready, to_ready, ticks = sem("cleared"), sem("from_ready"), sem("to_ready"), sem("ticks")
        rows_in, stored = k.rows_in, k.rows_out
        past = 16 * SLOTS[0] // U if layer else 0
        x_turned, xt_ready, projected, gated = sem("x_turned"), sem("xt_ready"), sem("projected"), sem("gated")
        hid_ready, h_turned, ht_ready, summed, y_ready = (
            sem("hid_ready"), sem("h_turned"), sem("ht_ready"), sem("summed"), sem("y_ready"))
        given = E - 1 if swiglu else E
        loads = 3 if swiglu else 4
        block = ctx.enter_context(nc.Block())

        def expert_of(eng, s):
            return eng.value_load(
                k.slot_expert[0:1, bass.ds(s, 1)], min_val=0, max_val=E - 1)

        class Experts:

            def __init__(self, eng, engine, lags):
                self.eng, self.engine, self.lags, self.of = eng, engine, lags, {}

            def fetch(self, it, kk):
                if kk == 0 and not isinstance(it, int):
                    first, count = -max(self.lags), U + max(self.lags) - min(self.lags)
                    _, values = nc.values_load_multi_w_load_instructions(
                        k.slot_expert[0:1, bass.ds(U * it + first, count)], engines=[self.engine],
                        min_val=0, max_val=E - 1,
                        skip_runtime_bounds_check_because="route() counts at most 7 experts for a slot tile")
                    self.of = {first + n: value for n, value in enumerate(values)}

            def __call__(self, it, kk, lag):
                if isinstance(it, int):
                    return expert_of(self.eng, U * it + kk)
                return self.of[kk if kk < U - lag else kk - U]

        @block.gpsimd
        def _(pool):
            if swiglu:
                nc.gpsimd.memset(w_in[:, given * F:], 0.0).then_inc(cleared, 1)
                nc.gpsimd.memset(w_gate[:, given * F:], 0.0).then_inc(cleared, 1)
                nc.gpsimd.memset(w_out[:, given * FB * D:], 0.0).then_inc(cleared, 1)

            def gather(it, kk):
                s = U * it + kk
                pool.wait_ge(from_ready, s + 1)
                if reused(s, U):
                    pool.wait_ge(x_turned, s - U + 1)
                absorb(pool, ticks)
                nc.gpsimd.indirect_dma_start(xs[kk][:], None, k.xn,
                                             bass.IndirectOffsetOnAxis(ap=rows_from[kk][:, 0:1], axis=0)
                                             ).then_inc(rows_in[kk], 16)

            def scatter(it, kk):
                s = U * it + kk
                pool.wait_ge(to_ready, s + 1)
                pool.wait_ge(y_ready, s + 1)
                absorb(pool, ticks)
                nc.gpsimd.indirect_dma_start(k.ys[layer], bass.IndirectOffsetOnAxis(ap=rows_to[kk][:, 0:1], axis=0),
                                             y[kk][:], None).then_inc(stored[kk], 16)

            pipeline(pool, slots, U, [(0, gather), (7, scatter)], peeled=1)
            for kk in range(U):
                pool.wait_ge(stored[kk], past + 16 * slots // U)

        @block.tensor
        def _(pe):
            ident = k.const[:, C_IDENT:C_IDENT + P]
            pe.wait_ge(k.weights_in, 16 * loads)
            if swiglu:
                pe.wait_ge(cleared, 3)

            experts = Experts(pe, mybir.EngineType.PE, (1, 4))

            def turn_x(it, kk):
                s, par = U * it + kk, kk % 2
                pe.wait_ge(rows_in[kk], past + 16 * (it + 1))
                if reused(s, 1):
                    pe.wait_ge(xt_ready, s)
                nc.tensor.transpose(ps_x[:, 0:P], xs[kk][:], ident).then_inc(x_turned, 1)

            def project_in(it, kk):
                s, par = U * it + kk, kk % 2
                e = experts(it, kk, 1)
                pe.wait_ge(xt_ready, s + 1)
                if reused(s, 2):
                    pe.wait_ge(hid_ready, s - 1)
                if swiglu:
                    nc.tensor.matmul(ps_g[par][:], xt[par][:], w_gate[:, bass.ts(e, F)], start=True, stop=True)
                nc.tensor.matmul(ps_u[par][:], xt[par][:], w_in[:, bass.ts(e, F)],
                                 start=True, stop=True).then_inc(projected, 1)

            def turn_h(it, kk):
                s, par = U * it + kk, kk % 2
                pe.wait_ge(hid_ready, s + 1)
                if reused(s, 2):
                    pe.wait_ge(ht_ready, s - 1)
                for c in range(FB):
                    last = nc.tensor.transpose(ps_h[par][:, c * P:(c + 1) * P], hid[par][:, c * P:(c + 1) * P], ident)
                last.then_inc(h_turned, 1)

            def project_out(it, kk):
                s, par = U * it + kk, kk % 2
                e = experts(it, kk, 4)
                pe.wait_ge(ht_ready, s + 1)
                if reused(s, 1):
                    pe.wait_ge(y_ready, s)
                for c in range(FB):
                    last = nc.tensor.matmul(ps_y[:, 0:D], ht[par][:, c, :],
                                            w_out[:, bass.ds(e * (FB * D) + c * D, D)],
                                            start=c == 0, stop=c == FB - 1)
                last.then_inc(summed, 1)

            pipeline(pe, slots, U, [(0, experts.fetch), (0, turn_x), (3, turn_h), (1, project_in), (4, project_out)], peeled=1)

        @block.scalar
        def _(act):
            def x_out(it, kk):
                s, par = U * it + kk, kk % 2
                act.wait_ge(x_turned, s + 1)
                if reused(s, 2):
                    act.wait_ge(projected, s - 1)
                nc.scalar.activation(xt[par][:], ps_x[:, 0:P], ACT.Copy).then_inc(xt_ready, 1)

            def gate(it, kk):
                s, par = U * it + kk, kk % 2
                act.wait_ge(projected, s + 1)
                if reused(s, 2):
                    act.wait_ge(hid_ready, s - 1)
                nc.scalar.activation(act_g[par][:], ps_g[par][:], ACT.Silu).then_inc(gated, 1)

            def h_out(it, kk):
                s, par = U * it + kk, kk % 2
                act.wait_ge(h_turned, s + 1)
                if reused(s, 2):
                    act.wait_ge(summed, s - 1)
                nc.scalar.activation(ht[par][:].rearrange("p c t -> p (c t)"), ps_h[par][:],
                                     ACT.Copy if swiglu else ACT.Gelu).then_inc(ht_ready, 1)

            pipeline(act, slots, U, [(0, x_out), (3, h_out)] + ([(1, gate)] if swiglu else []), peeled=1)

        @block.vector
        def _(dve):
            if not swiglu:
                dve.wait_ge(k.weights_in, 16 * loads)

            def index_from(it, kk):
                s = U * it + kk
                if reused(s, U):
                    dve.wait_ge(rows_in[kk], past + 16 * it)
                nc.vector.tensor_scalar(rows_from[kk][:], k.slot_rows[:, 0, bass.ds(s, 1)],
                                        1.0, None, ALU.mult).then_inc(from_ready, 1)

            def index_to(it, kk):
                s = U * it + kk
                if reused(s, U):
                    dve.wait_ge(stored[kk], past + 16 * it)
                nc.vector.tensor_scalar(rows_to[kk][:], k.slot_rows[:, 1, bass.ds(s, 1)],
                                        1.0, None, ALU.mult).then_inc(to_ready, 1)

            def hidden(it, kk):
                s, par = U * it + kk, kk % 2
                if swiglu:
                    dve.wait_ge(gated, s + 1)
                else:
                    e = expert_of(dve, s)
                    dve.wait_ge(projected, s + 1)
                if reused(s, 2):
                    dve.wait_ge(h_turned, s - 1)
                other = act_g[par][:] if swiglu else b1[:, bass.ts(e, F)]
                nc.vector.tensor_tensor(hid[par][:], ps_u[par][:], other,
                                        ALU.mult if swiglu else ALU.add).then_inc(hid_ready, 1)

            def output(it, kk):
                s, par = U * it + kk, kk % 2
                if not swiglu:
                    e = expert_of(dve, s)
                dve.wait_ge(summed, s + 1)
                if reused(s, U):
                    dve.wait_ge(stored[kk], past + 16 * it)
                if swiglu:
                    nc.vector.tensor_copy(y[kk][:], ps_y[:, 0:D]).then_inc(y_ready, 1)
                else:
                    nc.vector.tensor_tensor(y[kk][:], ps_y[:, 0:D], b2[:, bass.ts(e, D)],
                                            ALU.add).then_inc(y_ready, 1)

            pipeline(dve, slots, U, [(0, index_from), (4, hidden), (7, index_to), (7, output)])


def combine(nc, k, layer):
    picks = layer + 1
    with ExitStack() as ctx:
        def sem(n):
            return ctx.enter_context(nc.semaphore(f"co{layer}_{n}"))

        U = 4
        rows = [[ctx.enter_context(nc.sbuf_tensor(f"co{layer}_rows{i}_{j}", [P, CHUNK, D], F32)) for i in range(U)]
                for j in range(picks)]
        added, stored = sem("added"), sem("stored")
        counted, dve_ticks, awake = sem("counted"), sem("dve_ticks"), sem("awake")
        loaded = [sem(f"loaded{i}") for i in range(U)]
        block = ctx.enter_context(nc.Block())

        @block.sync
        def _(sp):
            def load(it, kk):
                c = U * it + kk
                if reused(c, U):
                    sp.wait_ge(added, picks * CHUNK * (c - U + 1))
                for i in range(picks):
                    yv = k.ys[layer][i * TOKENS:(i + 1) * TOKENS, :].rearrange("(t p) d -> p t d", p=P)
                    sp.dma_start(rows[i][kk][:], yv[:, bass.ts(c, CHUNK), :]).then_inc(loaded[kk], 16)

            pipeline(sp, CHUNKS, U, [(0, load)], peeled=1)

        @block.vector
        def _(dve):
            def add(it, kk):
                c = U * it + kk
                dve.wait_ge(loaded[kk], 16 * picks * (it + 1))
                for i in range(picks):
                    if i:
                        dve.wait_ge(added, picks * CHUNK * c + CHUNK)
                    for j in range(CHUNK):
                        t = CHUNK * c + j
                        xt = k.x[:, bass.ds(t, 1), :].rearrange("p a d -> p (a d)")
                        nc.vector.scalar_tensor_tensor(xt, rows[i][kk][:, j, :], k.weight[i][:, bass.ds(t, 1)], xt,
                                                       ALU.mult, ALU.add).then_inc(added, 1)
                if not layer:
                    dve.wait_ge(added, CHUNK * (c + 1))
                    absorb(dve, dve_ticks)
                    for j in range(CHUNK):
                        gather_stats(nc, k, CHUNK * c + j).then_inc(counted, 1)

            pipeline(dve, CHUNKS, U, [(0, add)], peeled=1)
            if not layer:
                dve.wait_ge(counted, TILES)

        if not layer:
            @block.gpsimd
            def _(pool):
                wake_pool(nc, k).then_inc(awake, 1)

        if layer:
            @block.scalar
            def _(act):
                ov = k.out.rearrange("(t p) d -> p t d", p=P)

                def store(it, kk):
                    c = U * it + kk
                    act.wait_ge(added, picks * CHUNK * (c + 1))
                    act.dma_start(ov[:, bass.ts(c, CHUNK), :], k.x[:, bass.ts(c, CHUNK), :]).then_inc(stored, 16)

                pipeline(act, CHUNKS, U, [(0, store)], peeled=1)
                act.wait_ge(stored, 16 * CHUNKS)


def clear_semaphores(nc, numbers):
    with nc.Block() as block:
        @block.gpsimd
        def _(pool):
            pool.sem_clear(numbers)


class Tensors:
    pass


def build(nc, tensors):
    k = tensors
    k.qt = nc.dram_tensor("qt", (D, TOKENS), F32).ap()
    k.kt = nc.dram_tensor("kt", (D, TOKENS), F32).ap()
    k.v = nc.dram_tensor("v", (TOKENS, D), F32).ap()
    k.xn = nc.dram_tensor("xn", (TOKENS, D), F32).ap()
    k.ys = [nc.dram_tensor(f"ys{i}", ((i + 1) * TOKENS + SLOTS[i] * P, D), F32).ap() for i in range(2)]
    with ExitStack() as ctx:
        def sb(n, shape, dt=F32):
            return ctx.enter_context(nc.sbuf_tensor(n, shape, dt))

        k.x = sb("x", [P, TILES, D])
        k.const = sb("const", [P, C_ALL])
        k.gates = sb("gates", [P, 4])
        k.stats = sb("stats", [P, TILES, 6])
        k.scratch = sb("scratch", [P, 1])
        k.mean, k.rstd = sb("mean", [P, TILES]), sb("rstd", [P, TILES])
        k.weight = [sb(f"weight{i}", [P, TILES]) for i in range(2)]
        k.tile_at = [sb(f"tile_at{i}", [P, TILES]) for i in range(2)]
        k.lane = [sb(f"lane{i}", [P, TILES]) for i in range(2)]
        k.slot_rows = sb("slot_rows", [P, 2, MAX_SLOTS])
        k.slot_expert = sb("slot_expert", [P, MAX_SLOTS], I32)
        k.rows_in = [ctx.enter_context(nc.semaphore(f"rows_in{i}")) for i in range(LANES)]
        k.rows_out = [ctx.enter_context(nc.semaphore(f"rows_out{i}")) for i in range(LANES)]
        numbers = range(min(nc.free_semaphores), max(nc.free_semaphores) + 1)
        assert set(numbers) <= set(nc.free_semaphores)
        load_inputs(nc, k)
        for layer in range(2):
            if layer:
                clear_semaphores(nc, numbers)
            with ExitStack() as own:
                if layer == 0:
                    k.mask0 = own.enter_context(nc.sbuf_tensor("mask0", [P, SEQ], I32))
                    k.bias0 = own.enter_context(nc.sbuf_tensor("bias0", [P, SEQ], F32))
                else:
                    k.mask1 = own.enter_context(nc.sbuf_tensor("mask1", [P, TILES, SEQ], I32))
                    k.bias1 = own.enter_context(nc.sbuf_tensor("bias1", [P, TILES, SEQ], F32))
                layer_stats(nc, k, f"lnq{layer}")
                project(nc, k, layer)
                attend(nc, k, layer)
            with ExitStack() as own:
                def weights(n, shape):
                    return own.enter_context(nc.sbuf_tensor(f"{n}{layer}", shape, F32))

                k.w_in, k.w_out = weights("w_in", [P, E * F]), weights("w_out", [P, E * FB * D])
                if layer == 0:
                    k.w_gate = weights("w_gate", [P, E * F])
                else:
                    k.b1_all, k.b2_all = weights("b1_all", [P, E * F]), weights("b2_all", [P, E * D])
                k.weights_in = own.enter_context(nc.semaphore(f"weights_in{layer}"))
                with ExitStack() as shared:
                    layer_stats(nc, k, f"lnf{layer}")
                    if layer == 0:
                        k.xnt = shared.enter_context(nc.sbuf_tensor("xnt", [P, TOKENS], F32))
                        k.shared_w = [shared.enter_context(nc.sbuf_tensor(f"shared_{n}", shape, F32)) for n, shape in
                                      (("up_w", [P, F]), ("gate_w", [P, F]), ("down_w", [P, FB, D]))]
                    route(nc, k, layer)
                    place(nc, k, layer)
                experts(nc, k, layer)
            combine(nc, k, layer)


def kernel(**inputs):
    import concourse.bacc as bacc
    from concourse.bass_utils import run_bass_kernel_spmd

    a = {n: np.asarray(v) for n, v in inputs.items()}
    ctx = a["ctx_1024"].reshape(TOKENS, D)
    given = {
        "x_in": a["x"].reshape(TOKENS, D),
        "ctx_in": ctx,
        "ctxt_in": ctx.T,
        "mask0_in": a["mask_1x1xSxS2_ik0"].reshape(SEQ, SEQ),
        "mask1_in": a["mask_BxSxS2_ik1"],
        "g_xattn": a["g_xattn"],
        "g_ffn": a["g_ffn"],
        "wq": a["L0_xattn_wq_w"].T,
        "wk": a["L0_xattn_wk_w"].T,
        "wv": a["L0_xattn_wv_w"].T,
        "wo": a["L0_xattn_wo_w"].T,
        "bq": a["L0_xattn_wq_b"].reshape(D, 1),
        "bk": a["L0_xattn_wk_b"].reshape(D, 1),
        "bv": a["L0_xattn_wv_b"],
        "bo": a["L0_xattn_wo_b"],
        "router0": a["L0_ffn_Wr"],
        "router1": a["L1_ffn_Wg"],
        "up": a["L0_ffn_Wu"],
        "gate": a["L0_ffn_Wg"],
        "down": a["L0_ffn_Wd"],
        "shared_up": a["L0_ffn_Wu_s"],
        "shared_gate": a["L0_ffn_Wg_s"],
        "shared_down": a["L0_ffn_Wd_s"],
        "w1": a["L1_ffn_W1"],
        "b1": a["L1_ffn_b1"],
        "w2": a["L1_ffn_W2"],
        "b2": a["L1_ffn_b2"],
        "const_in": constants(),
    }
    given = {n: np.ascontiguousarray(v) for n, v in given.items()}
    nc = bacc.Bacc("TRN2", target_bir_lowering=False, num_devices=1)
    t = Tensors()
    for n, v in given.items():
        t.__dict__[n] = nc.dram_tensor(n, v.shape, mybir.dt.from_np(v.dtype), kind="ExternalInput").ap()
    t.out = nc.dram_tensor("out", (TOKENS, D), F32, kind="ExternalOutput").ap()
    t.routers = [t.router0, t.router1]
    build(nc, t)
    result = run_bass_kernel_spmd(nc, [given], core_ids=[0])
    return result.results[0]["out"].reshape(BATCH, SEQ, D)
```
